# Optimizing a Trainium2 kernel written in Bass

```python
import numpy as np
import jax
import jax.numpy as jnp

def _softmax(x, axis=-1):
    return jax.nn.softmax(x, axis=axis)

def _gelu(x):
    return jax.nn.gelu(x, approximate=True)

def _silu(x):
    return jax.nn.silu(x)

def _sigmoid(x):
    return jax.nn.sigmoid(x)

def _layernorm(x, axis=-1, eps=1e-05):
    m = jnp.mean(x, axis=axis, keepdims=True)
    v = jnp.var(x, axis=axis, keepdims=True)
    return (x - m) / jnp.sqrt(v + eps)

def _scatter_add(tgt, idx, src, axis=0):
    return tgt.at[idx].add(src)

def _segment_sum(src, seg, n):
    return jax.ops.segment_sum(src, seg, n)
kernel_name = 'mk_gnn_ffn_d4_gnn_r16_9f5d5f'

def setup_inputs(seed: int=0):
    np.random.seed(seed)
    _w = jnp.asarray

    def _rec_inputs():
        import jax
        import jax.numpy as jnp
        _gk = jax.random.key(seed)
        x = -0.0001126 + 1 * jax.random.normal(jax.random.fold_in(_gk, 1), (625, 768), jnp.float32)
        src = jax.random.randint(jax.random.fold_in(_gk, 2), (10000,), 0, 625, jnp.int32)
        dst = jnp.minimum((625 * jax.random.uniform(jax.random.fold_in(_gk, 3), (10000,)) ** 2.0).astype(jnp.int32), 9999)
        _o = jnp.argsort(dst, stable=True)
        src = src[_o]
        dst = dst[_o]
        edge_type_3 = jax.random.randint(jax.random.fold_in(_gk, 13), (10000,), 0, 3, jnp.int32)
        node_type_3 = jax.random.randint(jax.random.fold_in(_gk, 14), (625,), 0, 3, jnp.int32)
        return (x, src, dst, edge_type_3, node_type_3)
    x, src, dst, edge_type_3, node_type_3 = _rec_inputs()

    def _L0_gnn_setup():
        import jax, jax.numpy as jnp
        import numpy as np
        N = 625
        E = 6250
        D = 768
        H = 1536
        EPS_MSG = 1e-07
        EPS_BN = 1e-05

        def segment_softmax(logits, seg, num_segments):
            m = jax.ops.segment_max(logits, seg, num_segments=num_segments)
            m = jnp.where(jnp.isfinite(m), m, 0.0)
            e = jnp.exp(logits - m[seg])
            s = jax.ops.segment_sum(e, seg, num_segments=num_segments)
            return e / (s[seg] + 1e-16)
        key = jax.random.key(seed)
        ks = jax.random.split(key, 8)
        x = jax.random.normal(ks[0], (N, D), dtype=jnp.float32)
        edge_index = jax.random.randint(ks[1], (2, E), 0, N, dtype=jnp.int32)
        batch = jnp.zeros((N,), dtype=jnp.int32)
        t = jnp.asarray(1.0, dtype=jnp.float32)
        s1 = 1.0 / np.sqrt(D)
        s2 = 1.0 / np.sqrt(H)
        W1 = jax.random.uniform(ks[2], (D, H), jnp.float32, -s1, s1)
        b1 = jax.random.uniform(ks[3], (H,), jnp.float32, -s1, s1)
        bn_gamma = jnp.ones((H,), jnp.float32)
        bn_beta = jnp.zeros((H,), jnp.float32)
        bn_mean = jnp.zeros((H,), jnp.float32)
        bn_var = jnp.ones((H,), jnp.float32)
        W2 = jax.random.uniform(ks[4], (H, D), jnp.float32, -s2, s2)
        b2 = jax.random.uniform(ks[5], (D,), jnp.float32, -s2, s2)
        return {'x': x, 'edge_index': edge_index, 'batch': batch, 't': t, 'W1': W1, 'b1': b1, 'bn_gamma': bn_gamma, 'bn_beta': bn_beta, 'bn_mean': bn_mean, 'bn_var': bn_var, 'W2': W2, 'b2': b2}
    _L0_gnn_all = _L0_gnn_setup()
    _L0_gnn_in = {k: v for k, v in _L0_gnn_all.items() if k in ('t', 'W1', 'b1', 'bn_gamma', 'bn_beta', 'bn_mean', 'bn_var', 'W2', 'b2')}
    del _L0_gnn_all

    def _L0_ffn_setup():
        import jax, jax.numpy as jnp
        import numpy as np
        TOP_K = 2
        key = jax.random.key(seed)
        ks = jax.random.split(key, 5)
        B, S, D, H, E = (1, 128, 768, 192, 8)
        x = jax.random.normal(ks[0], (B, S, D), dtype=jnp.float32)
        gate_w = jax.random.normal(ks[1], (E, D), dtype=jnp.float32) * 0.02
        w1 = jax.random.normal(ks[2], (E, D, H), dtype=jnp.float32) * 0.02
        b1 = jnp.zeros((E, H), dtype=jnp.float32)
        w2 = jax.random.normal(ks[3], (E, H, D), dtype=jnp.float32) * 0.02
        b2 = jnp.zeros((E, D), dtype=jnp.float32)
        return {'x': x, 'gate_w': gate_w, 'w1': w1, 'b1': b1, 'w2': w2, 'b2': b2}
    _L0_ffn_all = _L0_ffn_setup()
    _L0_ffn_in = {k: v for k, v in _L0_ffn_all.items() if k in ('gate_w', 'w1', 'b1', 'w2', 'b2')}
    del _L0_ffn_all

    def _L1_gnn_setup():
        import jax, jax.numpy as jnp
        import numpy as np
        N_NODES = 625
        D = 768
        N_EDGES = 10000

        def gcn_conv(x, W, b, src, dst, n_nodes):
            h = x @ W
            deg = jax.ops.segment_sum(jnp.ones_like(dst, dtype=h.dtype), dst, num_segments=n_nodes)
            dinv = jnp.where(deg > 0, jax.lax.rsqrt(deg), 0.0)
            norm = dinv[src] * dinv[dst]
            msgs = h[src] * norm[:, None]
            out = jax.ops.segment_sum(msgs, dst, num_segments=n_nodes)
            return out + b

        def add_self_loops(edge_index, n_nodes):
            loop = jnp.arange(n_nodes, dtype=edge_index.dtype)
            src = jnp.concatenate([edge_index[0], loop])
            dst = jnp.concatenate([edge_index[1], loop])
            return (src, dst)
        key = jax.random.key(seed)
        k1, k2, k3, k4 = jax.random.split(key, 4)
        x = jax.random.normal(k1, (N_NODES, D), dtype=jnp.float32)
        edge_index = jax.random.randint(k2, (2, N_EDGES), 0, N_NODES, dtype=jnp.int32)
        glorot = float(np.sqrt(6.0 / (D + D)))
        W1 = jax.random.uniform(k3, (D, D), jnp.float32, -glorot, glorot)
        W2 = jax.random.uniform(k4, (D, D), jnp.float32, -glorot, glorot)
        b1 = jnp.zeros((D,), jnp.float32)
        b2 = jnp.zeros((D,), jnp.float32)
        return {'x': x, 'W1': W1, 'b1': b1, 'W2': W2, 'b2': b2, 'edge_index': edge_index}
    _L1_gnn_all = _L1_gnn_setup()
    _L1_gnn_in = {k: v for k, v in _L1_gnn_all.items() if k in ('W1', 'b1', 'W2', 'b2')}
    del _L1_gnn_all

    def _L1_ffn_setup():
        import jax, jax.numpy as jnp
        import numpy as np
        DECAY = 0.9
        EPS = 0.01
        TOP_K = 2
        key = jax.random.key(seed)
        k1, k2, k3, k4 = jax.random.split(key, 4)
        B, S, H, I, E = (4, 128, 768, 128, 8)
        return {'hidden_states': jax.random.normal(k1, (B, S, H), jnp.float32), 'router_w': jax.random.normal(k2, (E, H), jnp.float32) * 0.02, 'w1': jax.random.normal(k3, (E, I, H), jnp.float32) * 0.02, 'w2': jax.random.normal(k4, (E, H, I), jnp.float32) * 0.02}
    _L1_ffn_all = _L1_ffn_setup()
    _L1_ffn_in = {k: v for k, v in _L1_ffn_all.items() if k in ('router_w', 'w1', 'w2')}
    del _L1_ffn_all

    def _L2_gnn_setup():
        import jax, jax.numpy as jnp
        import numpy as np
        N_NODES = 625
        NEG_SLOPE = 0.2
        EPS = 1e-16

        def gat_layer(x, W, att_src, att_dst, bias, src, dst, heads, out_ch, concat):
            n = x.shape[0]
            h = (x @ W.T).reshape(n, heads, out_ch)
            a_src = jnp.einsum('nhc,hc->nh', h, att_src)
            a_dst = jnp.einsum('nhc,hc->nh', h, att_dst)
            e = a_src[src] + a_dst[dst]
            e = jax.nn.leaky_relu(e, NEG_SLOPE)
            m = jax.ops.segment_max(e, dst, num_segments=n)
            ex = jnp.exp(e - m[dst])
            denom = jax.ops.segment_sum(ex, dst, num_segments=n)
            alpha = ex / (denom[dst] + EPS)
            msg = alpha[:, :, None] * h[src]
            out = jax.ops.segment_sum(msg, dst, num_segments=n)
            if concat:
                out = out.reshape(n, heads * out_ch)
            else:
                out = out.mean(axis=1)
            return out + bias
        key = jax.random.key(seed)
        ks = jax.random.split(key, 12)
        x = jax.random.normal(ks[0], (N_NODES, 768), dtype=jnp.float32)
        edge_index = jax.random.randint(ks[1], (2, 10000), 0, N_NODES, dtype=jnp.int64)
        s1 = 1.0 / np.sqrt(768.0)
        W1 = jax.random.normal(ks[2], (8 * 128, 768), dtype=jnp.float32) * s1
        att_src1 = jax.random.normal(ks[3], (8, 128), dtype=jnp.float32) * (1.0 / np.sqrt(128.0))
        att_dst1 = jax.random.normal(ks[4], (8, 128), dtype=jnp.float32) * (1.0 / np.sqrt(128.0))
        b1 = jnp.zeros((8 * 128,), dtype=jnp.float32)
        s2 = 1.0 / np.sqrt(1024.0)
        W2 = jax.random.normal(ks[5], (1 * 768, 1024), dtype=jnp.float32) * s2
        att_src2 = jax.random.normal(ks[6], (1, 768), dtype=jnp.float32) * (1.0 / np.sqrt(768.0))
        att_dst2 = jax.random.normal(ks[7], (1, 768), dtype=jnp.float32) * (1.0 / np.sqrt(768.0))
        b2 = jnp.zeros((768,), dtype=jnp.float32)
        return {'x': x, 'edge_index': edge_index, 'W1': W1, 'att_src1': att_src1, 'att_dst1': att_dst1, 'b1': b1, 'W2': W2, 'att_src2': att_src2, 'att_dst2': att_dst2, 'b2': b2}
    _L2_gnn_all = _L2_gnn_setup()
    _L2_gnn_in = {k: v for k, v in _L2_gnn_all.items() if k in ('W1', 'att_src1', 'att_dst1', 'b1', 'W2', 'att_src2', 'att_dst2', 'b2')}
    del _L2_gnn_all

    def _L2_ffn_setup():
        import jax, jax.numpy as jnp
        import numpy as np
        EPS = 1e-06

        def l2_normalize(x, axis):
            norm = jnp.sqrt(jnp.square(x).sum(axis=axis, keepdims=True))
            return x * (1.0 / (norm + EPS))
        key = jax.random.key(seed)
        ks = jax.random.split(key, 8)
        b, m, d = (32, 1024, 768)
        n, p = (8, 4)
        h = d // 8
        X = jax.random.normal(ks[0], (b, m, d), dtype=jnp.float32)
        std_slot = float(np.sqrt(2.0 / (d + n * p)))
        slot_params = jax.random.normal(ks[1], (d, n, p), dtype=jnp.float32) * std_slot
        scale = jnp.ones((), dtype=jnp.float32)
        W_down = jax.random.normal(ks[2], (n, d, h), dtype=jnp.float32) * float(np.sqrt(1.0 / d))
        b_down = jnp.zeros((n, h), dtype=jnp.float32)
        W_up = jax.random.normal(ks[3], (n, h, d), dtype=jnp.float32) * float(np.sqrt(1.0 / h))
        b_up = jnp.zeros((n, d), dtype=jnp.float32)
        return {'X': X, 'slot_params': slot_params, 'scale': scale, 'W_down': W_down, 'b_down': b_down, 'W_up': W_up, 'b_up': b_up}
    _L2_ffn_all = _L2_ffn_setup()
    _L2_ffn_in = {k: v for k, v in _L2_ffn_all.items() if k in ('slot_params', 'scale', 'W_down', 'b_down', 'W_up', 'b_up')}
    del _L2_ffn_all

    def _L3_gnn_setup():
        import jax, jax.numpy as jnp
        import numpy as np
        NUM_NODES = 625
        NUM_EDGES = 10000
        IN_CH = 768
        TYPE_DIM = 128
        HID = 768
        OUT = 768
        NUM_REL = 3
        NUM_NODE_TYPE = 3

        def _glorot(key, shape):
            fan_in, fan_out = (shape[-2], shape[-1])
            lim = (6.0 / (fan_in + fan_out)) ** 0.5
            return jax.random.uniform(key, shape, jnp.float32, -lim, lim)

        def rgcn_conv(h, src, dst, edge_type, w_rel, w_root, bias):
            num_nodes = h.shape[0]
            xw = jnp.einsum('nd,rde->rne', h, w_rel)
            msg = xw[edge_type, src]
            onehot = jax.nn.one_hot(edge_type, NUM_REL, dtype=h.dtype)
            count = jax.ops.segment_sum(onehot, dst, num_segments=num_nodes)
            inv = jnp.where(count > 0, 1.0 / jnp.maximum(count, 1.0), 0.0)
            msg = msg * inv[dst, edge_type][:, None]
            agg = jax.ops.segment_sum(msg, dst, num_segments=num_nodes)
            return agg + h @ w_root + bias
        key = jax.random.key(seed)
        ks = jax.random.split(key, 16)
        d1 = IN_CH + TYPE_DIM
        inp = {'x': jax.random.normal(ks[0], (NUM_NODES, IN_CH), jnp.float32), 'node_type': jax.random.randint(ks[1], (NUM_NODES,), 0, NUM_NODE_TYPE, jnp.int32), 'edge_index': jax.random.randint(ks[2], (2, NUM_EDGES), 0, NUM_NODES, jnp.int32), 'edge_type': jax.random.randint(ks[3], (NUM_EDGES,), 0, NUM_REL, jnp.int32), 'node_emb': jax.random.normal(ks[4], (NUM_NODE_TYPE, TYPE_DIM), jnp.float32), 'w_rel1': _glorot(ks[5], (NUM_REL, d1, d1)), 'w_root1': _glorot(ks[6], (d1, d1)), 'b1': jnp.zeros((d1,), jnp.float32), 'w_rel2': _glorot(ks[7], (NUM_REL, d1, HID)), 'w_root2': _glorot(ks[8], (d1, HID)), 'b2': jnp.zeros((HID,), jnp.float32), 'w_rel3': _glorot(ks[9], (NUM_REL, HID, OUT)), 'w_root3': _glorot(ks[10], (HID, OUT)), 'b3': jnp.zeros((OUT,), jnp.float32)}
        return inp
    _L3_gnn_all = _L3_gnn_setup()
    _L3_gnn_in = {k: v for k, v in _L3_gnn_all.items() if k in ('node_emb', 'w_rel1', 'w_root1', 'b1', 'w_rel2', 'w_root2', 'b2', 'w_rel3', 'w_root3', 'b3')}
    del _L3_gnn_all

    def _L3_ffn_setup():
        import jax, jax.numpy as jnp
        import numpy as np
        EMBED = 768
        HIDDEN = 192
        N_EXPERTS = 8
        TOP_K = 2
        key = jax.random.key(seed)
        ks = jax.random.split(key, 6)
        x = jax.random.normal(ks[0], (2, 128, EMBED), dtype=jnp.float32)
        gate_w = 0.02 * jax.random.normal(ks[1], (N_EXPERTS, EMBED), dtype=jnp.float32)
        w1 = 0.02 * jax.random.normal(ks[2], (N_EXPERTS, EMBED, HIDDEN), dtype=jnp.float32)
        b1 = jnp.zeros((N_EXPERTS, HIDDEN), dtype=jnp.float32)
        w2 = 0.02 * jax.random.normal(ks[3], (N_EXPERTS, HIDDEN, EMBED), dtype=jnp.float32)
        b2 = jnp.zeros((N_EXPERTS, EMBED), dtype=jnp.float32)
        return {'x': x, 'gate_w': gate_w, 'w1': w1, 'b1': b1, 'w2': w2, 'b2': b2}
    _L3_ffn_all = _L3_ffn_setup()
    _L3_ffn_in = {k: v for k, v in _L3_ffn_all.items() if k in ('gate_w', 'w1', 'b1', 'w2', 'b2')}
    del _L3_ffn_all
    return {'x': x, 'src': src, 'dst': dst, 'edge_type_3': edge_type_3, 'node_type_3': node_type_3, 'L0_gnn_t': _L0_gnn_in['t'], 'L0_gnn_W1': _L0_gnn_in['W1'], 'L0_gnn_b1': _L0_gnn_in['b1'], 'L0_gnn_bn_gamma': _L0_gnn_in['bn_gamma'], 'L0_gnn_bn_beta': _L0_gnn_in['bn_beta'], 'L0_gnn_bn_mean': _L0_gnn_in['bn_mean'], 'L0_gnn_bn_var': _L0_gnn_in['bn_var'], 'L0_gnn_W2': _L0_gnn_in['W2'], 'L0_gnn_b2': _L0_gnn_in['b2'], 'L0_ffn_gate_w': _L0_ffn_in['gate_w'], 'L0_ffn_w1': _L0_ffn_in['w1'], 'L0_ffn_b1': _L0_ffn_in['b1'], 'L0_ffn_w2': _L0_ffn_in['w2'], 'L0_ffn_b2': _L0_ffn_in['b2'], 'L1_gnn_W1': _L1_gnn_in['W1'], 'L1_gnn_b1': _L1_gnn_in['b1'], 'L1_gnn_W2': _L1_gnn_in['W2'], 'L1_gnn_b2': _L1_gnn_in['b2'], 'L1_ffn_router_w': _L1_ffn_in['router_w'], 'L1_ffn_w1': _L1_ffn_in['w1'], 'L1_ffn_w2': _L1_ffn_in['w2'], 'L2_gnn_W1': _L2_gnn_in['W1'], 'L2_gnn_att_src1': _L2_gnn_in['att_src1'], 'L2_gnn_att_dst1': _L2_gnn_in['att_dst1'], 'L2_gnn_b1': _L2_gnn_in['b1'], 'L2_gnn_W2': _L2_gnn_in['W2'], 'L2_gnn_att_src2': _L2_gnn_in['att_src2'], 'L2_gnn_att_dst2': _L2_gnn_in['att_dst2'], 'L2_gnn_b2': _L2_gnn_in['b2'], 'L2_ffn_slot_params': _L2_ffn_in['slot_params'], 'L2_ffn_scale': _L2_ffn_in['scale'], 'L2_ffn_W_down': _L2_ffn_in['W_down'], 'L2_ffn_b_down': _L2_ffn_in['b_down'], 'L2_ffn_W_up': _L2_ffn_in['W_up'], 'L2_ffn_b_up': _L2_ffn_in['b_up'], 'L3_gnn_node_emb': _L3_gnn_in['node_emb'], 'L3_gnn_w_rel1': _L3_gnn_in['w_rel1'], 'L3_gnn_w_root1': _L3_gnn_in['w_root1'], 'L3_gnn_b1': _L3_gnn_in['b1'], 'L3_gnn_w_rel2': _L3_gnn_in['w_rel2'], 'L3_gnn_w_root2': _L3_gnn_in['w_root2'], 'L3_gnn_b2': _L3_gnn_in['b2'], 'L3_gnn_w_rel3': _L3_gnn_in['w_rel3'], 'L3_gnn_w_root3': _L3_gnn_in['w_root3'], 'L3_gnn_b3': _L3_gnn_in['b3'], 'L3_ffn_gate_w': _L3_ffn_in['gate_w'], 'L3_ffn_w1': _L3_ffn_in['w1'], 'L3_ffn_b1': _L3_ffn_in['b1'], 'L3_ffn_w2': _L3_ffn_in['w2'], 'L3_ffn_b2': _L3_ffn_in['b2']}

def reference(x, src, dst, edge_type_3, node_type_3, L0_gnn_t, L0_gnn_W1, L0_gnn_b1, L0_gnn_bn_gamma, L0_gnn_bn_beta, L0_gnn_bn_mean, L0_gnn_bn_var, L0_gnn_W2, L0_gnn_b2, L0_ffn_gate_w, L0_ffn_w1, L0_ffn_b1, L0_ffn_w2, L0_ffn_b2, L1_gnn_W1, L1_gnn_b1, L1_gnn_W2, L1_gnn_b2, L1_ffn_router_w, L1_ffn_w1, L1_ffn_w2, L2_gnn_W1, L2_gnn_att_src1, L2_gnn_att_dst1, L2_gnn_b1, L2_gnn_W2, L2_gnn_att_src2, L2_gnn_att_dst2, L2_gnn_b2, L2_ffn_slot_params, L2_ffn_scale, L2_ffn_W_down, L2_ffn_b_down, L2_ffn_W_up, L2_ffn_b_up, L3_gnn_node_emb, L3_gnn_w_rel1, L3_gnn_w_root1, L3_gnn_b1, L3_gnn_w_rel2, L3_gnn_w_root2, L3_gnn_b2, L3_gnn_w_rel3, L3_gnn_w_root3, L3_gnn_b3, L3_ffn_gate_w, L3_ffn_w1, L3_ffn_b1, L3_ffn_w2, L3_ffn_b2):
    import jax
    import jax.numpy as jnp

    def _L0_gnn_ref(x, edge_index, batch, t, W1, b1, bn_gamma, bn_beta, bn_mean, bn_var, W2, b2):
        import jax, jax.numpy as jnp
        import numpy as np
        N = 625
        E = 6250
        D = 768
        H = 1536
        EPS_MSG = 1e-07
        EPS_BN = 1e-05

        def segment_softmax(logits, seg, num_segments):
            m = jax.ops.segment_max(logits, seg, num_segments=num_segments)
            m = jnp.where(jnp.isfinite(m), m, 0.0)
            e = jnp.exp(logits - m[seg])
            s = jax.ops.segment_sum(e, seg, num_segments=num_segments)
            return e / (s[seg] + 1e-16)
        src, dst = (edge_index[0], edge_index[1])
        msg = jax.nn.relu(x[src]) + EPS_MSG
        alpha = segment_softmax(msg * t, dst, N)
        agg = jax.ops.segment_sum(msg * alpha, dst, num_segments=N)
        out = agg + x
        z = out @ W1 + b1
        z = (z - bn_mean) * jax.lax.rsqrt(bn_var + EPS_BN) * bn_gamma + bn_beta
        z = jax.nn.relu(z)
        z = z @ W2 + b2
        return x + z

    def _L0_ffn_ref(x, gate_w, w1, b1, w2, b2):
        import jax, jax.numpy as jnp
        import numpy as np
        TOP_K = 2
        B, S, D = x.shape
        E, _, H = w1.shape
        T = B * S
        K = TOP_K
        xf = x.reshape(T, D)
        logits = xf @ gate_w.T
        probs = jax.nn.softmax(logits, axis=-1)
        top_w, top_i = jax.lax.top_k(probs, K)
        top_w = top_w / (jnp.sum(top_w, axis=-1, keepdims=True) + 1e-09)
        flat_e = top_i.reshape(-1)
        flat_w = top_w.reshape(-1)
        tok_idx = jnp.repeat(jnp.arange(T), K)
        order = jnp.argsort(flat_e)
        se = flat_e[order]
        pt = tok_idx[order]
        pw = flat_w[order]
        counts = jax.ops.segment_sum(jnp.ones(T * K, jnp.int32), se, num_segments=E)
        starts = jnp.concatenate([jnp.zeros((1,), jnp.int32), jnp.cumsum(counts)[:-1]])
        pos = jnp.arange(T * K) - starts[se]
        cap = T * K
        padded = jnp.zeros((E, cap, D), x.dtype).at[se, pos].set(xf[pt])
        hidden = jax.nn.gelu(jnp.einsum('ecd,edh->ech', padded, w1) + b1[:, None, :], approximate=False)
        out = jnp.einsum('ech,ehd->ecd', hidden, w2) + b2[:, None, :]
        expert_out = out[se, pos] * pw[:, None]
        final = jnp.zeros((T, D), x.dtype).at[pt].add(expert_out)
        return final.reshape(B, S, D)

    def _L1_gnn_ref(x, W1, b1, W2, b2, edge_index):
        import jax, jax.numpy as jnp
        import numpy as np
        N_NODES = 625
        D = 768
        N_EDGES = 10000

        def gcn_conv(x, W, b, src, dst, n_nodes):
            h = x @ W
            deg = jax.ops.segment_sum(jnp.ones_like(dst, dtype=h.dtype), dst, num_segments=n_nodes)
            dinv = jnp.where(deg > 0, jax.lax.rsqrt(deg), 0.0)
            norm = dinv[src] * dinv[dst]
            msgs = h[src] * norm[:, None]
            out = jax.ops.segment_sum(msgs, dst, num_segments=n_nodes)
            return out + b

        def add_self_loops(edge_index, n_nodes):
            loop = jnp.arange(n_nodes, dtype=edge_index.dtype)
            src = jnp.concatenate([edge_index[0], loop])
            dst = jnp.concatenate([edge_index[1], loop])
            return (src, dst)
        n = x.shape[0]
        src, dst = add_self_loops(edge_index, n)
        h = gcn_conv(x, W1, b1, src, dst, n)
        h = jax.nn.relu(h)
        out = gcn_conv(h, W2, b2, src, dst, n)
        return out

    def _L1_ffn_ref(hidden_states, router_w, w1, w2):
        import jax, jax.numpy as jnp
        import numpy as np
        DECAY = 0.9
        EPS = 0.01
        TOP_K = 2
        B, S, H = hidden_states.shape
        E = router_w.shape[0]
        flat = hidden_states.reshape(B * S, H)
        logits = flat @ router_w.T
        probs = jax.nn.softmax(logits, axis=-1)
        topk_probs, topk_idx = jax.lax.top_k(probs, TOP_K)
        importance = jax.lax.stop_gradient(probs).sum(axis=0)
        running = jnp.ones((E,), dtype=flat.dtype)
        blended = running + (1.0 - DECAY) * (importance - running)
        running = blended + EPS
        balance = running[topk_idx]
        balanced = topk_probs / balance
        balanced = balanced / balanced.sum(axis=-1, keepdims=True)
        h = jnp.einsum('th,eih->tei', flat, w1)
        h = jax.nn.silu(h)
        outs = jnp.einsum('tei,ehi->teh', h, w2)
        sel = jnp.take_along_axis(outs, topk_idx[:, :, None], axis=1)
        combined = (sel * balanced[..., None]).sum(axis=1)
        return combined.reshape(B, S, H)

    def _L2_gnn_ref(x, edge_index, W1, att_src1, att_dst1, b1, W2, att_src2, att_dst2, b2):
        import jax, jax.numpy as jnp
        import numpy as np
        N_NODES = 625
        NEG_SLOPE = 0.2
        EPS = 1e-16

        def gat_layer(x, W, att_src, att_dst, bias, src, dst, heads, out_ch, concat):
            n = x.shape[0]
            h = (x @ W.T).reshape(n, heads, out_ch)
            a_src = jnp.einsum('nhc,hc->nh', h, att_src)
            a_dst = jnp.einsum('nhc,hc->nh', h, att_dst)
            e = a_src[src] + a_dst[dst]
            e = jax.nn.leaky_relu(e, NEG_SLOPE)
            m = jax.ops.segment_max(e, dst, num_segments=n)
            ex = jnp.exp(e - m[dst])
            denom = jax.ops.segment_sum(ex, dst, num_segments=n)
            alpha = ex / (denom[dst] + EPS)
            msg = alpha[:, :, None] * h[src]
            out = jax.ops.segment_sum(msg, dst, num_segments=n)
            if concat:
                out = out.reshape(n, heads * out_ch)
            else:
                out = out.mean(axis=1)
            return out + bias
        src, dst = (edge_index[0], edge_index[1])
        h = gat_layer(x, W1, att_src1, att_dst1, b1, src, dst, heads=8, out_ch=128, concat=True)
        h = jax.nn.relu(h)
        out = gat_layer(h, W2, att_src2, att_dst2, b2, src, dst, heads=1, out_ch=768, concat=True)
        return out

    def _L2_ffn_ref(X, slot_params, scale, W_down, b_down, W_up, b_up):
        import jax, jax.numpy as jnp
        import numpy as np
        EPS = 1e-06

        def l2_normalize(x, axis):
            norm = jnp.sqrt(jnp.square(x).sum(axis=axis, keepdims=True))
            return x * (1.0 / (norm + EPS))
        b, m, d = X.shape
        _, n, p = slot_params.shape
        Xn = l2_normalize(X, axis=-1)
        sp = l2_normalize(slot_params, axis=1) * scale
        logits = jnp.einsum('bmd,dnp->bmnp', Xn, sp)
        D = jax.nn.softmax(logits, axis=1)
        C = jax.nn.softmax(logits.reshape(b, m, n * p), axis=2).reshape(b, m, n, p)
        X_tilde = jnp.einsum('bmd,bmnp->bnpd', Xn, D)
        H = jax.nn.gelu(jnp.einsum('bnpd,ndh->bnph', X_tilde, W_down) + b_down[None, :, None, :], approximate=False)
        Y_tilde = jnp.einsum('bnph,nhd->bnpd', H, W_up) + b_up[None, :, None, :]
        Y = jnp.einsum('bnpd,bmnp->bmd', Y_tilde, C)
        return Y

    def _L3_gnn_ref(x, node_type, edge_index, edge_type, node_emb, w_rel1, w_root1, b1, w_rel2, w_root2, b2, w_rel3, w_root3, b3):
        import jax, jax.numpy as jnp
        import numpy as np
        NUM_NODES = 625
        NUM_EDGES = 10000
        IN_CH = 768
        TYPE_DIM = 128
        HID = 768
        OUT = 768
        NUM_REL = 3
        NUM_NODE_TYPE = 3

        def _glorot(key, shape):
            fan_in, fan_out = (shape[-2], shape[-1])
            lim = (6.0 / (fan_in + fan_out)) ** 0.5
            return jax.random.uniform(key, shape, jnp.float32, -lim, lim)

        def rgcn_conv(h, src, dst, edge_type, w_rel, w_root, bias):
            num_nodes = h.shape[0]
            xw = jnp.einsum('nd,rde->rne', h, w_rel)
            msg = xw[edge_type, src]
            onehot = jax.nn.one_hot(edge_type, NUM_REL, dtype=h.dtype)
            count = jax.ops.segment_sum(onehot, dst, num_segments=num_nodes)
            inv = jnp.where(count > 0, 1.0 / jnp.maximum(count, 1.0), 0.0)
            msg = msg * inv[dst, edge_type][:, None]
            agg = jax.ops.segment_sum(msg, dst, num_segments=num_nodes)
            return agg + h @ w_root + bias
        src, dst = (edge_index[0], edge_index[1])
        h = jnp.concatenate([x, node_emb[node_type]], axis=-1)
        h = jax.nn.relu(rgcn_conv(h, src, dst, edge_type, w_rel1, w_root1, b1))
        h = jax.nn.relu(rgcn_conv(h, src, dst, edge_type, w_rel2, w_root2, b2))
        h = jax.nn.relu(rgcn_conv(h, src, dst, edge_type, w_rel3, w_root3, b3))
        return h

    def _L3_ffn_ref(x, gate_w, w1, b1, w2, b2):
        import jax, jax.numpy as jnp
        import numpy as np
        EMBED = 768
        HIDDEN = 192
        N_EXPERTS = 8
        TOP_K = 2
        orig_shape = x.shape
        xf = x.reshape(-1, EMBED)
        T = xf.shape[0]
        logits = jnp.einsum('td,ed->te', xf, gate_w)
        probs = jax.nn.softmax(logits, axis=-1)
        top_w, top_i = jax.lax.top_k(probs, TOP_K)
        top_w = top_w / (top_w.sum(axis=-1, keepdims=True) + 1e-09)
        combine = jnp.zeros((T, N_EXPERTS), dtype=xf.dtype)
        combine = combine.at[jnp.arange(T)[:, None], top_i].add(top_w)
        h = jax.nn.gelu(jnp.einsum('td,edh->teh', xf, w1) + b1[None, :, :])
        y = jnp.einsum('teh,ehd->ted', h, w2) + b2[None, :, :]
        out = jnp.einsum('ted,te->td', y, combine)
        return out.reshape(orig_shape)
    edge_index = jnp.stack([src, dst])
    batch0 = jnp.zeros((625,), jnp.int32)
    x = x + _L0_gnn_ref(_layernorm(x, axis=-1), edge_index, batch0, L0_gnn_t, L0_gnn_W1, L0_gnn_b1, L0_gnn_bn_gamma, L0_gnn_bn_beta, L0_gnn_bn_mean, L0_gnn_bn_var, L0_gnn_W2, L0_gnn_b2)
    x = x + _L0_ffn_ref(_layernorm(x, axis=-1)[None], L0_ffn_gate_w, L0_ffn_w1, L0_ffn_b1, L0_ffn_w2, L0_ffn_b2)[0]
    x = x + _L1_gnn_ref(_layernorm(x, axis=-1), L1_gnn_W1, L1_gnn_b1, L1_gnn_W2, L1_gnn_b2, edge_index)
    x = x + _L1_ffn_ref(_layernorm(x, axis=-1)[None], L1_ffn_router_w, L1_ffn_w1, L1_ffn_w2)[0]
    x = x + _L2_gnn_ref(_layernorm(x, axis=-1), edge_index, L2_gnn_W1, L2_gnn_att_src1, L2_gnn_att_dst1, L2_gnn_b1, L2_gnn_W2, L2_gnn_att_src2, L2_gnn_att_dst2, L2_gnn_b2)
    x = x + _L2_ffn_ref(_layernorm(x, axis=-1)[None], L2_ffn_slot_params, L2_ffn_scale, L2_ffn_W_down, L2_ffn_b_down, L2_ffn_W_up, L2_ffn_b_up)[0]
    x = x + _L3_gnn_ref(_layernorm(x, axis=-1), node_type_3, edge_index, edge_type_3, L3_gnn_node_emb, L3_gnn_w_rel1, L3_gnn_w_root1, L3_gnn_b1, L3_gnn_w_rel2, L3_gnn_w_root2, L3_gnn_b2, L3_gnn_w_rel3, L3_gnn_w_root3, L3_gnn_b3)
    x = x + _L3_ffn_ref(_layernorm(x, axis=-1)[None], L3_ffn_gate_w, L3_ffn_w1, L3_ffn_b1, L3_ffn_w2, L3_ffn_b2)[0]
    return x

_drawn_inputs = setup_inputs


def setup_inputs(seed=0):
    import zlib

    import numpy as np

    out = dict(_drawn_inputs(seed))
    spreads = {'L0_gnn_bn_gamma': (1.0, 0.2),
     'L0_gnn_bn_beta': (0.0, 0.375),
     'L0_gnn_bn_mean': (0.0, 0.345),
     'L0_gnn_bn_var': (1.0, 0.6),
     'L0_ffn_b1': (0.0, 0.8),
     'L0_ffn_b2': (0.0, 0.1),
     'L1_gnn_b1': (0.0, 0.1),
     'L1_gnn_b2': (0.0, 0.1),
     'L2_gnn_b1': (0.0, 0.287),
     'L2_gnn_b2': (0.0, 0.1),
     'L2_ffn_b_down': (0.0, 0.754),
     'L2_ffn_b_up': (0.0, 0.429),
     'L3_gnn_b1': (0.0, 0.1),
     'L3_gnn_b2': (0.0, 0.267),
     'L3_gnn_b3': (0.0, 0.275),
     'L3_ffn_b1': (0.0, 0.8),
     'L3_ffn_b2': (0.0, 0.29)}
    factors = {'L0_gnn_b1': 8.0,
     'L0_gnn_b2': 6.077,
     'L1_ffn_router_w': 3.007,
     'L1_ffn_w1': 2.703,
     'L2_gnn_att_dst1': 25.384,
     'L2_gnn_att_src2': 8.0,
     'L2_gnn_att_dst2': 31.635,
     'L2_ffn_slot_params': 8.0,
     'L2_ffn_W_down': 8.0,
     'L2_ffn_W_up': 5.672}
    for name, (base, spread) in spreads.items():
        noise = np.random.default_rng([zlib.crc32(name.encode()), seed]).standard_normal(out[name].shape)
        drawn = base * np.exp(spread * noise) if base else spread * noise
        out[name] = jnp.asarray(drawn.astype(out[name].dtype))
    for name, factor in factors.items():
        out[name] = (out[name] * factor).astype(out[name].dtype)
    return out
```

```python
import numpy as np
import concourse.bass as bass
import concourse.mybir as mybir
from concourse.alu_op_type import AluOpType as ALU
from contextlib import ExitStack

f32, f32r = mybir.dt.float32, mybir.dt.float32r
bf16, i16, i32, u32 = mybir.dt.bfloat16, mybir.dt.int16, mybir.dt.int32, mybir.dt.uint32
ACT = mybir.ActivationFunctionType
AX = mybir.AxisListType

P = 128
NODES, D = 625, 768
NT, TN = 5, 125
NP = NODES + 1
CH = [(0, 314), (314, 312)]
KD = D // P
EDGES = 10000
ET = EDGES // TN
TYPE_DIM = 128
D1 = D + TYPE_DIM
K1 = D1 // P
RELS = 3
EXPERTS = 8
HEADS, HEAD_DIM = 8, 128
SLOTS = 32
SLOT_H = 96
UNIT, UNIT_WIDE = 768, 896
RING = 3
SMALL = 568
EXPERT_LAG = 4
LN_EPS = 1e-5
FAR = -1e30

UP_UNITS = dict(g0=12, f0=12, f1=8, f3=12)
DOWN = {
    "g0d": (12, 384, 2, 2), "f0d": (12, 384, 2, 2), "g1a": (6, 384, 2, 2), "g1b": (6, 384, 2, 2),
    "f1d": (8, 384, 2, 2), "g2a": (6, 256, 4, 3), "g2b": (8, 384, 2, 2),
    "g3a": (K1, 448, 2, 2), "g3b": (K1, 384, 2, 2), "g3c": (KD, 384, 2, 2), "f3d": (12, 384, 2, 2),
}
FEEDS = RELS + 1


def down_units(key):
    k, _, chunks, per = DOWN[key]
    n = k * chunks * (FEEDS if key in ("g3a", "g3b", "g3c") else 1)
    assert n % per == 0
    return n // per


SEQ_A = [("u", "g0"), ("d", "g0d"), ("u", "f0"), ("d", "f0d"), ("d", "g1a"), ("d", "g1b"),
         ("u", "f1"), ("d", "f1d"), ("d", "g2a"), ("d", "g2b")]
SEQ_B = [("d", "g3a")]
SEQ_C = [("d", "g3b"), ("d", "g3c"), ("u", "f3"), ("d", "f3d")]
FIRST_UNIT, at = {}, 0
for kind, key in SEQ_A + SEQ_B + SEQ_C:
    FIRST_UNIT[kind, key] = at
    at += UP_UNITS[key] if kind == "u" else down_units(key)
UNITS_A, UNITS_B = FIRST_UNIT["d", "g3a"], down_units("g3a")
UNITS = at
UNITS_C = UNITS - UNITS_A - UNITS_B

COLS, at = {}, 0
for name, n in [("bn_b1", 12), ("bn_gamma", 12), ("bn_beta", 12), ("bn_mean", 12), ("bn_var", 12),
                ("f0_b1", 12), ("f3_b1", 12), ("g2_b1", 8), ("f0_gate", 48), ("f1_gate", 48),
                ("f3_gate", 48), ("slots", KD * SLOTS), ("b_down", 8)]:
    COLS[name] = (at, at + n)
    at += n
NCOLS = at


def plan_groups():
    groups = []
    where = {}

    def add(label, idx, sem, value):
        where[label, idx] = len(groups)
        groups.append((sem, value))

    def several(label, n, sem, first=0, per=1):
        for i in range(n):
            add(label, i, sem, first + (i + 1) * per)

    def sweep(label):
        for c in range(2):
            for s in range(NT):
                add(label, c * NT + s, label + "_counted", c * NT + s + 1)

    def ffn(f, tiles):
        several(f + "_xT", 2 * NT, f + "_xT_low")
        several(f + "_router", NT, f + "_routed")
        jobs, lag = 2 * tiles, EXPERT_LAG
        for j in range(jobs + lag):
            if j < jobs:
                add(f + "_hidden", j, f + "_activated", j + 1)
            if j == lag - 1:
                if f == "f1":
                    add(f + "_importance", 0, f + "_importance_read", 1)
                several(f + "_cT", NT, f + "_combineT")
            if j >= lag:
                add(f + "_cB", j - lag, f + "_weighted", j - lag + 1)
        several(f + "_down", 2 * NT, f + "_x")

    several("g0_xT", 2 * NT, "g0_xT_low")
    add("g0_maxT", 0, "g0_max_read", 1)
    add("g0_maxB", 0, "g0_maxB_read", 1)
    sweep("A")
    for j in range(2 * KD):
        add("g0_num", j, "g0_num_read", j + 1)
        add("g0_den", j, "g0_den_read", j + 1)
    several("g0_hidden", 24, "g0_activated")
    several("g0d", 2 * NT, "g0_x")
    ffn("f0", 12)
    several("g1_deg", 2, "g1_deg_read")
    several("g1_dinv", NT, "g1_dinv_read")
    several("g1a_agg", 2 * KD, "g1a_scaled")
    several("g1a", 2 * NT, "g1a_read")
    several("g1b_agg", 2 * KD, "g1b_scaled")
    several("g1b", 2 * NT, "g1_x")
    ffn("f1", 8)
    several("g2_xT", 2 * NT, "g2_xT_low")
    several("g2_maskT", NT * NT, "g2_masked")
    several("g2a", 4 * NT, "g2_h1")
    for layer, heads in (("g2p", HEADS), ("g2q", 1)):
        several(layer + "_asT", NT, layer + "_asT_read")
        several(layer + "_asB", 2 * heads, layer + "_asB_read")
        several(layer + "_uvT", 2 * NT, layer + "_uvT_read")
        for h in range(heads):
            for i in range(4):
                add(layer + "_uvB", 4 * h + i, layer + "_uvB_read", 4 * h + i + 1)
            if layer == "g2p" and h:
                for c in range(2):
                    add("g2p_den", 2 * (h - 1) + c, "g2p_den_read", 2 * (h - 1) + c + 1)
                    add("g2p_agg", 2 * (h - 1) + c, "g2p_agg_read", 2 * (h - 1) + c + 1)
        if layer == "g2p":
            for c in range(2):
                add("g2p_den", 2 * (HEADS - 1) + c, "g2p_den_read", 2 * (HEADS - 1) + c + 1)
                add("g2p_agg", 2 * (HEADS - 1) + c, "g2p_agg_read", 2 * (HEADS - 1) + c + 1)
            several("g2b", 2 * NT, "g2_h2")
    several("g2q_agg", 2 * NT, "g2_x")
    several("f2_xT", 2 * NT, "f2_xT_low")
    several("f2_logits", NT, "f2_logits_read")
    several("f2_logitsT", NT, "f2_logitsT_read")
    several("f2_dispatch", NT, "f2_dispatch_read")
    several("f2_combineT", NT, "f2_combineT_read")
    several("f2_tilde", KD, "f2_tilde_read")
    several("f2_hidden", 1, "f2_hidden_read")
    several("f2_up", 2, "f2_up_read")
    several("f2_down", 2 * NT, "f2_x")
    several("g3_emb", NT, "g3_emb_low")
    for r in range(RELS):
        sweep(f"R{r}")
    for key, k in (("g3a", K1), ("g3b", K1), ("g3c", KD)):
        several(key + "_hT", 2 * NT, key + "_hT_low")
        several(key + "_root", 2 * NT, key + "_acc", 0)
        for r in range(RELS):
            several(f"{key}_deg{r}", 2, f"{key}_deg_read", 2 * r)
            several(f"{key}_agg{r}", 2 * k, f"{key}_scaled", 2 * k * r)
            several(f"{key}_rel{r}", 2 * NT, key + "_acc", 2 * NT * (r + 1))
    ffn("f3", 12)
    return groups, where


GROUPS, WHERE = plan_groups()


def families():
    table = {}

    def family(kind, totals):
        base = 0
        for layer, total in totals:
            table[layer + "_" + kind] = (kind, base)
            base += total

    def each(layers, total):
        return [(s, total) for s in layers.split()]

    for kind, n in (("var", 1), ("std", 1), ("xn", NT)):
        family(kind, each("g0 f0 g1 f1 g2 f2 g3 f3", n))
    for half in ("high", "low"):
        family("T_" + half, each("g0_x f0_x f1_x g2_x f2_x g3a_h g3b_h g3c_h f3_x", 2 * NT))
        for layer in "g0_x f0_x f1_x g2_x f2_x g3a_h g3b_h g3c_h f3_x".split():
            table[layer + "T_" + half] = table.pop(layer + "_T_" + half)
        family(half, [("g0", 24), ("f0", 24), ("g1a", 12), ("g1b", 12), ("f1", 16), ("g2p", 16),
                      ("g3a", 6 * K1), ("g3b", 6 * K1), ("g3c", 6 * KD), ("f3", 24)])
        family("nodes_" + half, [("g1", NT), ("g1b", 2 * NT), ("g3a", NT), ("g3b", NT), ("g3c", NT)])
    family("T_pad", each("g0_x f0_x f1_x g2_x g3a_h g3b_h g3c_h f3_x", 2))
    for layer in "g0_x f0_x f1_x g2_x g3a_h g3b_h g3c_h f3_x".split():
        table[layer + "T_pad"] = table.pop(layer + "_T_pad")
    family("scaled", [("g1a", 12), ("g1b", 12), ("g3a", 6 * K1), ("g3b", 6 * K1), ("g3c", 6 * KD)])
    family("activated", [("g0", 24), ("f0", 24), ("f1", 16), ("f3", 24)])
    family("weighted", [("f0", 24), ("f1", 16), ("f3", 24)])
    family("x", each("g0 f0 g1 f1 g2 f2", 2 * NT) + [("g3", NT), ("f3", 2 * NT)])
    for kind, n in (("routed", NT), ("shifted", 1), ("exp", 1), ("probs", 1), ("combine", 1), ("cT_pad", 1),
                    ("combineT", NT), ("cpad_clear", 1)):
        family(kind, each("f0 f1 f3", n))
    family("bias_full", [("g0", 16), ("f0", 64), ("g1", 16), ("g1b", 16), ("g2", 16), ("f2", 16), ("g3a", 16),
                         ("g3b", 16), ("g3c", 16), ("f3", 64)])
    family("rows_clear", each("f0 f3", 1))
    family("hot", each("A R0 R1 R2", 4 * ET))
    family("hot_used", each("A R0 R1 R2", 2 * (ET - 1)))
    family("counted", each("A R0 R1 R2", 2 * NT))
    family("nodes", each("g3b g3c", NT))
    family("acc", each("g3a g3b g3c", 2 * NT * FEEDS))
    family("deg_read", each("g3a g3b g3c", 2 * RELS))
    for kind, n in (("asB_read", 2), ("max_done", NT), ("uvB_read", 4), ("shift", NT), ("leaky", NT), ("powers", 1),
                    ("prob", 1)):
        family(kind, [("g2p", n * HEADS), ("g2q", n)])
    for kind, n in (("asT_read", NT), ("uvT_read", 2 * NT), ("uv", 2), ("pads", 3)):
        family(kind, each("g2p g2q", n))
    return table


FAMILY = families()


def network(nc, x_in, edges_in, wa, wb, wc, cols_in, bias_in, rows_in, att_in, scalars_in, w_down_in,
            w_up_in, emb_in, types_in, out):
    ctx = ExitStack()
    with ctx:
        sems = {}

        def S(event):
            name = FAMILY.get(event, (event, 0))[0]
            if name not in sems:
                sems[name] = ctx.enter_context(nc.semaphore(name))
            return sems[name]

        def E(event, count):
            return S(event), count + FAMILY.get(event, (event, 0))[1]

        arena_bytes = 212800
        start = -(-nc.sbuf_base // 64) * 64
        arena = ctx.enter_context(nc.sbuf_tensor("arena", [P, arena_bytes], mybir.dt.uint8))
        top = [start]

        def up32(n):
            return -(-n // 32) * 32

        def region(nbytes):
            off = top[0]
            top[0] += up32(nbytes)
            assert top[0] <= start + arena_bytes, (top[0] - start, arena_bytes)
            return off

        size = {f32: 4, f32r: 4, i32: 4, u32: 4, bf16: 2, i16: 2}

        def at_(name, shape, dt, off):
            return nc.alloc_sbuf_tensor_at(name, shape, dt, offset=off)

        def new(name, shape, dt=f32):
            return at_(name, shape, dt, region(int(np.prod(shape[1:])) * size[dt]))

        x = new("x", [TN, NT, D])
        XT = region(2 * up32(K1 * NP * 4) + 64)
        HT = region(2 * 12 * NP * 4)
        NM = region(2 * NT * D1 * 4)
        xt_lo_off = XT + up32(K1 * NP * 4)
        xT_hi, xT_lo = at_("xT_hi", [P, K1, NP], f32r, XT), at_("xT_lo", [P, K1, NP], f32r, xt_lo_off)
        ht_lo_off = HT + 12 * NP * 4
        hT_hi, hT_lo = at_("hT_hi", [P, 12, NP], f32r, HT), at_("hT_lo", [P, 12, NP], f32r, ht_lo_off)
        nm_hi = at_("nm_hi", [TN, NT, D1], f32r, NM)
        nm_lo = at_("nm_lo", [TN, NT, D1], f32r, NM + NT * D1 * 4)
        xn = at_("xn", [TN, NT, D], f32, HT)
        e_hi = at_("e_hi", [TN, NT, D], f32r, HT + 15360)
        e_lo = at_("e_lo", [TN, NT, D], f32r, HT + 30720)
        acc = at_("acc", [TN, NT, D1], f32, HT)
        rel = at_("rel", [TN, RELS, NT, NP], f32r, HT + 17920)
        OH = HT + 17920 + up32(RELS * NT * NP * 4)
        OSLOTS = 2
        src_hot = at_("src_hot", [TN, OSLOTS, NODES], bf16, OH)
        dst_hot = at_("dst_hot", [TN, OSLOTS, CH[0][1]], bf16, OH + 2528)
        assert OH + 2528 + OSLOTS * CH[0][1] * 2 <= NM
        h1 = at_("h1", [TN, NT, HEADS * HEAD_DIM], f32, NM)
        maskT = at_("maskT", [TN, NT, NP], bf16, NM + 20480)
        gat_small = NM + 20480 + up32(NT * NP * 2)
        h2 = at_("h2", [TN, NT, D + 2], f32, NM)
        prob = [at_(f"prob{i}", [TN, NT, NP], f32, XT + i * up32(NT * NP * 4)) for i in range(2)]
        uB = [at_(f"uB{i}", [TN, 2, NP], f32, XT + 2 * up32(NT * NP * 4) + i * up32(2 * NP * 4)) for i in range(2)]
        att = at_("att", [TN, 2, HEADS * HEAD_DIM], f32, HT + 8 * NP * 4)
        w_down = at_("w_down", [P, EXPERTS, KD, SLOT_H], f32, HT + 15360)
        w_up = at_("w_up", [SLOT_H, EXPERTS, D], f32, HT + 15360 + 18432)
        sp_hi = at_("sp_hi", [P, KD, SLOTS], f32r, XT + up32(KD * NP * 4))
        sp_lo = at_("sp_lo", [P, KD, SLOTS], f32r, xt_lo_off + up32(KD * NP * 4))

        adj = new("adj", [TN, NT, NP], f32r)
        raw = new("raw", [P, RING, UNIT_WIDE])
        w_hi = new("w_hi", [P, RING, UNIT_WIDE], f32r)
        w_lo = new("w_lo", [P, RING, UNIT_WIDE], f32r)
        bias_off = region(D1 * 4)
        bias = at_("bias", [TN, D1], f32, bias_off)
        bias8 = at_("bias8", [P, D], f32, bias_off)
        TSLOTS = 4
        tmp_off = region(TSLOTS * CH[0][1] * 4)
        tmp = at_("tmp", [P, TSLOTS, CH[0][1]], f32, tmp_off)
        iota = new("iota", [TN, NP], i16)
        ident = new("ident", [P, P])
        ones_r = new("ones_r", [P, P], f32r)
        ones = ones_r[:].bitcast(f32)
        scale_off = region(NP * 4)
        dscale = at_("dscale", [P, NP], f32, scale_off)
        cT = at_("cT", [P, NP], f32, scale_off)
        pat = new("pat", [P, 3, P])
        cols = new("cols", [P, NCOLS])
        gate_hi = new("gate_hi", [P, 3 * 48], f32r)
        gate_lo = new("gate_lo", [P, 3 * 48], f32r)
        e_int = at_("e_int", [TN, 3, ET], i32, NM)
        edge = new("edge", [TN, 3, ET])
        small = new("small", [P, SMALL])
        sp_tmp = at_("sp_tmp", [P, KD, SLOTS], f32, tmp_off)

        used_small = [0]

        def sm(n):
            a = used_small[0]
            used_small[0] += n
            assert used_small[0] <= SMALL
            return small[:, a:a + n]

        stats, moments, rstd = sm(NT * 12), sm(NT * 2), sm(NT)
        t_col, slot_scale = sm(1), sm(1)
        dinv = sm(NT)
        peak, peak_all = sm(8), sm(2)
        bn_s, bn_b = sm(12), sm(12)
        iota8, rel_index = sm(8), sm(1)
        logit8, prob8, hot8, top8, idx8f = (sm(NT * 8) for _ in range(5))
        sum8, run8 = sm(NT), sm(8)
        sel8 = sm(SLOTS)
        a_src, a_dst, a_src5, a_max = (sm(NT * 8) for _ in range(4))
        a_top, no_edge = sm(8), sm(NT)
        a_part = sm(NT * 4)
        idx8 = new("idx8", [P, NT * 8], u32)
        cpad = at_("cpad", [TN, NT, P], f32, xt_lo_off + up32(KD * NP * 4))
        emb = at_("emb", [RELS, TYPE_DIM], f32, tmp_off + 3200)
        asT = at_("asT", [HEADS, NP], f32, gat_small)
        uT = at_("uT", [HEADS, NP], f32, gat_small + up32(NP * 4))
        vT = at_("vT", [HEADS, NP], f32, gat_small + 2 * up32(NP * 4))
        assert gat_small + 3 * up32(NP * 4) <= NM + 2 * NT * D1 * 4
        head_sel = at_("head_sel", [HEADS, HEADS, P], f32, ht_lo_off + 8 * NP * 4)
        uv = at_("uv", [TN, 2, NT, 8], f32, ht_lo_off + 8 * NP * 4 + 4096)
        asB = uB[0]
        junk = at_("junk", [TN, D], f32, ht_lo_off + 8 * NP * 4 + 4096 + 512)
        edge_scores = at_("edge_scores", [TN, 2, NP], f32, tmp_off)
        e_full = [at_(f"e_full{i}", [TN, D], f32, HT + 46080 + i * 3072) for i in range(2)]
        g0_junk = at_("g0_junk", [TN, D], f32, tmp_off)
        f2s = [NM]

        def f2_new(name, shape):
            off = f2s[0]
            f2s[0] += up32(int(np.prod(shape[1:])) * 4)
            assert f2s[0] <= NM + 2 * NT * D1 * 4
            return at_(name, shape, f32, off)

        slot_logits = f2_new("slot_logits", [TN, NT, SLOTS])
        combine = f2_new("combine", [TN, NT, SLOTS])
        dispatch = f2_new("dispatch", [TN, NT, SLOTS])
        logitsT, combineT = f2_new("logitsT", [SLOTS, NP]), f2_new("combineT", [SLOTS, NP])
        tildeT = f2_new("tildeT", [P, KD, SLOTS])
        slot_hidden = f2_new("slot_hidden", [SLOT_H, EXPERTS, 4])
        hidden_diag = f2_new("hidden_diag", [SLOT_H, EXPERTS * 36])
        slot_out = f2_new("slot_out", [SLOTS, D])
        slot_sum, col_peak, col_sum = f2_new("slot_sum", [P, KD * 4]), f2_new("col_peak", [TN, NT]), f2_new("col_sum", [TN, NT])
        row_peak, row_sum = f2_new("row_peak", [SLOTS, 1]), f2_new("row_sum", [SLOTS, 1])
        f2_junk = f2_new("f2_junk", [TN, D])
        node_type_i = at_("node_type_i", [RELS, NODES], i32, tmp_off)
        types = at_("types", [TN, ET], f32, tmp_off + 2560)
        src_plus = at_("src_plus", [TN, ET], f32, tmp_off + 2880)
        type_hot = at_("type_hot", [RELS, NODES], f32, scale_off)

        banks = [ctx.enter_context(nc.psum_tensor(f"bank{b}", [P, 512], f32)) for b in range(8)]
        block = ctx.enter_context(nc.Block())

        def bank(label, i):
            return banks[WHERE[label, i] % 8]

        def col(name, i=None):
            a, b = COLS[name]
            return cols[:, a:b] if i is None else cols[:, a + i:a + i + 1]

        def await_group(engine, label, i):
            engine.wait_ge(*E("group_closed", WHERE[label, i] + 1))

        def f(ap):
            return ap.bitcast(f32)

        node_view = "(n p) d -> p n d"

        def ring_units(engine, first, count, body):
            last = first + count
            q0, q1 = -(-first // RING), last // RING
            for u in range(first, q0 * RING):
                body(u, u // RING, u % RING)
            with engine.Fori(q0, q1) as q:
                for k in range(RING):
                    body(q * RING + k, q, k)
            for u in range(q1 * RING, last):
                body(u, u // RING, u % RING)

        SEGMENTS = [(0, UNITS_A, wa, UNIT), (UNITS_A, UNITS_B, wb, UNIT_WIDE),
                    (UNITS_A + UNITS_B, UNITS_C, wc, UNIT)]

        @block.sync
        def _(sp):
            sp.dma_start(x[:], x_in.rearrange(node_view, p=TN)).then_inc(S("x_loaded"), 16)
            sp.dma_start(e_int[:], edges_in).then_inc(S("edges_loaded"), 16)
            sp.dma_start(cols[:], cols_in).then_inc(S("cols_loaded"), 16)

            def load(first, src, width):
                def body(u, q, k):
                    sp.wait_ge(*E("unit_split", u - RING + 1))
                    sp.dma_start(raw[:, k, 0:width], src[bass.ds(u - first, 1)].rearrange("a p n -> (a p) n")
                                 ).then_inc(S(f"raw_full{k}"), 16)
                return body

            for k in range(RING):
                sp.dma_start(raw[:, k, 0:UNIT], wa[k]).then_inc(S(f"raw_full{k}"), 16)
            ring_units(sp, RING, UNITS_A - RING, load(0, wa, UNIT))
            sp.wait_ge(*E("g2q_uvB_read", 4))
            for e in range(EXPERTS):
                sp.dma_start(w_down[:, e], w_down_in[e].rearrange("(k p) h -> p k h", p=P)
                             ).then_inc(S("slot_weights"), 16)
            sp.dma_start(w_up[:], w_up_in.rearrange("e h d -> h e d")).then_inc(S("slot_weights"), 16)
            ring_units(sp, UNITS_A, UNITS_B, load(UNITS_A, wb, UNIT_WIDE))
            ring_units(sp, UNITS_A + UNITS_B, UNITS_C, load(UNITS_A + UNITS_B, wc, UNIT))
            for c in range(2):
                sp.wait_ge(*E("f3_x", NT * (c + 1)))
                sp.dma_start(out.rearrange(node_view, p=TN)[:, :, c * 384:(c + 1) * 384],
                             x[:, :, c * 384:(c + 1) * 384]).then_inc(S("stored"), 16)
            sp.wait_ge(*E("stored", 32))

        @block.gpsimd
        def _(pool):
            pool.iota(iota[:], pattern=[[1, NP]], base=0, channel_multiplier=0).then_inc(S("consts"), 1)
            pool.iota(idx8[:, 0:8].bitcast(i32), pattern=[[1, 8]], base=0, channel_multiplier=0).then_inc(S("consts"), 1)
            pool.iota(idx8[:, 8:9].bitcast(i32), pattern=[[0, 1]], base=0, channel_multiplier=1).then_inc(S("consts"), 1)
            pool.memset(ones, 1.0).then_inc(S("blanks"), 1)
            pool.memset(pat[:], 0.0).then_inc(S("blanks"), 1)
            pool.memset(sel8[0:8, :], 1.0).then_inc(S("blanks"), 1)
            pool.wait_ge(*E("blanks", 3))
            pool.affine_select(out=ident[:], in_=ones, compare_op=ALU.is_equal, fill=0.0, base=0,
                               pattern=[[-1, P]], channel_multiplier=1).then_inc(S("consts"), 1)
            pool.affine_select(out=sel8[0:8, :].rearrange("p (e s) -> p e s", e=8),
                               in_=sel8[0:8, :].rearrange("p (e s) -> p e s", e=8), compare_op=ALU.is_equal,
                               fill=0.0, base=0, pattern=[[-1, 8], [0, 4]], channel_multiplier=1
                               ).then_inc(S("consts"), 1)
            made = 5
            for q in range(4):
                rows = slice(32 * q, 32 * q + 2)
                for kind, a, b, first in ((0, 0, P, True), (1, 0, 64, True), (1, 64, P, False), (2, 0, P, False)):
                    pool.wait_ge(*E("consts", made))
                    made += 1
                    pool.affine_select(out=pat[rows, kind, a:b], in_=ones[rows, a:b],
                                       compare_op=ALU.is_equal, fill=0.0, base=0 if first else -1,
                                       pattern=[[0, b - a]], channel_multiplier=1).then_inc(S("consts"), 1)

            pool.wait_ge(*E("consts", made))

            def split(width):
                def body(u, q, k):
                    pool.wait_ge(*E(f"raw_full{k}", 16 * q + 16))
                    if not (isinstance(u, int) and u < RING):
                        pool.wait_ge(*E("unit_used", u - RING + 1))
                    pool.tensor_tensor(w_hi[:, k, 0:width], raw[:, k, 0:width],
                                       ones[:, 0:1].to_broadcast([P, width]), ALU.mult).then_inc(S("unit_high"), 1)
                    pool.wait_ge(*E("unit_high", u + 1))
                    pool.tensor_tensor(w_lo[:, k, 0:width], raw[:, k, 0:width], f(w_hi[:, k, 0:width]),
                                       ALU.subtract).then_inc(S("unit_split"), 1)
                return body

            for u in range(RING):
                split(UNIT)(u, 0, u)
            ring_units(pool, RING, UNITS_A - RING, split(UNIT))
            ring_units(pool, UNITS_A, UNITS_B, split(UNIT_WIDE))
            ring_units(pool, UNITS_A + UNITS_B, UNITS_C, split(UNIT))

        @block.scalar
        def _(act):
            done = [0]

            def link(ins):
                done[0] += 1
                ins.then_inc(S("act_step"), 1)
                act.wait_ge(*E("act_step", done[0]))

            def fill_bias(name, row, width):
                act.dma_start(bias[:, 0:width], bias_in[row:row + 1, 0:width].to_broadcast([TN, width])
                              ).then_inc(S(name), 16)

            def fill_pairs(name, row):
                for q in range(4):
                    act.dma_start(bias8[32 * q:32 * q + 2, :], rows_in[row + 2 * q:row + 2 * q + 2, :]
                                  ).then_inc(S(name), 16)

            def root_of_variance(s):
                act.wait_ge(*E(s + "_var", 1))
                act.activation(rstd[0:TN], rstd[0:TN], ACT.Sqrt).then_inc(S(s + "_std"), 1)

            def xT_high(label, k):
                for i in range(2 * NT):
                    n, (a, b) = i // 2, ((0, 4), (4, k))[i % 2]
                    await_group(act, label, i)
                    act.activation(xT_hi[:, a:b, n * TN:(n + 1) * TN],
                                   bank(label, i)[:, 0:(b - a) * TN].rearrange("p (k n) -> p k n", n=TN),
                                   ACT.Copy).then_inc(S(label + "_high"), 1)

            def nodes_high(full, width, src, high):
                for n in range(NT):
                    act.wait_ge(*E(full, n + 1))
                    act.activation(nm_hi[:, n, 0:width], src[:, n, 0:width], ACT.Copy).then_inc(S(high), 1)

            def messages_high(key, k, first=0):
                for j in range(first, first + 2 * k):
                    ft, (c0, cn) = (j - first) // 2, CH[(j - first) % 2]
                    act.wait_ge(*E(key + "_scaled", j + 1))
                    act.activation(xT_hi[:, ft, c0:c0 + cn], tmp[:, j % TSLOTS, 0:cn], ACT.Copy
                                   ).then_inc(S(key + "_high"), 1)

            def counts(label, target):
                for i in range(2 * NT):
                    c0, cn = CH[i // NT]
                    await_group(act, label, i)
                    act.activation(target[:, i % NT, c0:c0 + cn], bank(label, i)[0:TN, 0:cn], ACT.Copy
                                   ).then_inc(S(label + "_counted"), 1)

            def hidden(s, tiles, func, scale_bias, full):
                jobs = 2 * tiles
                for j in range(jobs + 3):
                    if j < jobs:
                        cn = CH[j % 2][1]
                        await_group(act, s + "_hidden", j)
                        if j >= TSLOTS:
                            act.wait_ge(*E(s + "_low", j - TSLOTS + 1))
                        act.activation(tmp[:, j % TSLOTS, 0:cn], bank(s + "_hidden", j)[:, 0:cn], func,
                                       **scale_bias(j // 2)).then_inc(S(s + "_activated"), 1)
                    if j >= 3:
                        i = j - 3
                        c0, cn = CH[i % 2]
                        act.wait_ge(*E(full, i + 1))
                        act.activation(hT_hi[:, i // 2, c0:c0 + cn], tmp[:, i % TSLOTS, 0:cn], ACT.Copy
                                       ).then_inc(S(s + "_high"), 1)

            def expert_layer(s, tiles, func, biased):
                root_of_variance(s)
                xT_high(s + "_xT", KD)
                act.wait_ge(*E(s + "_shifted", 1))
                act.activation(prob8[0:TN], prob8[0:TN], ACT.Exp).then_inc(S(s + "_exp"), 1)
                hidden(s, tiles, func, (lambda m: dict(bias=col(s + "_b1", m))) if biased else (lambda m: {}),
                       s + "_weighted")

            act.dma_start(t_col[0:TN, :], scalars_in[0:1, :].to_broadcast([TN, 1])).then_inc(S("scalars_loaded"), 16)
            act.dma_start(slot_scale, scalars_in[1:2, :].to_broadcast([P, 1])).then_inc(S("scalars_loaded"), 16)
            fill_bias("g0_bias_full", 0, D)
            act.wait_ge(*E("consts", 21))
            act.wait_ge(*E("cols_loaded", 16))
            act.activation(gate_hi[:], cols[:, COLS["f0_gate"][0]:COLS["f3_gate"][1]], ACT.Copy
                           ).then_inc(S("gates_high"), 1)
            act.wait_ge(*E("bn_var", 1))
            act.activation(bn_s, bn_s, ACT.Sqrt).then_inc(S("bn_std"), 1)

            root_of_variance("g0")
            xT_high("g0_xT", KD)
            act.wait_ge(*E("g0_maxB_read", 1))
            for n in range(NT):
                if n >= 2:
                    act.wait_ge(*E("g0_num_full", n - 1))
                act.activation(e_full[n % 2][:], xn[:, n], ACT.Exp, bias=peak_all[0:TN, 1:2], scale=t_col[0:TN, :]
                               ).then_inc(S("g0_exp"), 1)
                act.wait_ge(*E("g0_exp", n + 1))
                act.activation(e_hi[:, n], e_full[n % 2][:], ACT.Copy).then_inc(S("g0_exp_high"), 1)
                act.wait_ge(*E("g0_num_full", n + 1))
                act.activation(nm_hi[:, n, 0:D], xn[:, n], ACT.Copy).then_inc(S("g0_num_high"), 1)
            counts("A", adj)
            for j in range(2 * KD):
                c0, cn = CH[j % 2]
                act.wait_ge(*E("g0_sum", j + 1))
                act.activation(xT_hi[:, j // 2, c0:c0 + cn], tmp[:, j % 2, 0:cn], ACT.Copy
                               ).then_inc(S("g0_out_high"), 1)
            hidden("g0", 12, ACT.Relu, lambda m: dict(scale=bn_s[:, m:m + 1], bias=bn_b[:, m:m + 1]), "g0_activated")
            act.wait_ge(*E("f0_rows_clear", 1))
            fill_pairs("f0_bias_full", 0)
            expert_layer("f0", 12, ACT.Gelu, True)
            act.wait_ge(*E("f0_x", 2 * NT))
            fill_bias("g1_bias_full", 2, D)
            act.wait_ge(*E("g1_deg_read", 2))
            act.activation(dscale[:], dscale[:], ACT.Sqrt).then_inc(S("g1_dscale"), 1)
            root_of_variance("g1")
            nodes_high("g1_scaled_nodes", D, xn, "g1_nodes_high")
            act.wait_ge(*E("g1_bias_used", 1))
            fill_bias("g1b_bias_full", 1, D)
            messages_high("g1a", KD)
            for i in range(2 * NT):
                n, c = i % NT, i // NT
                act.wait_ge(*E("g1a_full", i + 1))
                act.activation(nm_hi[:, n, c * 384:(c + 1) * 384], xn[:, n, c * 384:(c + 1) * 384], ACT.Copy
                               ).then_inc(S("g1b_nodes_high"), 1)
            fill_bias("g2_bias_full", 3, D)
            messages_high("g1b", KD)
            expert_layer("f1", 8, ACT.Silu, False)
            act.dma_start(att[:], att_in[0:2, :].unsqueeze(0).to_broadcast([TN, 2, HEADS * HEAD_DIM])
                          ).then_inc(S("g2p_att_full"), 16)
            root_of_variance("g2")
            xT_high("g2_xT", KD)
            for i in range(4 * NT):
                n, c = i % NT, i // NT
                await_group(act, "g2a", i)
                act.activation(h1[:, n, c * 256:(c + 1) * 256], bank("g2a", i)[0:TN, 0:256], ACT.Copy
                               ).then_inc(S("g2_h1"), 1)

            def attention(layer, heads):
                for h in range(heads):
                    for c, (c0, cn) in enumerate(CH):
                        await_group(act, layer + "_asB", 2 * h + c)
                        if h >= 2:
                            act.wait_ge(*E(layer + "_max_done", NT * (h - 1)))
                        act.activation(asB[:, h % 2, c0:c0 + cn], bank(layer + "_asB", 2 * h + c)[0:TN, 0:cn],
                                       ACT.Copy).then_inc(S(layer + "_asB_read"), 1)
                act.wait_ge(*E(layer + "_max_done", NT * heads))

                def head_out(h):
                    for c, (c0, cn) in enumerate(CH):
                        j = 2 * h + c
                        act.wait_ge(*E("g2p_agg_read", j + 1))
                        act.activation(tmp[:, j % 2, 0:cn], tmp[:, j % 2, 0:cn], ACT.Relu, bias=col("g2_b1", h)
                                       ).then_inc(S("g2p_relu"), 1)
                        act.wait_ge(*E("g2p_relu", j + 1))
                        act.activation(hT_hi[:, h, c0:c0 + cn], tmp[:, j % 2, 0:cn], ACT.Copy
                                       ).then_inc(S("g2p_high"), 1)

                for h in range(heads):
                    for i in range(4):
                        c0, cn = CH[i % 2]
                        await_group(act, layer + "_uvB", 4 * h + i)
                        act.activation(uB[h % 2][:, i // 2, c0:c0 + cn], bank(layer + "_uvB", 4 * h + i)[0:TN, 0:cn],
                                       ACT.Copy).then_inc(S(layer + "_uvB_read"), 1)
                    act.wait_ge(*E(layer + "_uvB_read", 4 * h + 4))
                    for s in range(NT):
                        act.activation(prob[h % 2][:, s], uB[h % 2][:, 0], ACT.Identity,
                                       bias=a_src[0:TN, 8 * s + h:8 * s + h + 1]).then_inc(S(layer + "_shift"), 1)
                    act.wait_ge(*E(layer + "_leaky", NT * (h + 1)))
                    act.activation(prob[h % 2][:], prob[h % 2][:], ACT.Exp).then_inc(S(layer + "_powers"), 1)
                    if layer == "g2p" and h:
                        head_out(h - 1)
                if layer == "g2p":
                    head_out(heads - 1)

            attention("g2p", HEADS)
            act.wait_ge(*E("g2p_scores", 8 * 2 * NT))
            act.dma_start(att[:, :, 0:D], att_in[2:4, 0:D].unsqueeze(0).to_broadcast([TN, 2, D])
                          ).then_inc(S("g2q_att_full"), 16)
            for i in range(2 * NT):
                n, c = i % NT, i // NT
                await_group(act, "g2b", i)
                act.activation(h2[:, n, c * 384:(c + 1) * 384], bank("g2b", i)[0:TN, 0:384], ACT.Copy
                               ).then_inc(S("g2_h2"), 1)
            attention("g2q", 1)
            act.wait_ge(*E("g2_bias_used", 1))
            act.dma_start(bias8[0:8, :], rows_in[8:16, :]).then_inc(S("f2_bias_full"), 16)
            act.wait_ge(*E("slots_squared", 1))
            act.activation(slot_sum[:], slot_sum[:], ACT.Sqrt).then_inc(S("slots_norm"), 1)
            root_of_variance("f2")
            act.wait_ge(*E("f2_squared", NT))
            act.activation(sum8[0:TN], sum8[0:TN], ACT.Sqrt).then_inc(S("f2_norm"), 1)
            xT_high("f2_xT", KD)
            act.wait_ge(*E("f2_rows_shifted", 1))
            act.activation(combine[:], combine[:], ACT.Exp).then_inc(S("f2_row_exp"), 1)
            act.wait_ge(*E("f2_column_peak", 1))
            act.activation(logitsT[:, 0:NODES], logitsT[:, 0:NODES], ACT.Exp, bias=row_peak[:],
                           accum_out=row_sum[:]).then_inc(S("f2_column_exp"), 1)
            act.wait_ge(*E("f2_hidden_read", 1))
            act.wait_ge(*E("f2_diag_clear", 1))
            act.activation(hidden_diag[:].rearrange("p (e s) -> p e s", s=36)[:, :, 0:4], slot_hidden[:], ACT.Gelu
                           ).then_inc(S("f2_diag"), 1)
            act.wait_ge(*E("f2_up_read", 2))
            fill_bias("g3a_bias_full", 4, D1)
            act.dma_start(node_type_i[:], types_in.to_broadcast([RELS, NODES])).then_inc(S("types_loaded"), 16)
            act.dma_start(emb[:], emb_in).then_inc(S("emb_loaded"), 16)
            root_of_variance("g3")
            for r in range(RELS):
                counts(f"R{r}", rel[:, r])
            for key, k, full, prev in (("g3a", K1, "g3_emb_low", None), ("g3b", K1, "g3b_nodes", "g3a"),
                                       ("g3c", KD, "g3c_nodes", "g3b")):
                nodes_high(full, k * P, acc, key + "_nodes_high")
                xT_high(key + "_hT", k)
                for r in range(RELS):
                    messages_high(key, k, 2 * k * r)
                if key == "g3a":
                    act.wait_ge(*E("g3a_acc", 2 * NT))
                    fill_bias("g3b_bias_full", 5, D)
                elif key == "g3b":
                    act.wait_ge(*E("g3b_acc", 2 * NT))
                    fill_bias("g3c_bias_full", 6, D)
            act.wait_ge(*E("f3_rows_clear", 1))
            fill_pairs("f3_bias_full", 16)
            expert_layer("f3", 12, ACT.Gelu_apprx_tanh, True)

        @block.vector
        def _(dve):
            done = [0]

            def link(ins):
                done[0] += 1
                ins.then_inc(S("dve_step"), 1)
                dve.wait_ge(*E("dve_step", done[0]))

            TT, TS, STT = dve.tensor_tensor, dve.tensor_scalar, dve.scalar_tensor_tensor

            def layer_norm(s, dst):
                for n in range(NT):
                    for c in range(2):
                        last = dve.bn_stats(stats[0:TN, 12 * n + 6 * c:12 * n + 6 * c + 6], x[:, n, c * 384:(c + 1) * 384])
                link(last)
                for n in range(NT):
                    last = dve.bn_aggr(moments[0:TN, 2 * n:2 * n + 2], stats[0:TN, 12 * n:12 * n + 12])
                link(last)
                TS(rstd[0:TN], moments[0:TN].rearrange("p (n k) -> p n k", k=2)[:, :, 1], LN_EPS, None, ALU.add
                   ).then_inc(S(s + "_var"), 1)
                dve.wait_ge(*E(s + "_std", 1))
                link(dve.reciprocal(rstd[0:TN], rstd[0:TN]))
                for n in range(NT):
                    TS(dst(n), x[:, n], moments[0:TN, 2 * n:2 * n + 1], rstd[0:TN, n:n + 1], ALU.subtract, ALU.mult
                       ).then_inc(S(s + "_xn"), 1)
                dve.wait_ge(*E(s + "_xn", NT))

            def add_bias(s, n_cols=D):
                for n in range(NT):
                    last = TT(x[:, n], x[:, n], bias[:, 0:D], ALU.add)
                last.then_inc(S(s + "_bias_used"), 1)
                dve.wait_ge(*E(s + "_bias_used", 1))

            def clear_pad(name):
                dve.memset(f(xT_hi[:, :, NODES:NP]), 0.0).then_inc(S(name), 1)
                dve.memset(f(xT_lo[:, :, NODES:NP]), 0.0).then_inc(S(name), 1)

            def xT_low_half(label, k):
                clear_pad(label + "_pad")
                for i in range(2 * NT):
                    n, (a, b) = i // 2, ((0, 4), (4, k))[i % 2]
                    at = slice(n * TN, (n + 1) * TN)
                    dve.wait_ge(*E(label + "_high", i + 1))
                    TT(xT_lo[:, a:b, at], bank(label, i)[:, 0:(b - a) * TN].rearrange("p (k n) -> p k n", n=TN),
                       f(xT_hi[:, a:b, at]), ALU.subtract).then_inc(S(label + "_low"), 1)

            def nodes_low(width, src, high, low):
                for n in range(NT):
                    dve.wait_ge(*E(high, n + 1))
                    TT(nm_lo[:, n, 0:width], src[:, n, 0:width], f(nm_hi[:, n, 0:width]), ALU.subtract
                       ).then_inc(S(low), 1)

            def one_hots(label, source, destinations=edge[:, 1]):
                for c, (c0, cn) in enumerate(CH):
                    def hot(t, k):
                        TS(src_hot[:, k], iota[:, 0:NODES], source[:, bass.ds(t, 1)], None, ALU.is_equal
                           ).then_inc(S(label + "_hot"), 1)
                        TS(dst_hot[:, k, 0:cn], iota[:, c0:c0 + cn], destinations[:, bass.ds(t, 1)], None, ALU.is_equal
                           ).then_inc(S(label + "_hot"), 1)
                    if c:
                        await_group(dve, label, NT - 1)
                    for t in range(OSLOTS):
                        hot(t, t)
                    with dve.Fori(1, ET // OSLOTS) as q:
                        for k in range(OSLOTS):
                            dve.wait_ge(*E(label + "_hot_used", q * OSLOTS + k - OSLOTS + 1 + c * (ET - 1)))
                            hot(q * OSLOTS + k, k)

            def scaled_messages(key, label, k, first=0):
                jobs = 2 * k
                for i in range(jobs + 1):
                    if i < jobs:
                        c0, cn = CH[i % 2]
                        j = first + i
                        await_group(dve, label, i)
                        TT(tmp[:, j % TSLOTS, 0:cn], bank(label, i)[:, 0:cn], dscale[:, c0:c0 + cn], ALU.mult
                           ).then_inc(S(key + "_scaled"), 1)
                    if i >= 1:
                        ft, (c0, cn), j = (i - 1) // 2, CH[(i - 1) % 2], first + i - 1
                        dve.wait_ge(*E(key + "_high", j + 1))
                        TT(xT_lo[:, ft, c0:c0 + cn], tmp[:, j % TSLOTS, 0:cn], f(xT_hi[:, ft, c0:c0 + cn]),
                           ALU.subtract).then_inc(S(key + "_low"), 1)

            def add_to_nodes(s, label):
                for i in range(2 * NT):
                    n, c = i % NT, i // NT
                    at = slice(c * 384, (c + 1) * 384)
                    await_group(dve, label, i)
                    TT(x[:, n, at], bank(label, i)[0:TN, 0:384], x[:, n, at], ALU.add).then_inc(S(s + "_x"), 1)
                dve.wait_ge(*E(s + "_x", 2 * NT))

            def hidden_low(s, tiles, weigh):
                jobs = 2 * tiles
                for j in range(jobs + 1):
                    if j < jobs and weigh:
                        cn = CH[j % 2][1]
                        dve.wait_ge(*E(s + "_activated", j + 1))
                        await_group(dve, s + "_cB", j)
                        TT(tmp[:, j % TSLOTS, 0:cn], tmp[:, j % TSLOTS, 0:cn], bank(s + "_cB", j)[:, 0:cn], ALU.mult
                           ).then_inc(S(s + "_weighted"), 1)
                    if j >= 1:
                        i = j - 1
                        c0, cn = CH[i % 2]
                        dve.wait_ge(*E(s + "_high", i + 1))
                        TT(hT_lo[:, i // 2, c0:c0 + cn], tmp[:, i % TSLOTS, 0:cn], f(hT_hi[:, i // 2, c0:c0 + cn]),
                           ALU.subtract).then_inc(S(s + "_low"), 1)

            def bc(cols8, n=NT):
                return cols8.unsqueeze(2).to_broadcast([TN, n, 8])

            def v8(t):
                return t[0:TN].rearrange("p (n e) -> p n e", e=8)

            def route(s):
                dve.memset(cpad[:], 0.0).then_inc(S(s + "_cpad_clear"), 1)
                for n in range(NT):
                    await_group(dve, s + "_router", n)
                    dve.tensor_copy(logit8[0:TN, 8 * n:8 * n + 8], bank(s + "_router", n)[0:TN, 0:8]
                                    ).then_inc(S(s + "_routed"), 1)
                dve.wait_ge(*E(s + "_routed", NT))
                for n in range(NT):
                    last = dve.max(top8[0:TN, 8 * n:8 * n + 8], logit8[0:TN, 8 * n:8 * n + 8])
                link(last)
                TT(v8(prob8), v8(logit8), v8(top8)[:, :, 0:1].to_broadcast([TN, NT, 8]), ALU.subtract
                   ).then_inc(S(s + "_shifted"), 1)
                for n in range(NT):
                    last = dve.max_index(idx8[0:TN, 8 * n:8 * n + 8], top8[0:TN, 8 * n:8 * n + 8],
                                         logit8[0:TN, 8 * n:8 * n + 8])
                link(last)
                link(dve.tensor_copy(idx8f[0:TN], idx8[0:TN, 0:NT * 8]))
                experts = iota8[0:TN].unsqueeze(1).to_broadcast([TN, NT, 8])
                TT(v8(hot8), experts, v8(idx8f)[:, :, 0:1].to_broadcast([TN, NT, 8]), ALU.is_equal)
                link(TT(v8(logit8), experts, v8(idx8f)[:, :, 1:2].to_broadcast([TN, NT, 8]), ALU.is_equal))
                link(TT(hot8[0:TN], hot8[0:TN], logit8[0:TN], ALU.add))
                dve.wait_ge(*E(s + "_exp", 1))
                link(dve.tensor_reduce(sum8[0:TN], v8(prob8), AX.X, ALU.add))
                link(dve.reciprocal(sum8[0:TN], sum8[0:TN]))
                TT(v8(prob8), v8(prob8), bc(sum8[0:TN]), ALU.mult).then_inc(S(s + "_probs"), 1)
                dve.wait_ge(*E(s + "_probs", 1))
                link(TT(hot8[0:TN], hot8[0:TN], prob8[0:TN], ALU.mult))
                if s == "f1":
                    await_group(dve, "f1_importance", 0)
                    TS(run8[0:TN], bank("f1_importance", 0)[0:TN, 0:8], 1.0, 1.0 - 0.9, ALU.subtract, ALU.mult
                       ).then_inc(S("f1_importance_read"), 1)
                    dve.wait_ge(*E("f1_importance_read", 1))
                    link(TS(run8[0:TN], run8[0:TN], 1.0, 0.01, ALU.add, ALU.add))
                    link(dve.reciprocal(run8[0:TN], run8[0:TN]))
                    link(TT(v8(hot8), v8(hot8), run8[0:TN].unsqueeze(1).to_broadcast([TN, NT, 8]), ALU.mult))
                link(dve.tensor_reduce(sum8[0:TN], v8(hot8), AX.X, ALU.add))
                if s != "f1":
                    link(TS(sum8[0:TN], sum8[0:TN], 1e-9, None, ALU.add))
                link(dve.reciprocal(sum8[0:TN], sum8[0:TN]))
                link(TT(hot8[0:TN].rearrange("p (n e) -> p n e", e=8), v8(hot8), bc(sum8[0:TN]), ALU.mult))
                dve.wait_ge(*E(s + "_cpad_clear", 1))
                dve.tensor_copy(cpad[:].rearrange("p n (q s) -> p n q s", s=32)[:, :, :, 0:2],
                                hot8[0:TN].rearrange("p (n q s) -> p n q s", q=4, s=2)).then_inc(S(s + "_combine"), 1)
                dve.memset(cT[:, NODES:NP], 0.0).then_inc(S(s + "_cT_pad"), 1)
                for n in range(NT):
                    await_group(dve, s + "_cT", n)
                    dve.tensor_copy(cT[:, n * TN:(n + 1) * TN], bank(s + "_cT", n)[:, 0:TN]
                                    ).then_inc(S(s + "_combineT"), 1)

            def expert_layer(s, tiles):
                layer_norm(s, lambda n: xn[:, n])
                xT_low_half(s + "_xT", KD)
                route(s)
                hidden_low(s, tiles, True)
                add_to_nodes(s, s + "_down")

            dve.wait_ge(*E("consts", 21))
            dve.tensor_copy(iota8, idx8[:, 0:8])
            dve.tensor_copy(rel_index, idx8[:, 8:9])
            dve.wait_ge(*E("cols_loaded", 16))
            TS(bn_s, col("bn_var"), 1e-5, None, ALU.add).then_inc(S("bn_var"), 1)
            dve.wait_ge(*E("edges_loaded", 16))
            link(dve.tensor_copy(edge[:], e_int[:]))
            dve.wait_ge(*E("gates_high", 1))
            TT(gate_lo[:], cols[:, COLS["f0_gate"][0]:COLS["f3_gate"][1]], f(gate_hi[:]), ALU.subtract
               ).then_inc(S("gates_split"), 1)
            dve.wait_ge(*E("bn_std", 1))
            link(dve.reciprocal(bn_s, bn_s))
            TT(bn_b, col("bn_b1"), col("bn_mean"), ALU.subtract)
            link(TT(bn_s, bn_s, col("bn_gamma"), ALU.mult))
            link(TT(bn_b, bn_b, bn_s, ALU.mult))
            TT(bn_b, bn_b, col("bn_beta"), ALU.add).then_inc(S("bn_ready"), 1)

            dve.wait_ge(*E("x_loaded", 16))
            dve.wait_ge(*E("scalars_loaded", 32))
            layer_norm("g0", lambda n: xn[:, n])
            xT_low_half("g0_xT", KD)
            for n in range(NT):
                last = TT(x[:, n], x[:, n], xn[:, n], ALU.add)
            link(last)
            dve.wait_ge(*E("g0_bias_full", 16))
            add_bias("g0")
            dve.memset(bias8[:], 0.0).then_inc(S("f0_rows_clear"), 1)
            for n in range(NT):
                last = TS(xn[:, n], xn[:, n], 0.0, 1e-7, ALU.max, ALU.add)
            link(last)
            for n in range(NT):
                last = TS(g0_junk[:], xn[:, n], t_col[0:TN], None, ALU.mult)
                link(last)
                link(dve.tensor_reduce(peak[0:TN, n:n + 1], g0_junk[:], AX.X, ALU.max))
            dve.tensor_reduce(peak[0:TN, 5:6], peak[0:TN, 0:NT], AX.X, ALU.max).then_inc(S("g0_peak"), 1)
            await_group(dve, "g0_maxT", 0)
            dve.tensor_reduce(peak_all[0:1, 0:1], bank("g0_maxT", 0)[0:1, 0:TN], AX.X, ALU.max
                              ).then_inc(S("g0_max_read"), 1)
            await_group(dve, "g0_maxB", 0)
            TS(peak_all[0:TN, 1:2], bank("g0_maxB", 0)[0:TN, 0:1], -1.0, None, ALU.mult
               ).then_inc(S("g0_maxB_read"), 1)
            for n in range(NT):
                dve.wait_ge(*E("g0_exp_high", n + 1))
                TT(e_lo[:, n], e_full[n % 2][:], f(e_hi[:, n]), ALU.subtract).then_inc(S("g0_exp_low"), 1)
                TT(xn[:, n], xn[:, n], e_full[n % 2][:], ALU.mult).then_inc(S("g0_num_full"), 1)
                dve.wait_ge(*E("g0_num_high", n + 1))
                TT(nm_lo[:, n, 0:D], xn[:, n], f(nm_hi[:, n, 0:D]), ALU.subtract).then_inc(S("g0_num_low"), 1)
            one_hots("A", edge[:, 0])
            for j in range(2 * KD + 1):
                if j < 2 * KD:
                    (c0, cn), ft = CH[j % 2], j // 2
                    at, T, R = slice(c0, c0 + cn), tmp[:, j % 2, 0:cn], tmp[:, 2 + j % 2, 0:cn]
                    await_group(dve, "g0_den", j)
                    TS(R, bank("g0_den", j)[:, 0:cn], 1e-30, None, ALU.max).then_inc(S("g0_den_read"), 1)
                    dve.wait_ge(*E("g0_den_read", j + 1))
                    link(dve.reciprocal(R, R))
                    TT(T, bank("g0_num", j)[:, 0:cn], R, ALU.mult).then_inc(S("g0_num_read"), 1)
                    dve.wait_ge(*E("g0_num_read", j + 1))
                    link(TT(T, T, f(xT_hi[:, ft, at]), ALU.add))
                    TT(T, T, f(xT_lo[:, ft, at]), ALU.add).then_inc(S("g0_sum"), 1)
                if j >= 1:
                    i = j - 1
                    (c0, cn), ft = CH[i % 2], i // 2
                    dve.wait_ge(*E("g0_out_high", i + 1))
                    TT(xT_lo[:, ft, c0:c0 + cn], tmp[:, i % 2, 0:cn], f(xT_hi[:, ft, c0:c0 + cn]), ALU.subtract
                       ).then_inc(S("g0_out_low"), 1)
            hidden_low("g0", 12, False)
            add_to_nodes("g0", "g0d")
            expert_layer("f0", 12)

            for s in range(NT):
                at = slice(s * TN, (s + 1) * TN)
                TT(adj[:, s, at], f(adj[:, s, at]), ident[0:TN, 0:TN], ALU.add).then_inc(S("self_loops"), 1)
            for c, (c0, cn) in enumerate(CH):
                await_group(dve, "g1_deg", c)
                TS(dscale[:, c0:c0 + cn], bank("g1_deg", c)[:, 0:cn], 1.0, None, ALU.max
                   ).then_inc(S("g1_deg_copied"), 1)
                dve.wait_ge(*E("g1_deg_copied", c + 1))
                dve.reciprocal(dscale[:, c0:c0 + cn], dscale[:, c0:c0 + cn]).then_inc(S("g1_deg_read"), 1)
            layer_norm("g1", lambda n: xn[:, n])
            for n in range(NT):
                await_group(dve, "g1_dinv", n)
                dve.tensor_copy(dinv[0:TN, n:n + 1], bank("g1_dinv", n)[0:TN, 0:1]).then_inc(S("g1_dinv_read"), 1)
            dve.wait_ge(*E("g1_dinv_read", NT))
            for n in range(NT):
                TS(xn[:, n], xn[:, n], dinv[0:TN, n:n + 1], None, ALU.mult).then_inc(S("g1_scaled_nodes"), 1)
            nodes_low(D, xn, "g1_nodes_high", "g1_nodes_low")
            dve.wait_ge(*E("g1_bias_full", 16))
            add_bias("g1")
            dve.wait_ge(*E("g1_dscale", 1))
            scaled_messages("g1a", "g1a_agg", KD)
            dve.wait_ge(*E("g1b_bias_full", 16))
            for i in range(2 * NT + 1):
                if i < 2 * NT:
                    n, c = i % NT, i // NT
                    at = slice(c * 384, (c + 1) * 384)
                    await_group(dve, "g1a", i)
                    TT(xn[:, n, at], bank("g1a", i)[0:TN, 0:384], bias[:, at], ALU.add).then_inc(S("g1a_read"), 1)
                    dve.wait_ge(*E("g1a_read", i + 1))
                    TS(xn[:, n, at], xn[:, n, at], 0.0, dinv[0:TN, n:n + 1], ALU.max, ALU.mult
                       ).then_inc(S("g1a_full"), 1)
                if i >= 1:
                    n, c = (i - 1) % NT, (i - 1) // NT
                    at = slice(c * 384, (c + 1) * 384)
                    dve.wait_ge(*E("g1b_nodes_high", i))
                    TT(nm_lo[:, n, at], xn[:, n, at], f(nm_hi[:, n, at]), ALU.subtract).then_inc(S("g1b_nodes_low"), 1)
            scaled_messages("g1b", "g1b_agg", KD)
            add_to_nodes("g1", "g1b")
            expert_layer("f1", 8)

            for s in range(NT):
                at = slice(s * TN, (s + 1) * TN)
                TT(adj[:, s, at], f(adj[:, s, at]), ident[0:TN, 0:TN], ALU.subtract).then_inc(S("no_self_loops"), 1)
            layer_norm("g2", lambda n: xn[:, n])
            xT_low_half("g2_xT", KD)
            dve.wait_ge(*E("g2_bias_full", 16))
            add_bias("g2")
            dve.memset(maskT[:, :, NODES:NP], FAR)
            for i in range(NT * NT):
                d, s = i // NT, i % NT
                await_group(dve, "g2_maskT", i)
                TS(maskT[:, d, s * TN:(s + 1) * TN], bank("g2_maskT", i)[0:TN, 0:TN], 0.0, FAR,
                   ALU.is_equal, ALU.mult).then_inc(S("g2_masked"), 1)
            dve.wait_ge(*E("g2_masked", NT * NT))
            link(dve.tensor_reduce(no_edge[0:TN], maskT[:], AX.X, ALU.max))
            link(TS(no_edge[0:TN], no_edge[0:TN], -1.0, FAR, ALU.mult, ALU.add))
            dve.wait_ge(*E("g2p_att_full", 16))
            for i in range(4 * NT):
                n, c = i % NT, i // NT
                dve.wait_ge(*E("g2_h1", i + 1))
                for h in (2 * c, 2 * c + 1):
                    at = slice(h * HEAD_DIM, (h + 1) * HEAD_DIM)
                    for kind, dst in ((0, a_src), (1, a_dst)):
                        made = 4 * i + 2 * (h % 2) + kind
                        if made >= 4:
                            dve.wait_ge(*E("g2p_scores", made - 3))
                        dve.tensor_tensor_reduce(junk[:, kind * 256 + (h % 2) * 128:kind * 256 + (h % 2) * 128 + 128],
                                                 h1[:, n, at], att[:, kind, at], 1.0, 0.0,
                                                 ALU.mult, ALU.add, dst[0:TN, 8 * n + h:8 * n + h + 1]
                                                 ).then_inc(S("g2p_scores"), 1)
            dve.wait_ge(*E("g2p_scores", 8 * 2 * NT))
            dve.tensor_copy(head_sel[:], ident[0:8, 0:8].unsqueeze(2).to_broadcast([8, 8, P])).then_inc(S("head_sel"), 1)

            def attention(layer, heads):
                dve.memset(asT[:, NODES:NP], 0.0).then_inc(S(layer + "_pads"), 1)
                dve.memset(uT[:, NODES:NP], 0.0).then_inc(S(layer + "_pads"), 1)
                dve.memset(vT[:, NODES:NP], 0.0).then_inc(S(layer + "_pads"), 1)
                for n in range(NT):
                    await_group(dve, layer + "_asT", n)
                    dve.tensor_copy(asT[:, n * TN:(n + 1) * TN], bank(layer + "_asT", n)[0:8, 0:TN]
                                    ).then_inc(S(layer + "_asT_read"), 1)
                TS(a_src5[0:TN], a_src[0:TN], 0.2, None, ALU.mult)
                for h in range(heads):
                    dve.wait_ge(*E(layer + "_asB_read", 2 * h + 2))
                    dve.tensor_reduce(a_top[0:TN, h:h + 1], asB[:, h % 2, 0:NODES], AX.X, ALU.max)
                    for d in range(NT):
                        made = NT * h + d
                        if made >= 2:
                            dve.wait_ge(*E(layer + "_max_done", made - 1))
                        dve.tensor_tensor_reduce(edge_scores[:, made % 2], asB[:, h % 2], maskT[:, d], 1.0, -3e38,
                                                        ALU.add, ALU.max, a_max[0:TN, 8 * d + h:8 * d + h + 1]
                                                 ).then_inc(S(layer + "_max_done"), 1)
                dve.wait_ge(*E(layer + "_max_done", NT * heads))
                link(TT(v8(hot8), a_top[0:TN].unsqueeze(1).to_broadcast([TN, NT, 8]), bc(no_edge[0:TN]), ALU.add))
                link(TT(a_max[0:TN], a_max[0:TN], hot8[0:TN], ALU.max))
                link(TT(a_max[0:TN], a_max[0:TN], a_dst[0:TN], ALU.add))
                link(STT(hot8[0:TN], a_max[0:TN], 0.2, a_max[0:TN], ALU.mult, ALU.max))
                TT(uv[:, 0].rearrange("p n e -> p (n e)"), a_dst[0:TN], hot8[0:TN], ALU.subtract
                   ).then_inc(S(layer + "_uv"), 1)
                STT(uv[:, 1].rearrange("p n e -> p (n e)"), a_dst[0:TN], 0.2, hot8[0:TN], ALU.mult, ALU.subtract
                    ).then_inc(S(layer + "_uv"), 1)
                for i in range(2 * NT):
                    n, dst = i // 2, (uT, vT)[i % 2]
                    await_group(dve, layer + "_uvT", i)
                    dve.tensor_copy(dst[:, n * TN:(n + 1) * TN], bank(layer + "_uvT", i)[0:8, 0:TN]
                                    ).then_inc(S(layer + "_uvT_read"), 1)

                def head_out(h):
                    for c, (c0, cn) in enumerate(CH):
                        j = 2 * h + c
                        T, R = tmp[:, j % 2, 0:cn], tmp[:, 2 + j % 2, 0:cn]
                        await_group(dve, "g2p_den", j)
                        TS(R, bank("g2p_den", j)[:, 0:cn], 1e-16, None, ALU.add).then_inc(S("g2p_den_read"), 1)
                        dve.wait_ge(*E("g2p_den_read", j + 1))
                        link(dve.reciprocal(R, R))
                        await_group(dve, "g2p_agg", j)
                        TT(T, bank("g2p_agg", j)[:, 0:cn], R, ALU.mult).then_inc(S("g2p_agg_read"), 1)
                        dve.wait_ge(*E("g2p_agg_read", j + 1))
                    for c, (c0, cn) in enumerate(CH):
                        j = 2 * h + c
                        dve.wait_ge(*E("g2p_high", j + 1))
                        TT(hT_lo[:, h, c0:c0 + cn], tmp[:, j % 2, 0:cn], f(hT_hi[:, h, c0:c0 + cn]), ALU.subtract
                           ).then_inc(S("g2p_low"), 1)

                for h in range(heads):
                    pr = prob[h % 2]
                    for s in range(NT):
                        dve.wait_ge(*E(layer + "_shift", NT * h + s + 1))
                        STT(pr[:, s], uB[h % 2][:, 1], a_src5[0:TN, 8 * s + h:8 * s + h + 1], pr[:, s],
                            ALU.add, ALU.max).then_inc(S(layer + "_leaky"), 1)
                    dve.wait_ge(*E(layer + "_powers", h + 1))
                    STT(pr[:].rearrange("p n j -> p (n j)"), pr[:].rearrange("p n j -> p (n j)"), 3.0,
                        f(adj[:]).rearrange("p n j -> p (n j)"), ALU.min, ALU.mult).then_inc(S(layer + "_prob"), 1)
                    if layer == "g2p" and h:
                        head_out(h - 1)
                if layer == "g2p":
                    head_out(heads - 1)

            attention("g2p", HEADS)
            dve.wait_ge(*E("g2q_att_full", 16))
            dve.memset(a_src[0:TN], 0.0)
            link(dve.memset(a_dst[0:TN], 0.0))
            for i in range(2 * NT):
                n, c = i % NT, i // NT
                at = slice(c * 384, (c + 1) * 384)
                dve.wait_ge(*E("g2_h2", i + 1))
                for kind in range(2):
                    if i:
                        dve.wait_ge(*E("h2_scores", 2 * i + kind - 1))
                    dve.tensor_tensor_reduce(junk[:, kind * 384:kind * 384 + 384], h2[:, n, at],
                                                    att[:, kind, at], 1.0, 0.0, ALU.mult, ALU.add,
                                                    a_part[0:TN, (c * 2 + kind) * NT + n:(c * 2 + kind) * NT + n + 1]
                                             ).then_inc(S("h2_scores"), 1)
            dve.wait_ge(*E("h2_scores", 4 * NT))
            dve.memset(h2[:, :, D:D + 2], 1.0).then_inc(S("h2_ones"), 1)
            for kind, dst in ((0, a_src), (1, a_dst)):
                last = TT(v8(dst)[:, :, 0], a_part[0:TN, kind * NT:(kind + 1) * NT],
                          a_part[0:TN, (2 + kind) * NT:(3 + kind) * NT], ALU.add)
                last.then_inc(S("g2q_scores"), 1)
            dve.wait_ge(*E("g2q_scores", 2))
            attention("g2q", 1)
            for n in range(NT):
                for i, at, cn in ((2 * n, slice(384, D), 384), (2 * n + 1, slice(0, 384), 384)):
                    await_group(dve, "g2q_agg", i)
                    if i % 2 == 0:
                        link(TS(sum8[0:TN, n:n + 1], bank("g2q_agg", i)[0:TN, 384:385], 1e-16, None, ALU.add))
                        link(dve.reciprocal(sum8[0:TN, n:n + 1], sum8[0:TN, n:n + 1]))
                    STT(x[:, n, at], bank("g2q_agg", i)[0:TN, 0:cn], sum8[0:TN, n:n + 1], x[:, n, at],
                        ALU.mult, ALU.add).then_inc(S("g2_x"), 1)
            dve.wait_ge(*E("g2_x", 2 * NT))

            def kp(t):
                return t.rearrange("d (k p) -> d k p", k=KD)

            slots = col("slots").rearrange("d (k n p) -> d k n p", k=KD, n=EXPERTS)
            link(TT(sp_tmp[:], col("slots").rearrange("d (k s) -> d k s", k=KD),
                    col("slots").rearrange("d (k s) -> d k s", k=KD), ALU.mult))
            dve.tensor_reduce(kp(slot_sum[:]), sp_tmp[:].rearrange("d k (n p) -> d k p n", n=EXPERTS), AX.X, ALU.add
                              ).then_inc(S("slots_squared"), 1)
            dve.wait_ge(*E("slots_norm", 1))
            link(TS(slot_sum[:], slot_sum[:], 1e-6, None, ALU.add))
            link(dve.reciprocal(slot_sum[:], slot_sum[:]))
            for n in range(EXPERTS):
                last = TT(sp_tmp[:].rearrange("d k (n p) -> d k n p", n=EXPERTS)[:, :, n], slots[:, :, n],
                          kp(slot_sum[:]), ALU.mult)
            link(last)
            link(TS(sp_tmp[:], sp_tmp[:], slot_scale, None, ALU.mult))
            link(dve.tensor_copy(sp_hi[:], sp_tmp[:]))
            TT(sp_lo[:], sp_tmp[:], f(sp_hi[:]), ALU.subtract).then_inc(S("slots_split"), 1)
            layer_norm("f2", lambda n: xn[:, n])
            for n in range(NT):
                if n:
                    dve.wait_ge(*E("f2_squared", n))
                dve.tensor_tensor_reduce(f2_junk[:], xn[:, n], xn[:, n], 1.0, 0.0, ALU.mult, ALU.add,
                                         sum8[0:TN, n:n + 1]).then_inc(S("f2_squared"), 1)
            dve.wait_ge(*E("f2_norm", 1))
            link(TS(sum8[0:TN], sum8[0:TN], 1e-6, None, ALU.add))
            link(dve.reciprocal(sum8[0:TN], sum8[0:TN]))
            for n in range(NT):
                TS(xn[:, n], xn[:, n], sum8[0:TN, n:n + 1], None, ALU.mult).then_inc(S("f2_unit"), 1)
            for i in range(2 * NT):
                n, (a, b) = i // 2, ((0, 4), (4, KD))[i % 2]
                at = slice(n * TN, (n + 1) * TN)
                dve.wait_ge(*E("f2_xT_high", i + 1))
                TT(xT_lo[:, a:b, at], bank("f2_xT", i)[:, 0:(b - a) * TN].rearrange("p (k n) -> p k n", n=TN),
                   f(xT_hi[:, a:b, at]), ALU.subtract).then_inc(S("f2_xT_low"), 1)
            for n in range(NT):
                await_group(dve, "f2_logits", n)
                dve.tensor_copy(slot_logits[:, n], bank("f2_logits", n)[0:TN, 0:SLOTS]).then_inc(S("f2_logits_read"), 1)
            dve.wait_ge(*E("f2_logits_read", NT))
            link(dve.tensor_reduce(col_peak[:], slot_logits[:], AX.X, ALU.max))
            TT(combine[:], slot_logits[:], col_peak[:].unsqueeze(2).to_broadcast([TN, NT, SLOTS]), ALU.subtract
               ).then_inc(S("f2_rows_shifted"), 1)
            for n in range(NT):
                await_group(dve, "f2_logitsT", n)
                dve.tensor_copy(logitsT[:, n * TN:(n + 1) * TN], bank("f2_logitsT", n)[0:SLOTS, 0:TN]
                                ).then_inc(S("f2_logitsT_read"), 1)
            dve.wait_ge(*E("f2_logitsT_read", NT))
            dve.tensor_reduce(row_peak[:], logitsT[:, 0:NODES], AX.X, ALU.max, negate=True
                              ).then_inc(S("f2_column_peak"), 1)
            dve.wait_ge(*E("f2_row_exp", 1))
            link(dve.tensor_reduce(col_sum[:], combine[:], AX.X, ALU.add))
            link(dve.reciprocal(col_sum[:], col_sum[:]))
            TT(combine[:], combine[:], col_sum[:].unsqueeze(2).to_broadcast([TN, NT, SLOTS]), ALU.mult
               ).then_inc(S("f2_combine"), 1)
            dve.wait_ge(*E("f2_column_exp", 1))
            link(dve.reciprocal(row_sum[:], row_sum[:]))
            TS(logitsT[:, 0:NODES], logitsT[:, 0:NODES], row_sum[:], None, ALU.mult).then_inc(S("f2_dispatchT"), 1)
            for n in range(NT):
                await_group(dve, "f2_dispatch", n)
                dve.tensor_copy(dispatch[:, n], bank("f2_dispatch", n)[0:TN, 0:SLOTS]).then_inc(S("f2_dispatch_read"), 1)
            for n in range(NT):
                await_group(dve, "f2_combineT", n)
                dve.tensor_copy(combineT[:, n * TN:(n + 1) * TN], bank("f2_combineT", n)[0:SLOTS, 0:TN]
                                ).then_inc(S("f2_combineT_read"), 1)
            for k in range(KD):
                await_group(dve, "f2_tilde", k)
                dve.tensor_copy(tildeT[:, k], bank("f2_tilde", k)[:, 0:SLOTS]).then_inc(S("f2_tilde_read"), 1)
            dve.memset(hidden_diag[:], 0.0).then_inc(S("f2_diag_clear"), 1)
            await_group(dve, "f2_hidden", 0)
            TT(slot_hidden[:], bank("f2_hidden", 0)[0:SLOT_H, 0:SLOTS].rearrange("p (e s) -> p e s", s=4),
               col("b_down")[0:SLOT_H].unsqueeze(2).to_broadcast([SLOT_H, 8, 4]), ALU.add
               ).then_inc(S("f2_hidden_read"), 1)
            for c in range(2):
                await_group(dve, "f2_up", c)
                dve.tensor_copy(slot_out[:, c * 384:(c + 1) * 384], bank("f2_up", c)[0:SLOTS, 0:384]
                                ).then_inc(S("f2_up_read"), 1)
            add_to_nodes("f2", "f2_down")

            layer_norm("g3", lambda n: acc[:, n, 0:D])
            dve.wait_ge(*E("types_loaded", 16))
            TS(type_hot[:], node_type_i[:], rel_index[0:RELS], None, ALU.is_equal).then_inc(S("type_hot"), 1)
            for n in range(NT):
                await_group(dve, "g3_emb", n)
                dve.tensor_copy(acc[:, n, D:D1], bank("g3_emb", n)[0:TN, 0:TYPE_DIM]).then_inc(S("g3_emb_low"), 1)
            rel_source = edge[:, 2]
            link(dve.tensor_copy(types[:], edge[:, 2]))
            for r in range(RELS):
                if r:
                    await_group(dve, f"R{r - 1}", 2 * NT - 1)
                TS(rel_source, types[:], float(r), None, ALU.is_equal).then_inc(S("rel_source"), 1)
                dve.wait_ge(*E("rel_source", 3 * r + 1))
                TS(src_plus[:], edge[:, 0], 1.0, None, ALU.add).then_inc(S("rel_source"), 1)
                dve.wait_ge(*E("rel_source", 3 * r + 2))
                link(TT(rel_source, rel_source, src_plus[:], ALU.mult))
                TS(rel_source, rel_source, -1.0, None, ALU.add).then_inc(S("rel_source"), 1)
                dve.wait_ge(*E("rel_source", 3 * r + 3))
                one_hots(f"R{r}", rel_source)
            nodes_low(D1, acc, "g3a_nodes_high", "g3a_nodes_low")
            for key, k, width in (("g3a", K1, 448), ("g3b", K1, 384), ("g3c", KD, 384)):
                clear_pad(key + "_hT_pad")
                for i in range(2 * NT):
                    n, (a, b) = i // 2, ((0, 4), (4, k))[i % 2]
                    at = slice(n * TN, (n + 1) * TN)
                    dve.wait_ge(*E(key + "_hT_high", i + 1))
                    TT(xT_lo[:, a:b, at], bank(key + "_hT", i)[:, 0:(b - a) * TN].rearrange("p (k n) -> p k n", n=TN),
                       f(xT_hi[:, a:b, at]), ALU.subtract).then_inc(S(key + "_hT_low"), 1)
                dve.wait_ge(*E(key + "_bias_full", 16))
                for i in range(2 * NT):
                    n, c = i % NT, i // NT
                    at = slice(c * width, (c + 1) * width)
                    await_group(dve, key + "_root", i)
                    TT(acc[:, n, at], bank(key + "_root", i)[0:TN, 0:width], bias[:, at], ALU.add
                       ).then_inc(S(key + "_acc"), 1)
                for r in range(RELS):
                    for c, (c0, cn) in enumerate(CH):
                        await_group(dve, f"{key}_deg{r}", c)
                        TS(dscale[:, c0:c0 + cn], bank(f"{key}_deg{r}", c)[:, 0:cn], 1.0, None, ALU.max
                           ).then_inc(S(key + "_deg_read"), 1)
                    dve.wait_ge(*E(key + "_deg_read", 2 * r + 2))
                    link(dve.reciprocal(dscale[:], dscale[:]))
                    scaled_messages(key, f"{key}_agg{r}", k, 2 * k * r)
                    dve.wait_ge(*E(key + "_acc", 2 * NT * (r + 1)))
                    for i in range(2 * NT):
                        n, c = i % NT, i // NT
                        at = slice(c * width, (c + 1) * width)
                        await_group(dve, f"{key}_rel{r}", i)
                        TT(acc[:, n, at], bank(f"{key}_rel{r}", i)[0:TN, 0:width], acc[:, n, at], ALU.add
                           ).then_inc(S(key + "_acc"), 1)
                dve.wait_ge(*E(key + "_acc", 2 * NT * (RELS + 1)))
                if key != "g3c":
                    out_key, out_k = ("g3b", K1) if key == "g3a" else ("g3c", KD)
                    for n in range(NT):
                        TS(acc[:, n, 0:2 * width], acc[:, n, 0:2 * width], 0.0, None, ALU.max
                           ).then_inc(S(out_key + "_nodes"), 1)
                    nodes_low(2 * width, acc, out_key + "_nodes_high", out_key + "_nodes_low")
                else:
                    for n in range(NT):
                        STT(x[:, n], acc[:, n, 0:D], 0.0, x[:, n], ALU.max, ALU.add).then_inc(S("g3_x"), 1)
                    dve.wait_ge(*E("g3_x", NT))
            dve.memset(bias8[:], 0.0).then_inc(S("f3_rows_clear"), 1)
            expert_layer("f3", 12)

        @block.tensor
        def _(pe):
            def open_bank(label, i):
                g = WHERE[label, i]
                if g >= 8:
                    pe.wait_ge(*E(*GROUPS[g - 8]))
                return banks[g % 8]

            closed = [0]

            def close(ins, label, i):
                assert WHERE[label, i] == closed[0], (label, i)
                closed[0] += 1
                ins.then_inc(S("group_closed"), 1)

            def three(dst, l_hi, l_lo, r_hi, r_lo, start, stop):
                pe.matmul(dst, l_hi, r_hi, start=start, stop=False)
                pe.matmul(dst, l_hi, r_lo, start=False, stop=False)
                return pe.matmul(dst, l_lo, r_hi, start=False, stop=stop)

            def transposes(label, src, k, ready):
                for i in range(2 * NT):
                    n, (a, b) = i // 2, ((0, 4), (4, k))[i % 2]
                    if i % 2 == 0:
                        pe.wait_ge(*E(ready, n + 1))
                    dst = open_bank(label, i)
                    for j in range(a, b):
                        last = pe.transpose(dst[:, (j - a) * TN:(j - a + 1) * TN], src[:, n, j * P:(j + 1) * P],
                                            ident[0:TN, 0:TN])
                    close(last, label, i)

            def up(s, j):
                m, (c0, cn) = j // 2, CH[j % 2]
                u = FIRST_UNIT["u", s] + m
                if j % 2 == 0:
                    pe.wait_ge(*E("unit_split", u + 1))
                dst = open_bank(s + "_hidden", j)
                for k in range(KD):
                    w = slice(k * P, (k + 1) * P)
                    last = three(dst[:, 0:cn], w_hi[:, u % RING, w], w_lo[:, u % RING, w], xT_hi[:, k, c0:c0 + cn],
                                 xT_lo[:, k, c0:c0 + cn], k == 0, k == KD - 1)
                close(last, s + "_hidden", j)
                if j % 2:
                    pe.drain().then_inc(S("unit_used"), 1)

            def down(key, label, lhs_hi, lhs_lo, ready, feed=0, seed=None):
                kt, cw, chunks, per = DOWN[key]
                for c in range(chunks):
                    for k in range(kt):
                        u, pos = divmod(feed * kt * chunks + c * kt + k, per)
                        u += FIRST_UNIT["d", key]
                        w = slice(pos * cw, (pos + 1) * cw)
                        if pos == 0:
                            pe.wait_ge(*E("unit_split", u + 1))
                        if c == 0:
                            ready(k)
                        for n in range(NT):
                            i = c * NT + n
                            at = slice(n * TN, (n + 1) * TN)
                            if k == 0:
                                open_bank(label, i)
                                if seed:
                                    seed(bank(label, i), c, at)
                            last = three(bank(label, i)[0:TN, 0:cw], lhs_hi[:, k, at], lhs_lo[:, k, at],
                                         w_hi[:, u % RING, w], w_lo[:, u % RING, w], k == 0 and not seed, k == kt - 1)
                            if k == kt - 1:
                                close(last, label, i)
                        if pos == per - 1:
                            if k == kt - 1:
                                last = pe.drain()
                            last.then_inc(S("unit_used"), 1)

            def gather(label, k, counts_of, first=0):
                for j in range(2 * k):
                    ft, (c0, cn) = j // 2, CH[j % 2]
                    dst = open_bank(label, j)
                    for s in range(NT):
                        for half in (nm_hi, nm_lo):
                            last = pe.matmul(dst[:, 0:cn], half[:, s, ft * P:(ft + 1) * P], counts_of(s, c0, cn),
                                             start=(s == 0 and half is nm_hi), stop=(s == NT - 1 and half is nm_lo))
                    close(last, label, j)

            def of_adj(s, c0, cn):
                return adj[:, s, c0:c0 + cn]

            def of_rel(r):
                return lambda s, c0, cn: rel[:, r, s, c0:c0 + cn]

            def count_edges(label):
                for c, (c0, cn) in enumerate(CH):
                    def step(t, k, first=False, last_tile=False):
                        pe.wait_ge(*E(label + "_hot", t * 2 + 2 + c * 2 * ET))
                        for s in range(NT):
                            ins = pe.matmul(bank(label, c * NT + s)[0:TN, 0:cn], src_hot[:, k, s * TN:(s + 1) * TN],
                                            dst_hot[:, k, 0:cn], start=first, stop=last_tile)
                            if last_tile:
                                close(ins, label, c * NT + s)
                        if not last_tile:
                            ins.then_inc(S(label + "_hot_used"), 1)
                    for s in range(NT):
                        open_bank(label, c * NT + s)
                    for t in range(OSLOTS):
                        step(t, t, first=t == 0)
                    with pe.Fori(1, ET // OSLOTS - 1) as q:
                        for k in range(OSLOTS):
                            step(q * OSLOTS + k, k)
                    for k in range(OSLOTS):
                        step(ET - OSLOTS + k, k, last_tile=k == OSLOTS - 1)

            def sum_over_sources(label, counts_of):
                for c, (c0, cn) in enumerate(CH):
                    dst = open_bank(label, c)
                    for s in range(NT):
                        last = pe.matmul(dst[:, 0:cn], ones_r[0:TN, :], counts_of(s, c0, cn), start=s == 0, stop=s == NT - 1)
                    close(last, label, c)

            def expert_layer(s, tiles, gate):
                transposes(s + "_xT", xn, KD, s + "_xn")
                pe.wait_ge(*E(s + "_xT_pad", 2))
                for n in range(NT):
                    pe.wait_ge(*E(s + "_xT_low", 2 * n + 2))
                    dst = open_bank(s + "_router", n)
                    for k in range(KD):
                        g = slice(48 * gate + 8 * k, 48 * gate + 8 * k + 8)
                        at = slice(n * TN, (n + 1) * TN)
                        last = three(dst[0:TN, 0:8], xT_hi[:, k, at], xT_lo[:, k, at], gate_hi[:, g], gate_lo[:, g],
                                     k == 0, k == KD - 1)
                    close(last, s + "_router", n)
                jobs = 2 * tiles
                for j in range(jobs + EXPERT_LAG):
                    if j < jobs:
                        up(s, j)
                    if j == EXPERT_LAG - 1:
                        if s == "f1":
                            pe.wait_ge(*E("f1_probs", 1))
                            dst = open_bank("f1_importance", 0)
                            for n in range(NT):
                                last = pe.matmul(dst[0:TN, 0:8], ones[0:TN, 0:TN], prob8[0:TN, 8 * n:8 * n + 8],
                                                 start=n == 0, stop=n == NT - 1)
                            close(last, "f1_importance", 0)
                        pe.wait_ge(*E(s + "_combine", 1))
                        for n in range(NT):
                            dst = open_bank(s + "_cT", n)
                            close(pe.transpose(dst[:, 0:TN], cpad[:, n], ident[0:TN, 0:TN]), s + "_cT", n)
                        pe.wait_ge(*E(s + "_cT_pad", 1))
                        pe.wait_ge(*E(s + "_combineT", NT))
                    if j >= EXPERT_LAG:
                        i = j - EXPERT_LAG
                        m, (c0, cn) = i // 2, CH[i % 2]
                        q, kind = (m // 3, m % 3) if tiles == 12 else (m // 2, 2 * (m % 2))
                        rows = slice(32 * q, 32 * q + 2)
                        dst = open_bank(s + "_cB", i)
                        close(pe.matmul(dst[:, 0:cn], pat[rows, kind], cT[rows, c0:c0 + cn], start=True, stop=True),
                              s + "_cB", i)
                if s == "f1":
                    seed = None
                else:
                    pe.wait_ge(*E(s + "_bias_full", 64))

                    def seed(dst, c, at):
                        pe.matmul(dst[0:TN, 0:384], cT[:, at], bias8[:, c * 384:(c + 1) * 384], start=True, stop=False)
                down(s + "d", s + "_down", hT_hi, hT_lo, lambda k: pe.wait_ge(*E(s + "_low", 2 * k + 2)), seed=seed)

            pe.wait_ge(*E("consts", 21))
            transposes("g0_xT", xn, KD, "g0_xn")
            pe.wait_ge(*E("g0_peak", 1))
            dst = open_bank("g0_maxT", 0)
            close(pe.matmul(dst[0:1, 0:TN], peak[0:TN, 5:6], ident[0:TN, 0:TN], start=True, stop=True), "g0_maxT", 0)
            pe.wait_ge(*E("g0_max_read", 1))
            dst = open_bank("g0_maxB", 0)
            close(pe.matmul(dst[0:TN, 0:1], ones[0:1, 0:TN], peak_all[0:1, 0:1], start=True, stop=True), "g0_maxB", 0)
            count_edges("A")
            pe.wait_ge(*E("A_counted", 2 * NT))
            pe.wait_ge(*E("g0_exp_low", NT))
            pe.wait_ge(*E("g0_num_low", NT))
            for j in range(2 * KD):
                ft, (c0, cn) = j // 2, CH[j % 2]
                for label, halves in (("g0_num", (nm_hi, nm_lo)), ("g0_den", (e_hi, e_lo))):
                    dst = open_bank(label, j)
                    for s in range(NT):
                        for half in halves:
                            last = pe.matmul(dst[:, 0:cn], half[:, s, ft * P:(ft + 1) * P], of_adj(s, c0, cn),
                                             start=(s == 0 and half is halves[0]), stop=(s == NT - 1 and half is halves[1]))
                    close(last, label, j)
            pe.wait_ge(*E("g0_xT_pad", 2))
            pe.wait_ge(*E("g0_out_low", 2 * KD))
            pe.wait_ge(*E("bn_ready", 1))
            for j in range(24):
                up("g0", j)
            down("g0d", "g0d", hT_hi, hT_lo, lambda k: pe.wait_ge(*E("g0_low", 2 * k + 2)))
            pe.wait_ge(*E("gates_split", 1))
            expert_layer("f0", 12, 0)
            pe.wait_ge(*E("self_loops", NT))
            sum_over_sources("g1_deg", of_adj)
            pe.wait_ge(*E("g1_dscale", 1))
            for n in range(NT):
                dst = open_bank("g1_dinv", n)
                close(pe.matmul(dst[0:TN, 0:1], dscale[0:1, n * TN:(n + 1) * TN], ones[0:1, 0:1], start=True, stop=True),
                      "g1_dinv", n)
            pe.wait_ge(*E("g1_nodes_low", NT))
            gather("g1a_agg", KD, of_adj)
            down("g1a", "g1a", xT_hi, xT_lo, lambda k: pe.wait_ge(*E("g1a_low", 2 * k + 2)))
            pe.wait_ge(*E("g1b_nodes_low", 2 * NT))
            gather("g1b_agg", KD, of_adj)
            down("g1b", "g1b", xT_hi, xT_lo, lambda k: pe.wait_ge(*E("g1b_low", 2 * k + 2)))
            expert_layer("f1", 8, 1)
            transposes("g2_xT", xn, KD, "g2_xn")
            pe.wait_ge(*E("no_self_loops", NT))
            for i in range(NT * NT):
                d, s = i // NT, i % NT
                dst = open_bank("g2_maskT", i)
                close(pe.transpose(dst[0:TN, 0:TN], f(adj[:, s, d * TN:(d + 1) * TN]), ident[0:TN, 0:TN]),
                      "g2_maskT", i)
            pe.wait_ge(*E("g2_xT_low", 2 * NT))
            down("g2a", "g2a", xT_hi, xT_lo, lambda k: None)

            def attention(layer, heads, product):
                pe.wait_ge(*E("g2p_scores" if heads > 1 else "g2q_scores", 8 * 2 * NT if heads > 1 else 2))
                pe.wait_ge(*E("head_sel", 1))
                for n in range(NT):
                    dst = open_bank(layer + "_asT", n)
                    close(pe.transpose(dst[0:8, 0:TN], a_src[0:TN, 8 * n:8 * n + 8], ident[0:TN, 0:TN]),
                          layer + "_asT", n)
                pe.wait_ge(*E(layer + "_pads", 3))
                pe.wait_ge(*E(layer + "_asT_read", NT))
                for h in range(heads):
                    for c, (c0, cn) in enumerate(CH):
                        dst = open_bank(layer + "_asB", 2 * h + c)
                        close(pe.matmul(dst[0:TN, 0:cn], head_sel[:, h, 0:TN], asT[:, c0:c0 + cn], start=True, stop=True),
                              layer + "_asB", 2 * h + c)
                pe.wait_ge(*E(layer + "_uv", 2))
                for i in range(2 * NT):
                    dst = open_bank(layer + "_uvT", i)
                    close(pe.transpose(dst[0:8, 0:TN], uv[:, i % 2, i // 2], ident[0:TN, 0:TN]), layer + "_uvT", i)
                pe.wait_ge(*E(layer + "_uvT_read", 2 * NT))
                for h in range(heads):
                    for i in range(4):
                        c0, cn = CH[i % 2]
                        dst = open_bank(layer + "_uvB", 4 * h + i)
                        close(pe.matmul(dst[0:TN, 0:cn], head_sel[:, h, 0:TN], (uT, vT)[i // 2][:, c0:c0 + cn],
                                        start=True, stop=True), layer + "_uvB", 4 * h + i)
                    if h:
                        product(h - 1)
                product(heads - 1)

            def head_product(h):
                pe.wait_ge(*E("g2p_prob", h + 1))
                for c, (c0, cn) in enumerate(CH):
                    for label in ("g2p_den", "g2p_agg"):
                        dst = open_bank(label, 2 * h + c)
                        for s in range(NT):
                            lhs = ones[0:TN, :] if label == "g2p_den" else h1[:, s, h * HEAD_DIM:(h + 1) * HEAD_DIM]
                            last = pe.matmul(dst[:, 0:cn], lhs, prob[h % 2][:, s, c0:c0 + cn], start=s == 0, stop=s == NT - 1)
                        close(last, label, 2 * h + c)

            def last_product(_):
                pe.wait_ge(*E("g2q_prob", 1))
                for n in range(NT):
                    for i, at in ((2 * n, slice(384, D + 1)), (2 * n + 1, slice(0, 384))):
                        dst = open_bank("g2q_agg", i)
                        for s in range(NT):
                            last = pe.matmul(dst[0:TN, 0:at.stop - at.start], prob[0][:, s, n * TN:(n + 1) * TN],
                                             h2[:, s, at], start=s == 0, stop=s == NT - 1)
                        close(last, "g2q_agg", i)

            attention("g2p", HEADS, head_product)
            down("g2b", "g2b", hT_hi, hT_lo, lambda k: pe.wait_ge(*E("g2p_low", 2 * k + 2)))
            attention("g2q", 1, last_product)
            transposes("f2_xT", xn, KD, "f2_unit")
            pe.wait_ge(*E("slots_split", 1))
            for n in range(NT):
                pe.wait_ge(*E("f2_xT_low", 2 * n + 2))
                dst = open_bank("f2_logits", n)
                at = slice(n * TN, (n + 1) * TN)
                for k in range(KD):
                    last = three(dst[0:TN, 0:SLOTS], xT_hi[:, k, at], xT_lo[:, k, at], sp_hi[:, k], sp_lo[:, k],
                                 k == 0, k == KD - 1)
                close(last, "f2_logits", n)
            for n in range(NT):
                pe.wait_ge(*E("f2_logits_read", n + 1))
                dst = open_bank("f2_logitsT", n)
                close(pe.transpose(dst[0:SLOTS, 0:TN], slot_logits[:, n], ident[0:TN, 0:TN]), "f2_logitsT", n)
            pe.wait_ge(*E("f2_dispatchT", 1))
            for n in range(NT):
                dst = open_bank("f2_dispatch", n)
                close(pe.transpose(dst[0:TN, 0:SLOTS], logitsT[:, n * TN:(n + 1) * TN], ident[0:SLOTS, 0:SLOTS]),
                      "f2_dispatch", n)
            pe.wait_ge(*E("f2_combine", 1))
            for n in range(NT):
                dst = open_bank("f2_combineT", n)
                close(pe.transpose(dst[0:SLOTS, 0:TN], combine[:, n], ident[0:TN, 0:TN]), "f2_combineT", n)
            pe.wait_ge(*E("f2_dispatch_read", NT))
            for k in range(KD):
                dst = open_bank("f2_tilde", k)
                for n in range(NT):
                    last = pe.matmul(dst[:, 0:SLOTS], xn[:, n, k * P:(k + 1) * P], dispatch[:, n], start=n == 0, stop=n == NT - 1)
                close(last, "f2_tilde", k)
            pe.wait_ge(*E("slot_weights", 16 * (EXPERTS + 1)))
            pe.wait_ge(*E("f2_tilde_read", KD))
            dst = open_bank("f2_hidden", 0)
            for e in range(EXPERTS):
                for k in range(KD):
                    last = pe.matmul(dst[0:SLOT_H, 4 * e:4 * e + 4], w_down[:, e, k], tildeT[:, k, 4 * e:4 * e + 4],
                                     start=k == 0, stop=k == KD - 1)
            close(last, "f2_hidden", 0)
            pe.wait_ge(*E("f2_bias_full", 16))
            pe.wait_ge(*E("f2_diag", 1))
            for c in range(2):
                at = slice(c * 384, (c + 1) * 384)
                dst = open_bank("f2_up", c)
                pe.matmul(dst[0:SLOTS, 0:384], sel8[0:8, :], bias8[0:8, at], start=True, stop=False)
                for e in range(EXPERTS):
                    last = pe.matmul(dst[0:SLOTS, 0:384], hidden_diag[:, 32 * e:32 * e + 32], w_up[:, e, at],
                                     start=False, stop=e == EXPERTS - 1)
                close(last, "f2_up", c)
            pe.wait_ge(*E("f2_up_read", 2))
            pe.wait_ge(*E("f2_combineT_read", NT))
            for c in range(2):
                for n in range(NT):
                    dst = open_bank("f2_down", c * NT + n)
                    close(pe.matmul(dst[0:TN, 0:384], combineT[:, n * TN:(n + 1) * TN],
                                    slot_out[:, c * 384:(c + 1) * 384], start=True, stop=True), "f2_down", c * NT + n)
            pe.wait_ge(*E("type_hot", 1))
            pe.wait_ge(*E("emb_loaded", 16))
            for n in range(NT):
                dst = open_bank("g3_emb", n)
                close(pe.matmul(dst[0:TN, 0:TYPE_DIM], type_hot[:, n * TN:(n + 1) * TN], emb[:], start=True, stop=True),
                      "g3_emb", n)
            for r in range(RELS):
                count_edges(f"R{r}")
                pe.wait_ge(*E(f"R{r}_counted", 2 * NT))
            for key, k, ready in (("g3a", K1, "g3_emb_low"), ("g3b", K1, "g3b_nodes"), ("g3c", KD, "g3c_nodes")):
                transposes(key + "_hT", acc, k, ready)
                pe.wait_ge(*E(key + "_hT_pad", 2))
                pe.wait_ge(*E(key + "_hT_low", 2 * NT))
                down(key, key + "_root", xT_hi, xT_lo, lambda k: None)
                pe.wait_ge(*E(key + "_nodes_low", NT))
                for r in range(RELS):
                    sum_over_sources(f"{key}_deg{r}", of_rel(r))
                    gather(f"{key}_agg{r}", k, of_rel(r))
                    first = 2 * k * r
                    down(key, f"{key}_rel{r}", xT_hi, xT_lo,
                         lambda t: pe.wait_ge(*E(key + "_low", first + 2 * t + 2)), feed=r + 1)
            expert_layer("f3", 12, 2)
            assert closed[0] == len(GROUPS)


NAMES = ["x_in", "edges_in", "wa", "wb", "wc", "cols_in", "bias_in", "rows_in", "att_in", "scalars_in",
         "w_down_in", "w_up_in", "emb_in", "types_in"]


def up_units(w):
    m = w.shape[1] // P
    return w.reshape(KD, P, m, P).transpose(2, 1, 0, 3).reshape(m, P, UNIT)


def down_slices(w, key):
    k, cw, chunks, per = DOWN[key]
    ws = w if isinstance(w, list) else [w]
    s = np.concatenate([v.reshape(k, P, chunks, cw).transpose(2, 0, 1, 3).reshape(chunks * k, P, cw) for v in ws])
    return s.reshape(-1, per, P, cw).transpose(0, 2, 1, 3).reshape(-1, P, per * cw)


def laid_out(i):
    i = {k: np.asarray(v) for k, v in i.items()}

    def per_expert_in(w):
        return w.transpose(1, 0, 2).reshape(w.shape[1], -1)

    def tiles(v):
        return v.reshape(-1, P).T

    feeds = {"g3a": "1", "g3b": "2", "g3c": "3"}
    down = {
        "g0d": i["L0_gnn_W2"], "f0d": i["L0_ffn_w2"].reshape(-1, D), "g1a": i["L1_gnn_W1"], "g1b": i["L1_gnn_W2"],
        "f1d": i["L1_ffn_w2"].transpose(0, 2, 1).reshape(-1, D), "g2a": i["L2_gnn_W1"].T, "g2b": i["L2_gnn_W2"].T,
        "f3d": i["L3_ffn_w2"].reshape(-1, D),
    }
    for key, n in feeds.items():
        down[key] = [i["L3_gnn_w_root" + n]] + list(i["L3_gnn_w_rel" + n])
    up = {
        "g0": i["L0_gnn_W1"], "f0": per_expert_in(i["L0_ffn_w1"]),
        "f1": i["L1_ffn_w1"].transpose(2, 0, 1).reshape(D, -1), "f3": per_expert_in(i["L3_ffn_w1"]),
    }

    def stream(seq):
        return np.concatenate([up_units(up[key]) if kind == "u" else down_slices(down[key], key) for kind, key in seq])

    def gate(w):
        return w.T.reshape(KD, P, EXPERTS).transpose(1, 0, 2).reshape(P, -1)

    b_down = np.concatenate([i["L2_ffn_b_down"].T, np.zeros((P - SLOT_H, EXPERTS), np.float32)])
    cols = np.concatenate(
        [tiles(i["L0_gnn_b1"]), tiles(i["L0_gnn_bn_gamma"]), tiles(i["L0_gnn_bn_beta"]), tiles(i["L0_gnn_bn_mean"]),
         tiles(i["L0_gnn_bn_var"]), tiles(i["L0_ffn_b1"].reshape(-1)), tiles(i["L3_ffn_b1"].reshape(-1)),
         tiles(i["L2_gnn_b1"]), gate(i["L0_ffn_gate_w"]), gate(i["L1_ffn_router_w"]), gate(i["L3_ffn_gate_w"]),
         i["L2_ffn_slot_params"].reshape(KD, P, SLOTS).transpose(1, 0, 2).reshape(P, -1), b_down], axis=1)

    def row(v):
        return np.concatenate([v, np.zeros(D1 - v.size, np.float32)])[None]

    def wide(v):
        return np.concatenate([v.reshape(-1), np.zeros(HEADS * HEAD_DIM - v.size, np.float32)])[None]

    return dict(
        x_in=i["x"],
        edges_in=np.stack([i["src"].reshape(TN, ET), i["dst"].reshape(TN, ET), i["edge_type_3"].reshape(TN, ET)], axis=1),
        wa=stream(SEQ_A), wb=stream(SEQ_B), wc=stream(SEQ_C), cols_in=cols,
        bias_in=np.concatenate([row(i[k]) for k in ("L0_gnn_b2", "L1_gnn_b1", "L1_gnn_b2", "L2_gnn_b2", "L3_gnn_b1",
                                                    "L3_gnn_b2", "L3_gnn_b3")]),
        rows_in=np.concatenate([i["L0_ffn_b2"], i["L2_ffn_b_up"], i["L3_ffn_b2"]]),
        att_in=np.concatenate([wide(i[k]) for k in ("L2_gnn_att_src1", "L2_gnn_att_dst1", "L2_gnn_att_src2",
                                                    "L2_gnn_att_dst2")]),
        scalars_in=np.stack([i["L0_gnn_t"].reshape(1), i["L2_ffn_scale"].reshape(1)]),
        w_down_in=i["L2_ffn_W_down"], w_up_in=i["L2_ffn_W_up"], emb_in=i["L3_gnn_node_emb"],
        types_in=i["node_type_3"][None],
    )


def kernel(**inputs):
    import concourse.bacc as bacc
    from concourse.bass_utils import run_bass_kernel_spmd

    arrays = {k: np.ascontiguousarray(v) for k, v in laid_out(inputs).items()}
    nc = bacc.Bacc("TRN2", target_bir_lowering=False, num_devices=1)
    args = [nc.dram_tensor(k, arrays[k].shape, mybir.dt.from_np(arrays[k].dtype), kind="ExternalInput").ap() for k in NAMES]
    out = nc.dram_tensor("out", (NODES, D), f32, kind="ExternalOutput").ap()
    network(nc, *args, out)
    r = run_bass_kernel_spmd(nc, [arrays], core_ids=[0])
    return r.results[0]["out"]
```

```python
import numpy as np
import concourse.bass as bass
import concourse.mybir as mybir
from concourse.alu_op_type import AluOpType as ALU
from contextlib import ExitStack

f32, f32r = mybir.dt.float32, mybir.dt.float32r
bf16, i16, i32, u32 = mybir.dt.bfloat16, mybir.dt.int16, mybir.dt.int32, mybir.dt.uint32
ACT = mybir.ActivationFunctionType
AX = mybir.AxisListType

P = 128
NODES, D = 625, 768
NT, TN = 5, 125
NP = NODES + 1
CH = [(0, 314), (314, 312)]
KD = D // P
EDGES = 10000
ET = EDGES // TN
HALF = NP // 2
FRACTION = 2.0 ** -12
SPAN = 16
SPANS = ET // SPAN
assert SPAN * SPANS == ET and SPAN * TN < 2048
ROUNDER = 1.5 * 2.0 ** 23
TYPE_DIM = 128
D1 = D + TYPE_DIM
K1 = D1 // P
RELS = 3
EXPERTS = 8
HEADS, HEAD_DIM = 8, 128
SLOTS = 32
SLOT_H = 96
UNIT, UNIT_WIDE = 768, 896
RING = 3
SMALL = 592
EXPERT_LAG = 5
LN_EPS = 1e-5
FAR = -2.0 ** 100

UP_UNITS = dict(g0=12, f0=12, f1=8, f3=12)
DOWN = {
    "g0d": (12, 384, 2, 2), "f0d": (12, 384, 2, 2), "g1a": (6, 384, 2, 2), "g1b": (6, 384, 2, 2),
    "f1d": (8, 384, 2, 2), "g2a": (6, 256, 4, 3), "g2b": (8, 384, 2, 2),
    "g3a": (K1, 448, 2, 2), "g3b": (K1, 384, 2, 2), "g3c": (KD, 384, 2, 2), "f3d": (12, 384, 2, 2),
}
FEEDS = RELS + 1


def down_units(key):
    k, _, chunks, per = DOWN[key]
    n = k * chunks * (FEEDS if key in ("g3a", "g3b", "g3c") else 1)
    assert n % per == 0
    return n // per


SEQ_A = [("u", "g0"), ("d", "g0d"), ("u", "f0"), ("d", "f0d"), ("d", "g1a"), ("d", "g1b"),
         ("u", "f1"), ("d", "f1d"), ("d", "g2a"), ("d", "g2b")]
SEQ_B = [("d", "g3a")]
SEQ_C = [("d", "g3b"), ("d", "g3c"), ("u", "f3"), ("d", "f3d")]
FIRST_UNIT, at = {}, 0
for kind, key in SEQ_A + SEQ_B + SEQ_C:
    FIRST_UNIT[kind, key] = at
    at += UP_UNITS[key] if kind == "u" else down_units(key)
UNITS_A, UNITS_B = FIRST_UNIT["d", "g3a"], down_units("g3a")
UNITS = at
UNITS_C = UNITS - UNITS_A - UNITS_B

COLS, at = {}, 0
for name, n in [("bn_b1", 12), ("bn_gamma", 12), ("bn_beta", 12), ("bn_mean", 12), ("bn_var", 12),
                ("f0_b1", 12), ("f3_b1", 12), ("g2_b1", 8), ("f0_gate", 48), ("f1_gate", 48),
                ("f3_gate", 48), ("slots", KD * SLOTS), ("b_down", 8)]:
    COLS[name] = (at, at + n)
    at += n
NCOLS = at


def plan_groups():
    groups = []
    where = {}

    def add(label, idx, sem, value):
        where[label, idx] = len(groups)
        groups.append((sem, value))

    def several(label, n, sem, first=0, per=1):
        for i in range(n):
            add(label, i, sem, first + (i + 1) * per)

    def sweep(label):
        for i in range(SPANS * NT):
            add(label, i, label + "_counted", i + 1)

    def ffn(f, tiles):
        several(f + "_xT", 2 * NT, f + "_xT_low")
        several(f + "_routerT", 2, f + "_routerT_read")
        jobs, lag = 2 * tiles, EXPERT_LAG
        for j in range(jobs + lag):
            if j < jobs:
                add(f + "_hidden", j, f + "_activated", j + 1)
            if j == 0:
                add(f + "_router", 0, f + "_routed", 1)
            if j == lag - 1:
                if f == "f1":
                    add(f + "_importance", 0, f + "_importance_read", 1)
                several(f + "_cT", NT, f + "_combineT")
            if j >= lag:
                add(f + "_cB", j - lag, f + "_weighted", j - lag + 1)
        several(f + "_down", 2 * NT, f + "_x")

    def rows(c):
        for i in range(2):
            add("g2p_asT", 2 * c + i, "g2p_asT_read", 2 * c + i + 1)
        for i in range(4):
            add("g2p_asB", 4 * c + i, "g2p_asB_read", 4 * c + i + 1)

    def attention_groups(layer, heads):
        several(layer + "_uvT", 4, layer + "_uvT_read")
        for h in range(heads + 2):
            if h < heads:
                for i in range(4):
                    add(layer + "_uvB", 4 * h + i, layer + "_uvB_read", 4 * h + i + 1)
            if layer == "g2p" and h >= 2:
                for i in range(2):
                    add("g2p_outT", 2 * (h - 2) + i, "g2p_relu", 2 * (h - 2) + i + 1)
            if layer == "g2p" and 1 <= h <= heads:
                for n in range(NT):
                    add("g2p_agg", NT * (h - 1) + n, "g2p_mean", NT * (h - 1) + n + 1)

    add("g0_maxT", 0, "g0_max_read", 1)
    add("g0_maxB", 0, "g0_maxB_read", 1)
    sweep("A")
    several("g0_xT", 2 * NT, "g0_xT_copied")
    for j in range(2 * KD):
        add("g0_num", j, "g0_num_read", j + 1)
        add("g0_den", j, "g0_den_read", j + 1)
    add("g1_deg", 0, "g1_deg_read", 1)
    several("g0_hidden", 24, "g0_activated")
    several("g0d", 2 * NT, "g0_x")
    ffn("f0", 12)
    several("g1a_agg", 2 * KD, "g1a_low")
    several("g1a", 2 * NT, "g1a_read")
    several("g1b_agg", 2 * KD, "g1b_low")
    for n in range(NT):
        add("g1b", n, "g1_x", n + 1)
    several("g2_maskT", 2 * NT, "g2_masked")
    for n in range(NT):
        add("g1b", NT + n, "g1_x", NT + n + 1)
    ffn("f1", 8)
    several("g2_xT", 2 * NT, "g2_xT_low")
    for c in range(5):
        if c < 4:
            for n in range(NT):
                add("g2a", c * NT + n, "g2_h1", c * NT + n + 1)
        if c:
            rows(c - 1)
    attention_groups("g2p", HEADS)
    several("g2b", 2 * NT, "g2_h2")
    several("g2q_asT", 2, "g2q_asT_read")
    several("g2q_asB", 2, "g2q_asB_read")
    attention_groups("g2q", 1)
    several("g2q_agg", 2 * NT, "g2_x")
    several("f2_xT", 2 * NT, "f2_xT_low")
    several("f2_logitsT", 2, "f2_logitsT_read")
    several("f2_logits", 1, "f2_logits_read")
    several("f2_dispatch", 1, "f2_dispatch_read")
    several("f2_combineT", 2, "f2_combineT_read")
    several("f2_tilde", 1, "f2_tilde_read")
    several("f2_hidden", 1, "f2_hidden_read")
    several("f2_up", 2, "f2_up_read")
    several("f2_down", 2 * NT, "f2_x")
    several("g3_emb", NT, "g3_emb_low")
    for r in range(RELS - 1):
        sweep(f"R{r}")
    for key, k in (("g3a", K1), ("g3b", K1), ("g3c", KD)):
        several(key + "_hT", 2 * NT, key + "_hT_low")
        several(key + "_root", 2 * NT, key + "_acc", 0)
        for r in range(RELS):
            if key == "g3a":
                add("g3_deg", r, "g3_deg_read", r + 1)
            several(f"{key}_agg{r}", 2 * k, f"{key}_low", 2 * k * r)
            several(f"{key}_rel{r}", 2 * NT, key + "_acc", 2 * NT * (r + 1))
    ffn("f3", 12)
    return groups, where


GROUPS, WHERE = plan_groups()


def families():
    table = {}

    def family(kind, totals):
        base = 0
        for layer, total in totals:
            table[layer + "_" + kind] = (kind, base)
            base += total

    def each(layers, total):
        return [(s, total) for s in layers.split()]

    for kind, n in (("var", 1), ("std", 1), ("xn", NT)):
        family(kind, each("g0 f0 g1 f1 g2 f2 g3 f3", n))
    for half in ("high", "low"):
        family("T_" + half, each("f0_x f1_x g2_x f2_x g3a_h g3b_h g3c_h f3_x", 2 * NT))
        for layer in "f0_x f1_x g2_x f2_x g3a_h g3b_h g3c_h f3_x".split():
            table[layer + "T_" + half] = table.pop(layer + "_T_" + half)
        family(half, [("g0", 24), ("f0", 24), ("g1a", 12), ("g1b", 12), ("f1", 16), ("g2p", HEADS),
                      ("g3a", 6 * K1), ("g3b", 6 * K1), ("g3c", 6 * KD), ("f3", 24)])
        family("nodes_" + half, [("g1", NT), ("g1b", 2 * NT), ("g3a", NT), ("g3b", NT), ("g3c", NT)])
    family("T_pad", each("g0_x f0_x f1_x g2_x f2_x g3a_h g3b_h g3c_h f3_x", 2))
    for layer in "g0_x f0_x f1_x g2_x f2_x g3a_h g3b_h g3c_h f3_x".split():
        table[layer + "T_pad"] = table.pop(layer + "_T_pad")
    family("activated", [("g0", 24), ("f0", 24), ("f1", 16), ("f3", 24)])
    family("weighted", [("f0", 24), ("f1", 16), ("f3", 24)])
    family("x", each("g0 f0 g1 f1 g2 f2", 2 * NT) + [("g3", NT), ("f3", 2 * NT)])
    for kind, n in (("routed", 1), ("routerT_read", 2), ("shifted", 1), ("exp", 1), ("probs", 1), ("combine", 1), ("cT_pad", 2), ("cT_high", NT),
                    ("combineT", NT), ("cpad_clear", 1)):
        family(kind, each("f0 f1 f3", n))
    family("bias_full", [("g0", 16), ("f0", 64), ("g1", 16), ("g1b", 16), ("g2", 16), ("f2", 16), ("g3a", 16),
                         ("g3b", 16), ("g3c", 16), ("f3", 64)])
    family("rows_clear", each("f0 f3", 1))
    family("rows_split", each("f0 f3", 2))
    family("hot", each("A R0 R1", 2 * ET))
    family("hot_used", each("A R0 R1", ET - SPANS))
    for kind in ("rounded", "whole", "counted"):
        family(kind, each("A R0 R1", SPANS * NT))
    family("whole_added", each("A R0 R1", (SPANS - 1) * NT))
    family("fraction_added", each("A R0 R1", (SPANS - 2) * NT))
    family("fraction_summed", each("A R0 R1", NT))
    family("counts_ready", each("A R0 R1", NT))
    family("nodes", each("g3b g3c", NT))
    family("acc", each("g3a g3b g3c", 2 * NT * FEEDS))
    for kind, n in (("asB_read", 2), ("max_done", NT), ("uvB_read", 4), ("shift", NT), ("leaky", NT), ("powers", 1),
                    ("prob", 1)):
        family(kind, [("g2p", n * HEADS), ("g2q", n)])
    family("asT_read", [("g2p", 8), ("g2q", 2)])
    for kind, n in (("uvT_read", 4), ("uv", 2), ("pads", 2)):
        family(kind, each("g2p g2q", n))
    return table


FAMILY = families()


def network(nc, x_in, edges_in, wa, wb, wc, cols_in, bias_in, rows_in, att_in, scalars_in, w_down_in,
            w_up_in, emb_in, types_in, out):
    ctx = ExitStack()
    with ctx:
        sems = {}

        def S(event):
            name = FAMILY.get(event, (event, 0))[0]
            if name not in sems:
                sems[name] = ctx.enter_context(nc.semaphore(name))
            return sems[name]

        def E(event, count):
            return S(event), count + FAMILY.get(event, (event, 0))[1]

        arena_bytes = 212800
        start = -(-nc.sbuf_base // 64) * 64
        arena = ctx.enter_context(nc.sbuf_tensor("arena", [P, arena_bytes], mybir.dt.uint8))
        top = [start]

        def up32(n):
            return -(-n // 32) * 32

        def region(nbytes):
            off = top[0]
            top[0] += up32(nbytes)
            assert top[0] <= start + arena_bytes, (top[0] - start, arena_bytes)
            return off

        size = {f32: 4, f32r: 4, i32: 4, u32: 4, bf16: 2, i16: 2}

        def at_(name, shape, dt, off):
            return nc.alloc_sbuf_tensor_at(name, shape, dt, offset=off)

        def new(name, shape, dt=f32):
            return at_(name, shape, dt, region(int(np.prod(shape[1:])) * size[dt]))

        x = new("x", [TN, NT, D])
        XT = region(2 * up32(K1 * NP * 4) + 64)
        HT = region(2 * 12 * NP * 4)
        NM = region(2 * NT * D1 * 4)
        xt_lo_off = XT + up32(K1 * NP * 4)
        xT_hi, xT_lo = at_("xT_hi", [P, K1, NP], f32r, XT), at_("xT_lo", [P, K1, NP], f32r, xt_lo_off)
        ht_lo_off = HT + 12 * NP * 4
        hT_hi, hT_lo = at_("hT_hi", [P, 12, NP], f32r, HT), at_("hT_lo", [P, 12, NP], f32r, ht_lo_off)
        nm_hi = at_("nm_hi", [TN, NT, D1], f32r, NM)
        nm_lo = at_("nm_lo", [TN, NT, D1], f32r, NM + NT * D1 * 4)
        xn = at_("xn", [TN, NT, D], f32, HT)
        e_hi = at_("e_hi", [TN, NT, D], f32r, HT + 15360)
        e_lo = at_("e_lo", [TN, NT, D], f32r, HT + 30720)
        acc = at_("acc", [TN, NT, D1], f32, HT)
        rel = at_("rel", [TN, RELS, NT, NP], f32r, HT + 17920)
        OH = HT + 17920 + up32(RELS * NT * NP * 4)
        assert OH <= NM
        OSLOTS = 4
        src_hot = at_("src_hot", [TN, OSLOTS, NODES], bf16, XT)
        dst_hot = at_("dst_hot", [TN, OSLOTS, CH[0][1]], bf16, XT + up32(OSLOTS * NODES * 2))
        msg = at_("msg", [TN, NT, D], f32, xt_lo_off)
        xT_full = at_("xT_full", [P, KD, NP], f32, xt_lo_off)
        HD = HEAD_DIM + 2
        h1 = at_("h1", [TN, NT, HEADS, HD], f32, NM)
        mask_off = NM + NT * HEADS * HD * 4
        maskT = at_("maskT", [TN, NT, NP], bf16, mask_off)
        gat_small = mask_off + up32(NT * NP * 2)
        h2 = at_("h2", [TN, NT, D + 2], f32, NM)
        prob = [at_(f"prob{i}", [TN, NT, NP], f32, XT + i * up32(NT * NP * 4)) for i in range(2)]
        uB = [at_(f"uB{i}", [TN, 2, NP], f32, XT + 2 * up32(NT * NP * 4) + i * up32(2 * NP * 4)) for i in range(2)]
        att = at_("att", [TN, 2, HEADS * HEAD_DIM], f32, HT + 8 * NP * 4)
        w_down = at_("w_down", [P, EXPERTS, KD, SLOT_H], f32, HT + 15360)
        w_up = at_("w_up", [SLOT_H, EXPERTS, D], f32, HT + 15360 + 18432)
        sp_hi = at_("sp_hi", [P, KD, SLOTS], f32r, XT + up32(KD * NP * 4))
        sp_lo = at_("sp_lo", [P, KD, SLOTS], f32r, xt_lo_off + up32(KD * NP * 4))

        adj = new("adj", [TN, NT, NP], f32r)
        raw = new("raw", [P, RING, UNIT_WIDE])
        w_hi = new("w_hi", [P, RING, UNIT_WIDE], f32r)
        w_lo = new("w_lo", [P, RING, UNIT_WIDE], f32r)
        bias_off = region(D1 * 4)
        bias = at_("bias", [TN, D1], f32, bias_off)
        bias8 = at_("bias8", [P, D], f32, bias_off)
        TSLOTS = 6
        tmp_off = region(TSLOTS * CH[0][1] * 4)
        tmp = at_("tmp", [P, TSLOTS, CH[0][1]], f32, tmp_off)
        iota = new("iota", [TN, NP], i16)
        ident = new("ident", [P, P])
        ones_r = new("ones_r", [P, P], f32r)
        ones = ones_r[:].bitcast(f32)
        nm_at = [NM]

        def nm_new(name, shape, dt):
            off = nm_at[0]
            nm_at[0] += up32(int(np.prod(shape[1:])) * 4)
            return at_(name, shape, dt, off)

        cpad = nm_new("cpad", [TN, NT, P], f32)
        cT_hi, cT_lo = nm_new("cT_hi", [P, NP], f32r), nm_new("cT_lo", [P, NP], f32r)
        bias8_hi, bias8_lo = nm_new("bias8_hi", [P, D], f32r), nm_new("bias8_lo", [P, D], f32r)
        router_T = nm_new("router_T", [EXPERTS, NP], f32)
        assert nm_at[0] <= NM + 20480
        pat = new("pat", [P, 3, P], f32r)
        cols = new("cols", [P, NCOLS])
        gate_hi = new("gate_hi", [P, 3 * 48], f32r)
        gate_lo = new("gate_lo", [P, 3 * 48], f32r)
        e_int = at_("e_int", [TN, 3, ET], i32, NM)
        edge = new("edge", [TN, 3, ET])
        small = new("small", [P, SMALL])
        sp_tmp = at_("sp_tmp", [P, KD, SLOTS], f32, tmp_off)

        used_small = [0]

        def sm(n):
            a = used_small[0]
            used_small[0] += n
            assert used_small[0] <= SMALL
            return small[:, a:a + n]

        stats, moments, rstd = sm(NT * 12), sm(NT * 2), sm(NT)
        t_col, slot_scale, tiny, rounder, unrounder = (sm(1) for _ in range(5))
        dinv, rel_inv = sm(NT), sm(RELS * NT)
        peak, peak_all = sm(8), sm(2)
        bn_s, bn_b = sm(12), sm(12)
        iota8, rel_index = sm(8), sm(1)
        logit8, prob8, hot8, top8, idx8f = (sm(NT * 8) for _ in range(5))
        sum8, run8 = sm(NT), sm(8)
        sel8 = sm(SLOTS)
        a_src, a_dst, a_src5, a_max = (sm(NT * 8) for _ in range(4))
        no_edge = sm(NT)
        a_part = sm(NT * 4)
        idx8 = new("idx8", [P, NT * 8], u32)
        emb = at_("emb", [RELS, TYPE_DIM], f32, tmp_off + 3200)
        asT = at_("asT", [2, NP], f32, gat_small)
        uT = at_("uT", [HEADS, NP], f32, gat_small + up32(NP * 4))
        vT = at_("vT", [HEADS, NP], f32, gat_small + 2 * up32(NP * 4))
        assert gat_small + 3 * up32(NP * 4) <= NM + 2 * NT * D1 * 4
        head_sel = at_("head_sel", [HEADS, HEADS, P], f32, ht_lo_off + 8 * NP * 4)
        uv = at_("uv", [TN, 2, NT, 8], f32, ht_lo_off + 8 * NP * 4 + 4096)
        asB = at_("asB", [TN, 2, NP], f32, tmp_off)
        mean = at_("mean", [TN, 2, NT, HEAD_DIM], f32, tmp_off)
        junk = at_("junk", [TN, D], f32, ht_lo_off + 8 * NP * 4 + 4096 + 512)
        edge_scores = [at_("edge_scores0", [TN, NP], f32, xt_lo_off + up32(KD * NP * 4)),
                       at_("edge_scores1", [TN, NP], f32, tmp_off + up32(2 * NP * 4))]
        head_T = at_("head_T", [P, NODES], f32, ht_lo_off + 8 * NP * 4 + 4096 + 512)
        e_full = [at_(f"e_full{i}", [TN, D], f32, HT + 46080 + i * 3072) for i in range(2)]
        g0_junk = at_("g0_junk", [TN, D], f32, tmp_off)
        f2s = [NM]

        def f2_new(name, shape):
            off = f2s[0]
            f2s[0] += up32(int(np.prod(shape[1:])) * 4)
            assert f2s[0] <= NM + 2 * NT * D1 * 4
            return at_(name, shape, f32, off)

        slot_logits = f2_new("slot_logits", [TN, NT, SLOTS])
        combine = f2_new("combine", [TN, NT, SLOTS])
        dispatch = f2_new("dispatch", [TN, NT, SLOTS])
        logitsT, combineT = f2_new("logitsT", [SLOTS, NP]), f2_new("combineT", [SLOTS, NP])
        tildeT = f2_new("tildeT", [P, KD, SLOTS])
        slot_hidden = f2_new("slot_hidden", [SLOT_H, EXPERTS, 4])
        hidden_diag = f2_new("hidden_diag", [SLOT_H, EXPERTS * 36])
        slot_out = f2_new("slot_out", [SLOTS, D])
        slot_sum, col_peak, col_sum = f2_new("slot_sum", [P, KD * 4]), f2_new("col_peak", [TN, NT]), f2_new("col_sum", [TN, NT])
        row_peak, row_sum = f2_new("row_peak", [SLOTS, 1]), f2_new("row_sum", [SLOTS, 1])
        f2_junk = f2_new("f2_junk", [TN, D])
        node_type_i = at_("node_type_i", [RELS, NODES], i32, tmp_off)
        types = at_("types", [TN, ET], f32, NM)
        src_plus = at_("src_plus", [TN, ET], f32, NM + 320)
        rel_source = at_("rel_source", [TN, RELS - 1, ET], f32, NM + 640)
        rounded = at_("rounded", [TN, 2, HALF], f32, tmp_off)
        fraction_parts = at_("fraction_parts", [TN, 4, HALF], f32, tmp_off + up32(2 * HALF * 4))
        assert up32(2 * HALF * 4) + 4 * HALF * 4 <= TSLOTS * CH[0][1] * 4
        whole_parts = {"A": at_("whole_parts_A", [TN, NT, HALF], f32, HT + 52224),
                       "R": at_("whole_parts_R", [TN, NT, HALF], f32, xt_lo_off)}
        dst_place = at_("dst_place", [TN, ET], f32, XT + up32(OSLOTS * (NODES + 2 * HALF) * 2) + 64)
        dst_adds = at_("dst_adds", [TN, ET], f32, XT + up32(OSLOTS * (NODES + 2 * HALF) * 2) + 64 + 320)
        type_hot = at_("type_hot", [RELS, NODES], f32, tmp_off + 3712)

        banks = [ctx.enter_context(nc.psum_tensor(f"bank{b}", [P, 512], f32)) for b in range(8)]
        block = ctx.enter_context(nc.Block())

        def bank(label, i):
            return banks[WHERE[label, i] % 8]

        def col(name, i=None):
            a, b = COLS[name]
            return cols[:, a:b] if i is None else cols[:, a + i:a + i + 1]

        def await_group(engine, label, i):
            engine.wait_ge(*E("group_closed", WHERE[label, i] + 1))

        def f(ap):
            return ap.bitcast(f32)

        node_view = "(n p) d -> p n d"

        def ring_units(engine, first, count, body):
            last = first + count
            q0, q1 = -(-first // RING), last // RING
            for u in range(first, q0 * RING):
                body(u, u // RING, u % RING)
            with engine.Fori(q0, q1) as q:
                for k in range(RING):
                    body(q * RING + k, q, k)
            for u in range(q1 * RING, last):
                body(u, u // RING, u % RING)

        SEGMENTS = [(0, UNITS_A, wa, UNIT), (UNITS_A, UNITS_B, wb, UNIT_WIDE),
                    (UNITS_A + UNITS_B, UNITS_C, wc, UNIT)]

        @block.sync
        def _(sp):
            sp.dma_start(x[:], x_in.rearrange(node_view, p=TN)).then_inc(S("x_loaded"), 16)
            sp.dma_start(e_int[:], edges_in).then_inc(S("edges_loaded"), 16)
            sp.dma_start(cols[:], cols_in).then_inc(S("cols_loaded"), 16)

            def load(first, src, width):
                def body(u, q, k):
                    sp.wait_ge(*E("unit_split", u - RING + 1))
                    sp.dma_start(raw[:, k, 0:width], src[bass.ds(u - first, 1)].rearrange("a p n -> (a p) n")
                                 ).then_inc(S(f"raw_full{k}"), 16)
                return body

            for k in range(RING):
                sp.dma_start(raw[:, k, 0:UNIT], wa[k]).then_inc(S(f"raw_full{k}"), 16)
            ring_units(sp, RING, UNITS_A - RING, load(0, wa, UNIT))
            sp.wait_ge(*E("g2q_uvB_read", 4))
            for e in range(EXPERTS):
                sp.dma_start(w_down[:, e], w_down_in[e].rearrange("(k p) h -> p k h", p=P)
                             ).then_inc(S("slot_weights"), 16)
            sp.dma_start(w_up[:], w_up_in.rearrange("e h d -> h e d")).then_inc(S("slot_weights"), 16)
            ring_units(sp, UNITS_A, UNITS_B, load(UNITS_A, wb, UNIT_WIDE))
            ring_units(sp, UNITS_A + UNITS_B, UNITS_C, load(UNITS_A + UNITS_B, wc, UNIT))
            for c in range(2):
                sp.wait_ge(*E("f3_x", NT * (c + 1)))
                sp.dma_start(out.rearrange(node_view, p=TN)[:, :, c * 384:(c + 1) * 384],
                             x[:, :, c * 384:(c + 1) * 384]).then_inc(S("stored"), 16)
            sp.wait_ge(*E("stored", 32))

        @block.gpsimd
        def _(pool):
            pool.iota(iota[:], pattern=[[1, NP]], base=0, channel_multiplier=0).then_inc(S("consts"), 1)
            pool.iota(idx8[:, 0:8].bitcast(i32), pattern=[[1, 8]], base=0, channel_multiplier=0).then_inc(S("consts"), 1)
            pool.iota(idx8[:, 8:9].bitcast(i32), pattern=[[0, 1]], base=0, channel_multiplier=1).then_inc(S("consts"), 1)
            pool.memset(ones, 1.0).then_inc(S("blanks"), 1)
            pool.memset(f(pat[:]), 0.0).then_inc(S("blanks"), 1)
            pool.memset(sel8[0:8, :], 1.0).then_inc(S("blanks"), 1)
            pool.wait_ge(*E("blanks", 3))
            pool.affine_select(out=ident[:], in_=ones, compare_op=ALU.is_equal, fill=0.0, base=0,
                               pattern=[[-1, P]], channel_multiplier=1).then_inc(S("consts"), 1)
            pool.affine_select(out=sel8[0:8, :].rearrange("p (e s) -> p e s", e=8),
                               in_=sel8[0:8, :].rearrange("p (e s) -> p e s", e=8), compare_op=ALU.is_equal,
                               fill=0.0, base=0, pattern=[[-1, 8], [0, 4]], channel_multiplier=1
                               ).then_inc(S("consts"), 1)
            made = 5
            for q in range(4):
                rows = slice(32 * q, 32 * q + 2)
                for kind, a, b, first in ((0, 0, P, True), (1, 0, 64, True), (1, 64, P, False), (2, 0, P, False)):
                    pool.wait_ge(*E("consts", made))
                    made += 1
                    pool.affine_select(out=pat[rows, kind, a:b], in_=ones[rows, a:b],
                                       compare_op=ALU.is_equal, fill=0.0, base=0 if first else -1,
                                       pattern=[[0, b - a]], channel_multiplier=1).then_inc(S("consts"), 1)

            pool.wait_ge(*E("consts", made))

            def add_counts(label, target, span):
                for s in range(NT):
                    i = span * NT + s
                    pool.wait_ge(*E(label + "_whole", i + 1))
                    if span > 1:
                        pool.wait_ge(*E(label + "_whole_added", i - 2 * NT + 1))
                    pool.tensor_tensor(target[:, s, 0:HALF], f(target[:, s, 0:HALF]),
                                       whole_parts[label[0]][:, s], ALU.add).then_inc(S(label + "_whole_added"), 1)
                    if span < SPANS - 1:
                        pool.wait_ge(*E(label + "_counted", i + 1))
                        if span > 1:
                            pool.wait_ge(*E(label + "_fraction_added", i - 2 * NT + 1))
                        pool.tensor_tensor(target[:, s, HALF:NP], f(target[:, s, HALF:NP]),
                                           fraction_parts[:, i % 4], ALU.add
                                           ).then_inc(S(label + "_fraction_added"), 1)

            for n in range(NT):
                pool.wait_ge(*E("g0_exp_high", n + 1))
                pool.tensor_tensor(msg[:, n], msg[:, n], e_full[n % 2][:], ALU.mult).then_inc(S("g0_num_full"), 1)
                pool.tensor_tensor(e_lo[:, n], e_full[n % 2][:], f(e_hi[:, n]), ALU.subtract).then_inc(S("g0_exp_low"), 1)
                pool.wait_ge(*E("g0_num_high", n + 1))
                pool.tensor_tensor(nm_lo[:, n, 0:D], msg[:, n], f(nm_hi[:, n, 0:D]), ALU.subtract
                                   ).then_inc(S("g0_num_low"), 1)
                if n >= 2:
                    add_counts("A", adj, n - 1)
            add_counts("A", adj, SPANS - 1)
            pool.wait_ge(*E("g0_bias_full", 16))
            for n in range(NT):
                pool.tensor_tensor(x[:, n], x[:, n], xn[:, n], ALU.add).then_inc(S("g0_residual"), 1)
            for n in range(NT):
                pool.wait_ge(*E("g0_residual", NT + n))
                pool.tensor_tensor(x[:, n], x[:, n], bias[:, 0:D], ALU.add).then_inc(S("g0_residual"), 1)

            def split(width):
                def body(u, q, k):
                    pool.wait_ge(*E(f"raw_full{k}", 16 * q + 16))
                    if not (isinstance(u, int) and u < RING):
                        pool.wait_ge(*E("unit_used", u - RING + 1))
                    pool.tensor_tensor(w_hi[:, k, 0:width], raw[:, k, 0:width],
                                       ones[:, 0:1].to_broadcast([P, width]), ALU.mult).then_inc(S("unit_high"), 1)
                    pool.wait_ge(*E("unit_high", u + 1))
                    pool.tensor_tensor(w_lo[:, k, 0:width], raw[:, k, 0:width], f(w_hi[:, k, 0:width]),
                                       ALU.subtract).then_inc(S("unit_split"), 1)
                return body

            for u in range(RING):
                split(UNIT)(u, 0, u)
            ring_units(pool, RING, UNITS_A - RING, split(UNIT))
            for r in range(RELS - 1):
                for span in range(1, SPANS):
                    add_counts(f"R{r}", rel[:, r], span)
            ring_units(pool, UNITS_A, UNITS_B, split(UNIT_WIDE))
            ring_units(pool, UNITS_A + UNITS_B, UNITS_C, split(UNIT))

        @block.scalar
        def _(act):
            done = [0]

            def link(ins):
                done[0] += 1
                ins.then_inc(S("act_step"), 1)
                act.wait_ge(*E("act_step", done[0]))

            def fill_bias(name, row, width):
                act.dma_start(bias[:, 0:width], bias_in[row:row + 1, 0:width].to_broadcast([TN, width])
                              ).then_inc(S(name), 16)

            def fill_pairs(name, row):
                for q in range(4):
                    act.dma_start(bias8[32 * q:32 * q + 2, :], rows_in[row + 2 * q:row + 2 * q + 2, :]
                                  ).then_inc(S(name), 16)

            def root_of_variance(s):
                act.wait_ge(*E(s + "_var", 1))
                act.activation(rstd[0:TN], rstd[0:TN], ACT.Sqrt).then_inc(S(s + "_std"), 1)

            def xT_high(label, k):
                for i in range(2 * NT):
                    n, (a, b) = i // 2, ((0, 4), (4, k))[i % 2]
                    await_group(act, label, i)
                    act.activation(xT_hi[:, a:b, n * TN:(n + 1) * TN],
                                   bank(label, i)[:, 0:(b - a) * TN].rearrange("p (k n) -> p k n", n=TN),
                                   ACT.Copy).then_inc(S(label + "_high"), 1)

            def nodes_high(full, width, src, high):
                for n in range(NT):
                    act.wait_ge(*E(full, n + 1))
                    act.activation(nm_hi[:, n, 0:width], src[:, n, 0:width], ACT.Copy).then_inc(S(high), 1)

            def messages_high(key, label, k, first=0):
                for i in range(2 * k):
                    ft, (c0, cn) = i // 2, CH[i % 2]
                    await_group(act, label, i)
                    act.activation(xT_hi[:, ft, c0:c0 + cn], bank(label, i)[:, 0:cn], ACT.Copy
                                   ).then_inc(S(key + "_high"), 1)

            def counts(label, target, span):
                for i in range(span * NT, span * NT + NT + 1):
                    s = i - span * NT
                    if s < NT:
                        await_group(act, label, i)
                        if i >= 2 or label == "R1":
                            act.wait_ge(*E(label + "_counted", max(i - 1, 0)))
                            act.wait_ge(*E(label + "_whole", max(i - 1, 0)))
                        act.activation(rounded[:, i % 2], bank(label, i)[0:TN, 0:HALF], ACT.Identity,
                                       bias=rounder[0:TN]).then_inc(S(label + "_rounded"), 1)
                    if s:
                        s, j = s - 1, i - 1
                        act.wait_ge(*E(label + "_rounded", j + 1))
                        if span and (span > 1 or label == "R1"):
                            act.wait_ge(*E(label + "_whole_added", max(j - 2 * NT + 1, 0)))
                        dst = whole_parts[label[0]][:, s] if span else target[:, s, 0:HALF]
                        act.activation(dst, rounded[:, j % 2], ACT.Identity, bias=unrounder[0:TN]
                                       ).then_inc(S(label + "_whole"), 1)

            def second_half(label, target):
                for s in range(NT):
                    act.wait_ge(*E(label + "_fraction_summed", s + 1))
                    act.activation(target[:, s, HALF:NP], f(target[:, s, HALF:NP]), ACT.Copy, scale=-1 / FRACTION
                                   ).then_inc(S(label + "_counts_ready"), 1)

            def hidden(s, tiles, func, scale_bias, full):
                jobs = 2 * tiles
                for j in range(jobs + TSLOTS - 1):
                    if j < jobs:
                        cn = CH[j % 2][1]
                        await_group(act, s + "_hidden", j)
                        if j >= TSLOTS:
                            act.wait_ge(*E(s + "_low", j - TSLOTS + 1))
                        act.activation(tmp[:, j % TSLOTS, 0:cn], bank(s + "_hidden", j)[:, 0:cn], func,
                                       **scale_bias(j // 2)).then_inc(S(s + "_activated"), 1)
                    if j >= TSLOTS - 1:
                        i = j - TSLOTS + 1
                        c0, cn = CH[i % 2]
                        act.wait_ge(*E(full, i + 1))
                        act.activation(hT_hi[:, i // 2, c0:c0 + cn], tmp[:, i % TSLOTS, 0:cn], ACT.Copy
                                       ).then_inc(S(s + "_high"), 1)

            def expert_layer(s, tiles, func, biased):
                root_of_variance(s)
                xT_high(s + "_xT", KD)
                for c, (c0, cn) in enumerate(CH):
                    await_group(act, s + "_routerT", c)
                    act.activation(router_T[:, c0:c0 + cn], bank(s + "_routerT", c)[0:EXPERTS, 0:cn], ACT.Copy
                                   ).then_inc(S(s + "_routerT_read"), 1)
                act.wait_ge(*E(s + "_shifted", 1))
                act.activation(prob8[0:TN], prob8[0:TN], ACT.Exp).then_inc(S(s + "_exp"), 1)
                hidden(s, tiles, func, (lambda m: dict(bias=col(s + "_b1", m))) if biased else (lambda m: {}),
                       s + "_weighted")

            def rows_broadcast(layer, first, heads=2):
                for h in range(first, first + heads):
                    for c, (c0, cn) in enumerate(CH):
                        await_group(act, layer + "_asB", 2 * h + c)
                        if h >= 2:
                            act.wait_ge(*E(layer + "_max_done", NT * (h - 1)))
                        act.activation(asB[:, h % 2, c0:c0 + cn], bank(layer + "_asB", 2 * h + c)[0:TN, 0:cn],
                                       ACT.Copy).then_inc(S(layer + "_asB_read"), 1)

            act.dma_start(t_col[0:TN, :], scalars_in[0:1, :].to_broadcast([TN, 1])).then_inc(S("scalars_loaded"), 16)
            act.dma_start(slot_scale, scalars_in[1:2, :].to_broadcast([P, 1])).then_inc(S("scalars_loaded"), 16)
            fill_bias("g0_bias_full", 0, D)
            act.wait_ge(*E("consts", 21))
            act.wait_ge(*E("cols_loaded", 16))
            act.activation(gate_hi[:], cols[:, COLS["f0_gate"][0]:COLS["f3_gate"][1]], ACT.Copy
                           ).then_inc(S("gates_high"), 1)
            act.wait_ge(*E("bn_var", 1))
            act.activation(bn_s, bn_s, ACT.Sqrt).then_inc(S("bn_std"), 1)

            root_of_variance("g0")
            act.wait_ge(*E("g0_maxB_read", 1))
            for n in range(NT):
                if n >= 2:
                    act.wait_ge(*E("g0_exp_low", n - 1))
                act.activation(e_full[n % 2][:], msg[:, n], ACT.Exp, bias=peak_all[0:TN, 1:2], scale=t_col[0:TN, :]
                               ).then_inc(S("g0_exp"), 1)
                act.wait_ge(*E("g0_exp", n + 1))
                act.activation(e_hi[:, n], e_full[n % 2][:], ACT.Copy).then_inc(S("g0_exp_high"), 1)
                act.wait_ge(*E("g0_num_full", n + 1))
                act.activation(nm_hi[:, n, 0:D], msg[:, n], ACT.Copy).then_inc(S("g0_num_high"), 1)
                if n:
                    counts("A", adj, n - 1)
            counts("A", adj, NT - 1)
            second_half("A", adj)
            act.wait_ge(*E("g0_num_low", NT))
            for i in range(2 * NT):
                n, (a, b) = i // 2, ((0, 4), (4, KD))[i % 2]
                await_group(act, "g0_xT", i)
                act.activation(xT_full[:, a:b, n * TN:(n + 1) * TN],
                               bank("g0_xT", i)[:, 0:(b - a) * TN].rearrange("p (k n) -> p k n", n=TN),
                               ACT.Copy).then_inc(S("g0_xT_copied"), 1)
            for j in range(2 * KD + 1):
                if j < 2 * KD:
                    cn = CH[j % 2][1]
                    await_group(act, "g0_den", j)
                    if j >= 2:
                        act.wait_ge(*E("g0_num_read", j - 1))
                    act.activation(tmp[:, 2 + j % 2, 0:cn], bank("g0_den", j)[:, 0:cn], ACT.Identity, bias=tiny
                                   ).then_inc(S("g0_den_read"), 1)
                if j:
                    c0, cn = CH[(j - 1) % 2]
                    act.wait_ge(*E("g0_sum", j))
                    act.activation(xT_hi[:, (j - 1) // 2, c0:c0 + cn], tmp[:, (j - 1) % 2, 0:cn], ACT.Copy
                                   ).then_inc(S("g0_out_high"), 1)
            act.wait_ge(*E("g1_deg_ready", 1))
            act.activation(dinv[0:TN], dinv[0:TN], ACT.Sqrt).then_inc(S("g1_dinv"), 1)
            act.wait_ge(*E("g0_residual", NT))
            hidden("g0", 12, ACT.Relu, lambda m: dict(scale=bn_s[:, m:m + 1], bias=bn_b[:, m:m + 1]), "g0_activated")
            act.wait_ge(*E("f0_rows_clear", 1))
            fill_pairs("f0_bias_full", 0)
            expert_layer("f0", 12, ACT.Gelu, True)
            act.wait_ge(*E("f0_x", 2 * NT))
            fill_bias("g1_bias_full", 2, D)
            root_of_variance("g1")
            nodes_high("g1_scaled_nodes", D, xn, "g1_nodes_high")
            act.wait_ge(*E("g1_bias_used", 1))
            fill_bias("g1b_bias_full", 1, D)
            messages_high("g1a", "g1a_agg", KD)
            for i in range(2 * NT):
                n, c = i % NT, i // NT
                act.wait_ge(*E("g1a_full", i + 1))
                act.activation(nm_hi[:, n, c * 384:(c + 1) * 384], xn[:, n, c * 384:(c + 1) * 384], ACT.Copy
                               ).then_inc(S("g1b_nodes_high"), 1)
            fill_bias("g2_bias_full", 3, D)
            messages_high("g1b", "g1b_agg", KD)
            expert_layer("f1", 8, ACT.Silu, False)
            act.dma_start(att[:], att_in[0:2, :].unsqueeze(0).to_broadcast([TN, 2, HEADS * HEAD_DIM])
                          ).then_inc(S("g2p_att_full"), 16)
            root_of_variance("g2")
            xT_high("g2_xT", KD)
            for i in range(4 * NT):
                n, c = i % NT, i // NT
                await_group(act, "g2a", i)
                act.activation(h1[:, n, 2 * c:2 * c + 2, 0:HEAD_DIM],
                               bank("g2a", i)[0:TN, 0:256].rearrange("p (h d) -> p h d", h=2), ACT.Copy
                               ).then_inc(S("g2_h1"), 1)
                if n == NT - 1 and c:
                    rows_broadcast("g2p", 2 * c - 2)
            rows_broadcast("g2p", 6)

            def attention(layer, heads):
                act.wait_ge(*E(layer + "_max_done", NT * heads))

                def head_out(h):
                    for i, (a, b) in enumerate(((0, 4), (4, NT))):
                        await_group(act, "g2p_outT", 2 * h + i)
                        if h:
                            act.wait_ge(*E("g2p_low", h))
                        act.activation(head_T[:, a * TN:b * TN], bank("g2p_outT", 2 * h + i)[:, 0:(b - a) * TN],
                                       ACT.Relu, bias=col("g2_b1", h)).then_inc(S("g2p_relu"), 1)
                    act.wait_ge(*E("g2p_relu", 2 * h + 2))
                    act.activation(hT_hi[:, h, 0:NODES], head_T[:], ACT.Copy).then_inc(S("g2p_high"), 1)

                for h in range(heads + 2):
                    if h < heads:
                        for i in range(4):
                            c0, cn = CH[i % 2]
                            await_group(act, layer + "_uvB", 4 * h + i)
                            act.activation(uB[h % 2][:, i // 2, c0:c0 + cn], bank(layer + "_uvB", 4 * h + i)[0:TN, 0:cn],
                                           ACT.Copy).then_inc(S(layer + "_uvB_read"), 1)
                    if 1 <= h <= heads:
                        act.wait_ge(*E(layer + "_leaky", NT * h))
                        act.activation(prob[(h - 1) % 2][:], prob[(h - 1) % 2][:], ACT.Exp).then_inc(S(layer + "_powers"), 1)
                    if h < heads:
                        act.wait_ge(*E(layer + "_uvB_read", 4 * h + 4))
                        if h >= 2:
                            await_group(act, "g2p_agg", NT * (h - 2) + NT - 1)
                        for s in range(NT):
                            act.activation(prob[h % 2][:, s], uB[h % 2][:, 0], ACT.Identity,
                                           bias=a_src[0:TN, 8 * s + h:8 * s + h + 1]).then_inc(S(layer + "_shift"), 1)
                    if layer == "g2p" and h >= 2:
                        head_out(h - 2)

            attention("g2p", HEADS)
            act.wait_ge(*E("g2p_scores", 8 * 2 * NT))
            act.dma_start(att[:, :, 0:D], att_in[2:4, 0:D].unsqueeze(0).to_broadcast([TN, 2, D])
                          ).then_inc(S("g2q_att_full"), 16)
            for i in range(2 * NT):
                n, c = i % NT, i // NT
                await_group(act, "g2b", i)
                act.activation(h2[:, n, c * 384:(c + 1) * 384], bank("g2b", i)[0:TN, 0:384], ACT.Copy
                               ).then_inc(S("g2_h2"), 1)
            rows_broadcast("g2q", 0, 1)
            attention("g2q", 1)
            act.wait_ge(*E("g2_bias_used", 1))
            act.dma_start(bias8[0:8, :], rows_in[8:16, :]).then_inc(S("f2_bias_full"), 16)
            act.wait_ge(*E("slots_squared", 1))
            act.activation(slot_sum[:], slot_sum[:], ACT.Sqrt).then_inc(S("slots_norm"), 1)
            root_of_variance("f2")
            act.wait_ge(*E("f2_squared", NT))
            act.activation(sum8[0:TN], sum8[0:TN], ACT.Sqrt).then_inc(S("f2_norm"), 1)
            xT_high("f2_xT", KD)
            act.wait_ge(*E("f2_rows_shifted", 1))
            act.activation(combine[:], combine[:], ACT.Exp).then_inc(S("f2_row_exp"), 1)
            act.wait_ge(*E("f2_column_peak", 1))
            await_group(act, "f2_logits", 0)
            act.activation(logitsT[:, 0:NODES], logitsT[:, 0:NODES], ACT.Exp, bias=row_peak[:],
                           accum_out=row_sum[:]).then_inc(S("f2_column_exp"), 1)
            act.wait_ge(*E("f2_hidden_read", 1))
            act.wait_ge(*E("f2_diag_clear", 1))
            act.activation(hidden_diag[:].rearrange("p (e s) -> p e s", s=36)[:, :, 0:4], slot_hidden[:], ACT.Gelu
                           ).then_inc(S("f2_diag"), 1)
            act.wait_ge(*E("f2_up_read", 2))
            fill_bias("g3a_bias_full", 4, D1)
            act.dma_start(node_type_i[:], types_in.to_broadcast([RELS, NODES])).then_inc(S("types_loaded"), 16)
            act.dma_start(emb[:], emb_in).then_inc(S("emb_loaded"), 16)
            root_of_variance("g3")
            for r in range(RELS - 1):
                for span in range(SPANS):
                    counts(f"R{r}", rel[:, r], span)
                second_half(f"R{r}", rel[:, r])
            for key, k, full, prev in (("g3a", K1, "g3_emb_low", None), ("g3b", K1, "g3b_nodes", "g3a"),
                                       ("g3c", KD, "g3c_nodes", "g3b")):
                nodes_high(full, k * P, acc, key + "_nodes_high")
                xT_high(key + "_hT", k)
                for r in range(RELS):
                    messages_high(key, f"{key}_agg{r}", k)
                if key == "g3a":
                    act.wait_ge(*E("g3a_acc", 2 * NT))
                    fill_bias("g3b_bias_full", 5, D)
                elif key == "g3b":
                    act.wait_ge(*E("g3b_acc", 2 * NT))
                    fill_bias("g3c_bias_full", 6, D)
            act.wait_ge(*E("f3_rows_clear", 1))
            fill_pairs("f3_bias_full", 16)
            expert_layer("f3", 12, ACT.Gelu_apprx_tanh, True)

        @block.vector
        def _(dve):
            done = [0]

            def link(ins):
                done[0] += 1
                ins.then_inc(S("dve_step"), 1)
                dve.wait_ge(*E("dve_step", done[0]))

            TT, TS, STT = dve.tensor_tensor, dve.tensor_scalar, dve.scalar_tensor_tensor

            def node_stats(n, c):
                return dve.bn_stats(stats[0:TN, 12 * n + 6 * c:12 * n + 6 * c + 6], x[:, n, c * 384:(c + 1) * 384])

            def layer_norm(s, dst, measured=False):
                if not measured:
                    for n in range(NT):
                        for c in range(2):
                            last = node_stats(n, c)
                    link(last)
                for n in range(NT):
                    last = dve.bn_aggr(moments[0:TN, 2 * n:2 * n + 2], stats[0:TN, 12 * n:12 * n + 12])
                link(last)
                TS(rstd[0:TN], moments[0:TN].rearrange("p (n k) -> p n k", k=2)[:, :, 1], LN_EPS, None, ALU.add
                   ).then_inc(S(s + "_var"), 1)
                dve.wait_ge(*E(s + "_std", 1))
                link(dve.reciprocal(rstd[0:TN], rstd[0:TN]))
                for n in range(NT):
                    TS(dst(n), x[:, n], moments[0:TN, 2 * n:2 * n + 1], rstd[0:TN, n:n + 1], ALU.subtract, ALU.mult
                       ).then_inc(S(s + "_xn"), 1)

            def add_bias(s, n_cols=D):
                for n in range(NT):
                    last = TT(x[:, n], x[:, n], bias[:, 0:D], ALU.add)
                last.then_inc(S(s + "_bias_used"), 1)
                dve.wait_ge(*E(s + "_bias_used", 1))

            def clear_pad(name):
                dve.memset(f(xT_hi[:, :, NODES:NP]), 0.0).then_inc(S(name), 1)
                dve.memset(f(xT_lo[:, :, NODES:NP]), 0.0).then_inc(S(name), 1)

            def xT_low_half(label, k):
                clear_pad(label + "_pad")
                for i in range(2 * NT):
                    n, (a, b) = i // 2, ((0, 4), (4, k))[i % 2]
                    at = slice(n * TN, (n + 1) * TN)
                    dve.wait_ge(*E(label + "_high", i + 1))
                    TT(xT_lo[:, a:b, at], bank(label, i)[:, 0:(b - a) * TN].rearrange("p (k n) -> p k n", n=TN),
                       f(xT_hi[:, a:b, at]), ALU.subtract).then_inc(S(label + "_low"), 1)

            def nodes_low(width, src, high, low):
                for n in range(NT):
                    dve.wait_ge(*E(high, n + 1))
                    TT(nm_lo[:, n, 0:width], src[:, n, 0:width], f(nm_hi[:, n, 0:width]), ALU.subtract
                       ).then_inc(S(low), 1)

            def one_hots(sweeps):
                link(TS(dst_adds[:], edge[:, 1], float(HALF), None, ALU.is_ge))
                TS(dst_place[:], dst_adds[:], -float(HALF), None, ALU.mult).then_inc(S("dst_split"), 1)
                dve.wait_ge(*E("dst_split", 3 * (sweeps[0][0] != "A") + 1))
                TT(dst_place[:], dst_place[:], edge[:, 1], ALU.add).then_inc(S("dst_split"), 1)
                TS(dst_adds[:], dst_adds[:], FRACTION - 1.0, 1.0, ALU.mult, ALU.add).then_inc(S("dst_split"), 1)
                dve.wait_ge(*E("dst_split", 3 * (sweeps[0][0] != "A") + 3))

                def hot(label, source, t, k):
                    TS(src_hot[:, k], iota[:, 0:NODES], source[:, bass.ds(t, 1)], None, ALU.is_equal
                       ).then_inc(S(label + "_hot"), 1)
                    TS(dst_hot[:, k], iota[:, 0:HALF + 1], dst_place[:, bass.ds(t, 1)], dst_adds[:, bass.ds(t, 1)],
                       ALU.is_equal, ALU.mult).then_inc(S(label + "_hot"), 1)

                def settle(label, target, span):
                    for s in range(NT):
                        i = span * NT + s
                        dve.wait_ge(*E(label + "_rounded", i + 1))
                        if span and (i >= NT + 4 or label == "R1"):
                            dve.wait_ge(*E(label + "_fraction_added", max(0, min(i - NT - 3, (SPANS - 2) * NT))))
                            if i - 4 >= (SPANS - 1) * NT:
                                dve.wait_ge(*E(label + "_fraction_summed", i - 3 - (SPANS - 1) * NT))
                        dst = fraction_parts[:, i % 4] if span else target[:, s, HALF:NP]
                        STT(dst, rounded[:, i % 2], -ROUNDER, bank(label, i)[0:TN, 0:HALF],
                            ALU.add, ALU.subtract).then_inc(S(label + "_counted"), 1)
                        if span == SPANS - 1:
                            dve.wait_ge(*E(label + "_counted", i + 1))
                            TT(target[:, s, HALF:NP], f(target[:, s, HALF:NP]), dst, ALU.add
                               ).then_inc(S(label + "_fraction_summed"), 1)

                spans = [(label, source, target, span) for label, source, target in sweeps for span in range(SPANS)]
                for n, (label, source, target, span) in enumerate(spans):
                    first, used = span * SPAN, span * (SPAN - 1)
                    for t in range(OSLOTS):
                        if n:
                            before, last = spans[n - 1][0], spans[n - 1][3]
                            if t < OSLOTS - 1:
                                dve.wait_ge(*E(before + "_hot_used", last * (SPAN - 1) + SPAN - OSLOTS + t + 1))
                            else:
                                await_group(dve, before, last * NT + NT - 1)
                        hot(label, source, first + t, t)
                    if n:
                        before, _, its_target, last = spans[n - 1]
                        settle(before, its_target, last)
                    with dve.Fori(1, SPAN // OSLOTS) as q:
                        for k in range(OSLOTS):
                            dve.wait_ge(*E(label + "_hot_used", q * OSLOTS + (k - OSLOTS + 1 + used)))
                            hot(label, source, q * OSLOTS + (first + k), k)
                label, _, target, span = spans[-1]
                settle(label, target, span)

            def messages_low(key, label, k, first=0):
                for i in range(2 * k):
                    ft, (c0, cn) = i // 2, CH[i % 2]
                    dve.wait_ge(*E(key + "_high", first + i + 1))
                    TT(xT_lo[:, ft, c0:c0 + cn], bank(label, i)[:, 0:cn], f(xT_hi[:, ft, c0:c0 + cn]), ALU.subtract
                       ).then_inc(S(key + "_low"), 1)

            def add_to_nodes(s, label, factor=None, between=None):
                for i in range(2 * NT):
                    n, c = i % NT, i // NT
                    at = slice(c * 384, (c + 1) * 384)
                    await_group(dve, label, i)
                    if factor is None:
                        TT(x[:, n, at], bank(label, i)[0:TN, 0:384], x[:, n, at], ALU.add).then_inc(S(s + "_x"), 1)
                    else:
                        STT(x[:, n, at], bank(label, i)[0:TN, 0:384], factor[0:TN, n:n + 1], x[:, n, at],
                            ALU.mult, ALU.add).then_inc(S(s + "_x"), 1)
                    if i == NT - 1:
                        if between:
                            between()
                        if s != "f3":
                            dve.wait_ge(*E(s + "_x", NT))
                            for m in range(NT):
                                node_stats(m, 0)
                    if c and s != "f3":
                        if n:
                            dve.wait_ge(*E(s + "_x", i))
                            node_stats(n - 1, 1)
                        if n == NT - 1:
                            dve.wait_ge(*E(s + "_x", i + 1))
                            link(node_stats(n, 1))

            def hidden_low(s, tiles, weigh):
                jobs = 2 * tiles
                for j in range(jobs + 1):
                    if j < jobs and weigh:
                        cn = CH[j % 2][1]
                        dve.wait_ge(*E(s + "_activated", j + 1))
                        await_group(dve, s + "_cB", j)
                        TT(tmp[:, j % TSLOTS, 0:cn], tmp[:, j % TSLOTS, 0:cn], bank(s + "_cB", j)[:, 0:cn], ALU.mult
                           ).then_inc(S(s + "_weighted"), 1)
                    if j >= 1:
                        i = j - 1
                        c0, cn = CH[i % 2]
                        dve.wait_ge(*E(s + "_high", i + 1))
                        TT(hT_lo[:, i // 2, c0:c0 + cn], tmp[:, i % TSLOTS, 0:cn], f(hT_hi[:, i // 2, c0:c0 + cn]),
                           ALU.subtract).then_inc(S(s + "_low"), 1)

            def bc(cols8, n=NT):
                return cols8.unsqueeze(2).to_broadcast([TN, n, 8])

            def v8(t):
                return t[0:TN].rearrange("p (n e) -> p n e", e=8)

            def route(s):
                await_group(dve, s + "_router", 0)
                dve.tensor_copy(logit8[0:TN], bank(s + "_router", 0)[0:TN, 0:8 * NT]).then_inc(S(s + "_routed"), 1)
                dve.wait_ge(*E(s + "_routed", 1))
                for n in range(NT):
                    last = dve.max(top8[0:TN, 8 * n:8 * n + 8], logit8[0:TN, 8 * n:8 * n + 8])
                link(last)
                TT(v8(prob8), v8(logit8), v8(top8)[:, :, 0:1].to_broadcast([TN, NT, 8]), ALU.subtract
                   ).then_inc(S(s + "_shifted"), 1)
                for n in range(NT):
                    last = dve.max_index(idx8[0:TN, 8 * n:8 * n + 8], top8[0:TN, 8 * n:8 * n + 8],
                                         logit8[0:TN, 8 * n:8 * n + 8])
                link(last)
                link(dve.tensor_copy(idx8f[0:TN], idx8[0:TN, 0:NT * 8]))
                experts = iota8[0:TN].unsqueeze(1).to_broadcast([TN, NT, 8])
                TT(v8(hot8), experts, v8(idx8f)[:, :, 0:1].to_broadcast([TN, NT, 8]), ALU.is_equal)
                link(TT(v8(logit8), experts, v8(idx8f)[:, :, 1:2].to_broadcast([TN, NT, 8]), ALU.is_equal))
                link(TT(hot8[0:TN], hot8[0:TN], logit8[0:TN], ALU.add))
                dve.wait_ge(*E(s + "_exp", 1))
                link(dve.tensor_reduce(sum8[0:TN], v8(prob8), AX.X, ALU.add))
                link(dve.reciprocal(sum8[0:TN], sum8[0:TN]))
                TT(v8(prob8), v8(prob8), bc(sum8[0:TN]), ALU.mult).then_inc(S(s + "_probs"), 1)
                dve.wait_ge(*E(s + "_probs", 1))
                link(TT(hot8[0:TN], hot8[0:TN], prob8[0:TN], ALU.mult))
                if s == "f1":
                    await_group(dve, "f1_importance", 0)
                    TS(run8[0:TN], bank("f1_importance", 0)[0:TN, 0:8], 1.0, 1.0 - 0.9, ALU.subtract, ALU.mult
                       ).then_inc(S("f1_importance_read"), 1)
                    dve.wait_ge(*E("f1_importance_read", 1))
                    link(TS(run8[0:TN], run8[0:TN], 1.0, 0.01, ALU.add, ALU.add))
                    link(dve.reciprocal(run8[0:TN], run8[0:TN]))
                    link(TT(v8(hot8), v8(hot8), run8[0:TN].unsqueeze(1).to_broadcast([TN, NT, 8]), ALU.mult))
                link(dve.tensor_reduce(sum8[0:TN], v8(hot8), AX.X, ALU.add))
                if s != "f1":
                    link(TS(sum8[0:TN], sum8[0:TN], 1e-9, None, ALU.add))
                link(dve.reciprocal(sum8[0:TN], sum8[0:TN]))
                link(TT(hot8[0:TN].rearrange("p (n e) -> p n e", e=8), v8(hot8), bc(sum8[0:TN]), ALU.mult))
                dve.wait_ge(*E(s + "_cpad_clear", 1))
                dve.tensor_copy(cpad[:].rearrange("p n (q s) -> p n q s", s=32)[:, :, :, 0:2],
                                hot8[0:TN].rearrange("p (n q s) -> p n q s", q=4, s=2)).then_inc(S(s + "_combine"), 1)
                if s != "f1":
                    dve.wait_ge(*E(s + "_bias_full", 64))
                    dve.tensor_copy(bias8_hi[:], bias8[:]).then_inc(S(s + "_rows_split"), 1)
                for n in range(NT):
                    at = slice(n * TN, (n + 1) * TN)
                    await_group(dve, s + "_cT", n)
                    dve.tensor_copy(cT_hi[:, at], bank(s + "_cT", n)[:, 0:TN]).then_inc(S(s + "_cT_high"), 1)
                for n in range(NT):
                    at = slice(n * TN, (n + 1) * TN)
                    dve.wait_ge(*E(s + "_cT_high", n + 1))
                    TT(cT_lo[:, at], bank(s + "_cT", n)[:, 0:TN], f(cT_hi[:, at]), ALU.subtract
                       ).then_inc(S(s + "_combineT"), 1)
                if s != "f1":
                    dve.wait_ge(*E(s + "_rows_split", 1))
                    TT(bias8_lo[:], bias8[:], f(bias8_hi[:]), ALU.subtract).then_inc(S(s + "_rows_split"), 1)

            def expert_layer(s, tiles, measured=True):
                layer_norm(s, lambda n: xn[:, n], measured)
                dve.memset(cpad[:], 0.0).then_inc(S(s + "_cpad_clear"), 1)
                dve.memset(f(cT_hi[:, NODES:NP]), 0.0).then_inc(S(s + "_cT_pad"), 1)
                dve.memset(f(cT_lo[:, NODES:NP]), 0.0).then_inc(S(s + "_cT_pad"), 1)
                xT_low_half(s + "_xT", KD)
                route(s)
                hidden_low(s, tiles, True)
                add_to_nodes(s, s + "_down")

            dve.wait_ge(*E("consts", 21))
            dve.tensor_copy(iota8, idx8[:, 0:8])
            dve.tensor_copy(rel_index, idx8[:, 8:9])
            dve.memset(tiny, 1e-30)
            dve.memset(rounder, ROUNDER)
            dve.memset(unrounder, -ROUNDER)
            dve.wait_ge(*E("cols_loaded", 16))
            TS(bn_s, col("bn_var"), 1e-5, None, ALU.add).then_inc(S("bn_var"), 1)
            dve.wait_ge(*E("edges_loaded", 16))
            link(dve.tensor_copy(edge[:], e_int[:]))
            dve.wait_ge(*E("gates_high", 1))
            TT(gate_lo[:], cols[:, COLS["f0_gate"][0]:COLS["f3_gate"][1]], f(gate_hi[:]), ALU.subtract
               ).then_inc(S("gates_split"), 1)
            dve.wait_ge(*E("bn_std", 1))
            link(dve.reciprocal(bn_s, bn_s))
            TT(bn_b, col("bn_b1"), col("bn_mean"), ALU.subtract)
            link(TT(bn_s, bn_s, col("bn_gamma"), ALU.mult))
            link(TT(bn_b, bn_b, bn_s, ALU.mult))
            TT(bn_b, bn_b, col("bn_beta"), ALU.add).then_inc(S("bn_ready"), 1)

            dve.wait_ge(*E("x_loaded", 16))
            dve.wait_ge(*E("scalars_loaded", 32))
            layer_norm("g0", lambda n: xn[:, n])
            for n in range(NT):
                dve.wait_ge(*E("g0_xn", n + 1))
                TS(msg[:, n], xn[:, n], 0.0, 1e-7, ALU.max, ALU.add).then_inc(S("g0_msg"), 1)
            for n in range(NT):
                dve.wait_ge(*E("g0_msg", n + 1))
                if n:
                    dve.wait_ge(*E("g0_logits", n))
                dve.tensor_scalar(g0_junk[:], msg[:, n], t_col[0:TN], None, ALU.mult).then_inc(S("g0_logits"), 1)
                dve.wait_ge(*E("g0_logits", n + 1))
                link(dve.tensor_reduce(peak[0:TN, n:n + 1], g0_junk[:], AX.X, ALU.max))
            dve.tensor_reduce(peak[0:TN, 5:6], peak[0:TN, 0:NT], AX.X, ALU.max).then_inc(S("g0_peak"), 1)
            await_group(dve, "g0_maxT", 0)
            dve.tensor_reduce(peak_all[0:1, 0:1], bank("g0_maxT", 0)[0:1, 0:TN], AX.X, ALU.max
                              ).then_inc(S("g0_max_read"), 1)
            await_group(dve, "g0_maxB", 0)
            TS(peak_all[0:TN, 1:2], bank("g0_maxB", 0)[0:TN, 0:1], -1.0, None, ALU.mult
               ).then_inc(S("g0_maxB_read"), 1)
            one_hots([("A", edge[:, 0], adj)])
            await_group(dve, "A", SPANS * NT - 1)
            dve.memset(f(xT_hi[:, :, NODES:NP]), 0.0).then_inc(S("g0_xT_pad"), 1)
            dve.wait_ge(*E("g0_num_low", NT))
            dve.memset(xT_full[:, :, NODES:NP], 0.0).then_inc(S("g0_xT_pad"), 1)
            dve.wait_ge(*E("g0_xT_pad", 2))
            dve.wait_ge(*E("g0_xT_copied", 2 * NT))
            for j in range(2 * KD + 1):
                if j < 2 * KD:
                    (c0, cn), ft = CH[j % 2], j // 2
                    at, T, R = slice(c0, c0 + cn), tmp[:, j % 2, 0:cn], tmp[:, 2 + j % 2, 0:cn]
                    dve.wait_ge(*E("g0_den_read", j + 1))
                    link(dve.reciprocal(R, R))
                    TT(T, bank("g0_num", j)[:, 0:cn], R, ALU.mult).then_inc(S("g0_num_read"), 1)
                    dve.wait_ge(*E("g0_num_read", j + 1))
                    TT(T, T, xT_full[:, ft, at], ALU.add).then_inc(S("g0_sum"), 1)
                if j >= 1:
                    i = j - 1
                    (c0, cn), ft = CH[i % 2], i // 2
                    dve.wait_ge(*E("g0_out_high", i + 1))
                    TT(xT_lo[:, ft, c0:c0 + cn], tmp[:, i % 2, 0:cn], f(xT_hi[:, ft, c0:c0 + cn]), ALU.subtract
                       ).then_inc(S("g0_out_low"), 1)
            await_group(dve, "g1_deg", 0)
            TS(dinv[0:TN], bank("g1_deg", 0)[0:TN, 0:2 * NT].rearrange("p (n k) -> p n k", k=2)[:, :, 0], 1.0, None,
               ALU.add).then_inc(S("g1_deg_read"), 1)
            dve.wait_ge(*E("g1_deg_read", 1))
            dve.reciprocal(dinv[0:TN], dinv[0:TN]).then_inc(S("g1_deg_ready"), 1)
            for s in range(NT):
                at = slice(s * TN, (s + 1) * TN)
                TT(adj[:, s, at], f(adj[:, s, at]), ident[0:TN, 0:TN], ALU.add).then_inc(S("self_loops"), 1)
            dve.wait_ge(*E("g0_residual", 2 * NT))
            dve.memset(bias8[:], 0.0).then_inc(S("f0_rows_clear"), 1)
            hidden_low("g0", 12, False)
            add_to_nodes("g0", "g0d")
            expert_layer("f0", 12)

            layer_norm("g1", lambda n: xn[:, n], True)
            dve.wait_ge(*E("g1_dinv", 1))
            for n in range(NT):
                dve.wait_ge(*E("g1_xn", n + 1))
                TS(xn[:, n], xn[:, n], dinv[0:TN, n:n + 1], None, ALU.mult).then_inc(S("g1_scaled_nodes"), 1)
            nodes_low(D, xn, "g1_nodes_high", "g1_nodes_low")
            dve.wait_ge(*E("g1_bias_full", 16))
            add_bias("g1")
            messages_low("g1a", "g1a_agg", KD)
            dve.wait_ge(*E("g1b_bias_full", 16))
            for i in range(2 * NT + 1):
                if i < 2 * NT:
                    n, c = i % NT, i // NT
                    at = slice(c * 384, (c + 1) * 384)
                    await_group(dve, "g1a", i)
                    STT(xn[:, n, at], bank("g1a", i)[0:TN, 0:384], dinv[0:TN, n:n + 1], bias[:, at],
                        ALU.mult, ALU.add).then_inc(S("g1a_read"), 1)
                    dve.wait_ge(*E("g1a_read", i + 1))
                    TS(xn[:, n, at], xn[:, n, at], 0.0, dinv[0:TN, n:n + 1], ALU.max, ALU.mult
                       ).then_inc(S("g1a_full"), 1)
                if i >= 1:
                    n, c = (i - 1) % NT, (i - 1) // NT
                    at = slice(c * 384, (c + 1) * 384)
                    dve.wait_ge(*E("g1b_nodes_high", i))
                    TT(nm_lo[:, n, at], xn[:, n, at], f(nm_hi[:, n, at]), ALU.subtract).then_inc(S("g1b_nodes_low"), 1)
            messages_low("g1b", "g1b_agg", KD)
            await_group(dve, "g1b_agg", 2 * KD - 1)
            for s in range(NT):
                at = slice(s * TN, (s + 1) * TN)
                TT(adj[:, s, at], f(adj[:, s, at]), ident[0:TN, 0:TN], ALU.subtract).then_inc(S("no_self_loops"), 1)
            dve.memset(maskT[:, :, NODES:NP], FAR)

            def edge_mask():
                for i in range(2 * NT):
                    d, (a, b) = i // 2, ((0, 4), (4, NT))[i % 2]
                    await_group(dve, "g2_maskT", i)
                    TS(maskT[:, d, a * TN:b * TN], bank("g2_maskT", i)[0:TN, 0:(b - a) * TN], 0.0, FAR,
                       ALU.is_equal, ALU.mult).then_inc(S("g2_masked"), 1)

            add_to_nodes("g1", "g1b", dinv, edge_mask)
            expert_layer("f1", 8)

            layer_norm("g2", lambda n: xn[:, n], True)
            dve.tensor_copy(head_sel[:], ident[0:8, 0:8].unsqueeze(2).to_broadcast([8, 8, P])).then_inc(S("head_sel"), 1)
            dve.memset(asT[:, NODES:NP], 0.0).then_inc(S("asT_pad"), 1)
            dve.memset(h1[:, :, :, HEAD_DIM:HD], 1.0).then_inc(S("h1_ones"), 1)
            xT_low_half("g2_xT", KD)
            dve.wait_ge(*E("g2_bias_full", 16))
            add_bias("g2")
            dve.wait_ge(*E("g2_masked", 2 * NT))
            link(dve.tensor_reduce(no_edge[0:TN], maskT[:], AX.X, ALU.max))
            dve.wait_ge(*E("g2p_att_full", 16))

            def greatest_scores(layer, h):
                dve.wait_ge(*E(layer + "_asB_read", 2 * h + 2))
                for d in range(NT):
                    made = NT * h + d
                    if made >= 2:
                        dve.wait_ge(*E(layer + "_max_done", made - 1))
                    dve.tensor_tensor_reduce(edge_scores[made % 2][:], asB[:, h % 2], maskT[:, d], 1.0, -3e38,
                                             ALU.add, ALU.max, a_max[0:TN, 8 * d + h:8 * d + h + 1]
                                             ).then_inc(S(layer + "_max_done"), 1)

            def read_source_rows(layer, c):
                for i, (a, b) in enumerate(((0, 4), (4, NT))):
                    await_group(dve, layer + "_asT", 2 * c + i)
                    dve.tensor_copy(asT[:, a * TN:b * TN], bank(layer + "_asT", 2 * c + i)[0:2, 0:(b - a) * TN]
                                    ).then_inc(S(layer + "_asT_read"), 1)

            for c in range(4):
                for n in range(NT):
                    i = c * NT + n
                    dve.wait_ge(*E("g2_h1", i + 1))
                    for h in (2 * c, 2 * c + 1):
                        for kind, dst in ((0, a_src), (1, a_dst)):
                            made = 4 * i + 2 * (h % 2) + kind
                            if made >= 4:
                                dve.wait_ge(*E("g2p_scores", made - 3))
                            dve.tensor_tensor_reduce(
                                junk[:, kind * 256 + (h % 2) * 128:kind * 256 + (h % 2) * 128 + 128],
                                h1[:, n, h, 0:HEAD_DIM], att[:, kind, h * HEAD_DIM:(h + 1) * HEAD_DIM], 1.0, 0.0,
                                ALU.mult, ALU.add, dst[0:TN, 8 * n + h:8 * n + h + 1]).then_inc(S("g2p_scores"), 1)
                read_source_rows("g2p", c)
                if c:
                    for h in (2 * c - 2, 2 * c - 1):
                        greatest_scores("g2p", h)
            for h in (HEADS - 2, HEADS - 1):
                greatest_scores("g2p", h)
            dve.wait_ge(*E("g2p_scores", 8 * 2 * NT))

            def attention(layer, heads):
                dve.memset(uT[:, NODES:NP], 0.0).then_inc(S(layer + "_pads"), 1)
                dve.memset(vT[:, NODES:NP], 0.0).then_inc(S(layer + "_pads"), 1)
                TS(a_src5[0:TN], a_src[0:TN], 0.2, None, ALU.mult)
                dve.wait_ge(*E(layer + "_max_done", NT * heads))
                link(TT(v8(a_max), v8(a_max), bc(no_edge[0:TN]), ALU.subtract))
                link(TT(a_max[0:TN], a_max[0:TN], a_dst[0:TN], ALU.add))
                link(STT(hot8[0:TN], a_max[0:TN], 0.2, a_max[0:TN], ALU.mult, ALU.max))
                TT(uv[:, 0].rearrange("p n e -> p (n e)"), a_dst[0:TN], hot8[0:TN], ALU.subtract
                   ).then_inc(S(layer + "_uv"), 1)
                STT(uv[:, 1].rearrange("p n e -> p (n e)"), a_dst[0:TN], 0.2, hot8[0:TN], ALU.mult, ALU.subtract
                    ).then_inc(S(layer + "_uv"), 1)
                for i in range(4):
                    dst, (a, b) = (uT, vT)[i // 2], ((0, 4), (4, NT))[i % 2]
                    await_group(dve, layer + "_uvT", i)
                    dve.tensor_copy(dst[:, a * TN:b * TN], bank(layer + "_uvT", i)[0:8, 0:(b - a) * TN]
                                    ).then_inc(S(layer + "_uvT_read"), 1)

                def head_mean(h):
                    total = prob8[0:TN, NT * h:NT * h + NT]
                    for n in range(NT):
                        i = NT * h + n
                        await_group(dve, "g2p_agg", i)
                        TS(total[:, n:n + 1], bank("g2p_agg", i)[0:TN, HEAD_DIM:HEAD_DIM + 1], 1e-16, None, ALU.add
                           ).then_inc(S("g2p_sum"), 1)
                    dve.wait_ge(*E("g2p_sum", NT * (h + 1)))
                    link(dve.reciprocal(total, total))
                    if h >= 2:
                        await_group(dve, "g2p_outT", 2 * (h - 2) + 1)
                    for n in range(NT):
                        i = NT * h + n
                        TS(mean[:, h % 2, n], bank("g2p_agg", i)[0:TN, 0:HEAD_DIM], total[:, n:n + 1], None, ALU.mult
                           ).then_inc(S("g2p_mean"), 1)

                def head_low(h):
                    dve.wait_ge(*E("g2p_high", h + 1))
                    TT(hT_lo[:, h, 0:NODES], head_T[:], f(hT_hi[:, h, 0:NODES]), ALU.subtract).then_inc(S("g2p_low"), 1)

                for h in range(heads + 2):
                    if 1 <= h <= heads:
                        pr = prob[(h - 1) % 2]
                        dve.wait_ge(*E(layer + "_powers", h))
                        STT(pr[:].rearrange("p n j -> p (n j)"), pr[:].rearrange("p n j -> p (n j)"), 3.0,
                            f(adj[:]).rearrange("p n j -> p (n j)"), ALU.min, ALU.mult).then_inc(S(layer + "_prob"), 1)
                    if h < heads:
                        pr = prob[h % 2]
                        for s in range(NT):
                            dve.wait_ge(*E(layer + "_shift", NT * h + s + 1))
                            STT(pr[:, s], uB[h % 2][:, 1], a_src5[0:TN, 8 * s + h:8 * s + h + 1], pr[:, s],
                                ALU.add, ALU.max).then_inc(S(layer + "_leaky"), 1)
                    if layer == "g2p" and 1 <= h <= heads:
                        head_mean(h - 1)
                    if layer == "g2p" and h >= 2:
                        head_low(h - 2)

            attention("g2p", HEADS)
            dve.wait_ge(*E("g2q_att_full", 16))
            dve.memset(a_src[0:TN], 0.0)
            link(dve.memset(a_dst[0:TN], 0.0))
            for i in range(2 * NT):
                n, c = i % NT, i // NT
                at = slice(c * 384, (c + 1) * 384)
                dve.wait_ge(*E("g2_h2", i + 1))
                for kind in range(2):
                    if i:
                        dve.wait_ge(*E("h2_scores", 2 * i + kind - 1))
                    dve.tensor_tensor_reduce(junk[:, kind * 384:kind * 384 + 384], h2[:, n, at],
                                                    att[:, kind, at], 1.0, 0.0, ALU.mult, ALU.add,
                                                    a_part[0:TN, (c * 2 + kind) * NT + n:(c * 2 + kind) * NT + n + 1]
                                             ).then_inc(S("h2_scores"), 1)
            dve.wait_ge(*E("h2_scores", 4 * NT))
            dve.memset(h2[:, :, D:D + 2], 1.0).then_inc(S("h2_ones"), 1)
            for kind, dst in ((0, a_src), (1, a_dst)):
                last = TT(v8(dst)[:, :, 0], a_part[0:TN, kind * NT:(kind + 1) * NT],
                          a_part[0:TN, (2 + kind) * NT:(3 + kind) * NT], ALU.add)
                last.then_inc(S("g2q_scores"), 1)
            dve.wait_ge(*E("g2q_scores", 2))
            read_source_rows("g2q", 0)
            greatest_scores("g2q", 0)
            attention("g2q", 1)
            for n in range(NT):
                for i, at, cn in ((2 * n, slice(384, D), 384), (2 * n + 1, slice(0, 384), 384)):
                    await_group(dve, "g2q_agg", i)
                    if i % 2 == 0:
                        link(TS(sum8[0:TN, n:n + 1], bank("g2q_agg", i)[0:TN, 384:385], 1e-16, None, ALU.add))
                        link(dve.reciprocal(sum8[0:TN, n:n + 1], sum8[0:TN, n:n + 1]))
                    STT(x[:, n, at], bank("g2q_agg", i)[0:TN, 0:cn], sum8[0:TN, n:n + 1], x[:, n, at],
                        ALU.mult, ALU.add).then_inc(S("g2_x"), 1)
            dve.wait_ge(*E("g2_x", 2 * NT))

            def kp(t):
                return t.rearrange("d (k p) -> d k p", k=KD)

            slots = col("slots").rearrange("d (k n p) -> d k n p", k=KD, n=EXPERTS)
            link(TT(sp_tmp[:], col("slots").rearrange("d (k s) -> d k s", k=KD),
                    col("slots").rearrange("d (k s) -> d k s", k=KD), ALU.mult))
            dve.tensor_reduce(kp(slot_sum[:]), sp_tmp[:].rearrange("d k (n p) -> d k p n", n=EXPERTS), AX.X, ALU.add
                              ).then_inc(S("slots_squared"), 1)
            dve.wait_ge(*E("slots_norm", 1))
            link(TS(slot_sum[:], slot_sum[:], 1e-6, None, ALU.add))
            link(dve.reciprocal(slot_sum[:], slot_sum[:]))
            for n in range(EXPERTS):
                last = TT(sp_tmp[:].rearrange("d k (n p) -> d k n p", n=EXPERTS)[:, :, n], slots[:, :, n],
                          kp(slot_sum[:]), ALU.mult)
            link(last)
            link(TS(sp_tmp[:], sp_tmp[:], slot_scale, None, ALU.mult))
            link(dve.tensor_copy(sp_hi[:], sp_tmp[:]))
            TT(sp_lo[:], sp_tmp[:], f(sp_hi[:]), ALU.subtract).then_inc(S("slots_split"), 1)
            clear_pad("f2_xT_pad")
            layer_norm("f2", lambda n: xn[:, n])
            dve.wait_ge(*E("f2_xn", NT))
            for n in range(NT):
                if n:
                    dve.wait_ge(*E("f2_squared", n))
                dve.tensor_tensor_reduce(f2_junk[:], xn[:, n], xn[:, n], 1.0, 0.0, ALU.mult, ALU.add,
                                         sum8[0:TN, n:n + 1]).then_inc(S("f2_squared"), 1)
            dve.wait_ge(*E("f2_norm", 1))
            link(TS(sum8[0:TN], sum8[0:TN], 1e-6, None, ALU.add))
            link(dve.reciprocal(sum8[0:TN], sum8[0:TN]))
            for n in range(NT):
                TS(xn[:, n], xn[:, n], sum8[0:TN, n:n + 1], None, ALU.mult).then_inc(S("f2_unit"), 1)
            for i in range(2 * NT):
                n, (a, b) = i // 2, ((0, 4), (4, KD))[i % 2]
                at = slice(n * TN, (n + 1) * TN)
                dve.wait_ge(*E("f2_xT_high", i + 1))
                TT(xT_lo[:, a:b, at], bank("f2_xT", i)[:, 0:(b - a) * TN].rearrange("p (k n) -> p k n", n=TN),
                   f(xT_hi[:, a:b, at]), ALU.subtract).then_inc(S("f2_xT_low"), 1)
            for c, (c0, cn) in enumerate(CH):
                await_group(dve, "f2_logitsT", c)
                dve.tensor_copy(logitsT[:, c0:c0 + cn], bank("f2_logitsT", c)[0:SLOTS, 0:cn]
                                ).then_inc(S("f2_logitsT_read"), 1)
            dve.wait_ge(*E("f2_logitsT_read", 2))
            dve.tensor_reduce(row_peak[:], logitsT[:, 0:NODES], AX.X, ALU.max, negate=True
                              ).then_inc(S("f2_column_peak"), 1)
            await_group(dve, "f2_logits", 0)
            dve.tensor_copy(slot_logits[:].rearrange("p n s -> p (n s)"), bank("f2_logits", 0)[0:TN, 0:NT * SLOTS]
                            ).then_inc(S("f2_logits_read"), 1)
            dve.wait_ge(*E("f2_logits_read", 1))
            link(dve.tensor_reduce(col_peak[:], slot_logits[:], AX.X, ALU.max))
            TT(combine[:], slot_logits[:], col_peak[:].unsqueeze(2).to_broadcast([TN, NT, SLOTS]), ALU.subtract
               ).then_inc(S("f2_rows_shifted"), 1)
            dve.wait_ge(*E("f2_row_exp", 1))
            link(dve.tensor_reduce(col_sum[:], combine[:], AX.X, ALU.add))
            link(dve.reciprocal(col_sum[:], col_sum[:]))
            TT(combine[:], combine[:], col_sum[:].unsqueeze(2).to_broadcast([TN, NT, SLOTS]), ALU.mult
               ).then_inc(S("f2_combine"), 1)
            dve.wait_ge(*E("f2_column_exp", 1))
            link(dve.reciprocal(row_sum[:], row_sum[:]))
            TS(logitsT[:, 0:NODES], logitsT[:, 0:NODES], row_sum[:], None, ALU.mult).then_inc(S("f2_dispatchT"), 1)
            await_group(dve, "f2_dispatch", 0)
            dve.tensor_copy(dispatch[:].rearrange("p n s -> p (n s)"), bank("f2_dispatch", 0)[0:TN, 0:NT * SLOTS]
                            ).then_inc(S("f2_dispatch_read"), 1)
            for i, (a, b) in enumerate(((0, 4), (4, NT))):
                await_group(dve, "f2_combineT", i)
                dve.tensor_copy(combineT[:, a * TN:b * TN], bank("f2_combineT", i)[0:SLOTS, 0:(b - a) * TN]
                                ).then_inc(S("f2_combineT_read"), 1)
            await_group(dve, "f2_tilde", 0)
            dve.tensor_copy(tildeT[:].rearrange("p k s -> p (k s)"), bank("f2_tilde", 0)[:, 0:KD * SLOTS]
                            ).then_inc(S("f2_tilde_read"), 1)
            dve.memset(hidden_diag[:], 0.0).then_inc(S("f2_diag_clear"), 1)
            await_group(dve, "f2_hidden", 0)
            TT(slot_hidden[:], bank("f2_hidden", 0)[0:SLOT_H, 0:SLOTS].rearrange("p (e s) -> p e s", s=4),
               col("b_down")[0:SLOT_H].unsqueeze(2).to_broadcast([SLOT_H, 8, 4]), ALU.add
               ).then_inc(S("f2_hidden_read"), 1)
            for c in range(2):
                await_group(dve, "f2_up", c)
                dve.tensor_copy(slot_out[:, c * 384:(c + 1) * 384], bank("f2_up", c)[0:SLOTS, 0:384]
                                ).then_inc(S("f2_up_read"), 1)
            add_to_nodes("f2", "f2_down")

            layer_norm("g3", lambda n: acc[:, n, 0:D], True)
            dve.wait_ge(*E("types_loaded", 16))
            TS(type_hot[:], node_type_i[:], rel_index[0:RELS], None, ALU.is_equal).then_inc(S("type_hot"), 1)
            for n in range(NT):
                await_group(dve, "g3_emb", n)
                dve.tensor_copy(acc[:, n, D:D1], bank("g3_emb", n)[0:TN, 0:TYPE_DIM]).then_inc(S("g3_emb_low"), 1)
            link(dve.tensor_copy(types[:], edge[:, 2]))
            TS(src_plus[:], edge[:, 0], 1.0, None, ALU.add)
            for r in range(RELS - 1):
                last = TS(rel_source[:, r], types[:], float(r), None, ALU.is_equal)
            link(last)
            for r in range(RELS - 1):
                last = TT(rel_source[:, r], rel_source[:, r], src_plus[:], ALU.mult)
            link(last)
            for r in range(RELS - 1):
                last = TS(rel_source[:, r], rel_source[:, r], -1.0, None, ALU.add)
            link(last)
            one_hots([(f"R{r}", rel_source[:, r], rel[:, r]) for r in range(RELS - 1)])
            for s in range(NT):
                dve.wait_ge(*E("R0_whole_added", (SPANS - 1) * NT))
                dve.wait_ge(*E("R0_counts_ready", NT))
                TT(rel[:, 2, s], f(adj[:, s]), f(rel[:, 0, s]), ALU.subtract).then_inc(S("others"), 1)
            for s in range(NT):
                dve.wait_ge(*E("R1_whole_added", (SPANS - 1) * NT))
                dve.wait_ge(*E("R1_counts_ready", s + 1))
                dve.wait_ge(*E("others", s + 1))
                TT(rel[:, 2, s], f(rel[:, 2, s]), f(rel[:, 1, s]), ALU.subtract).then_inc(S("last_relation"), 1)
            nodes_low(D1, acc, "g3a_nodes_high", "g3a_nodes_low")
            for key, k, width in (("g3a", K1, 448), ("g3b", K1, 384), ("g3c", KD, 384)):
                clear_pad(key + "_hT_pad")
                for i in range(2 * NT):
                    n, (a, b) = i // 2, ((0, 4), (4, k))[i % 2]
                    at = slice(n * TN, (n + 1) * TN)
                    dve.wait_ge(*E(key + "_hT_high", i + 1))
                    TT(xT_lo[:, a:b, at], bank(key + "_hT", i)[:, 0:(b - a) * TN].rearrange("p (k n) -> p k n", n=TN),
                       f(xT_hi[:, a:b, at]), ALU.subtract).then_inc(S(key + "_hT_low"), 1)
                dve.wait_ge(*E(key + "_bias_full", 16))
                for i in range(2 * NT):
                    n, c = i % NT, i // NT
                    at = slice(c * width, (c + 1) * width)
                    await_group(dve, key + "_root", i)
                    TT(acc[:, n, at], bank(key + "_root", i)[0:TN, 0:width], bias[:, at], ALU.add
                       ).then_inc(S(key + "_acc"), 1)
                for r in range(RELS):
                    if key == "g3a":
                        inv = rel_inv[0:TN, r * NT:(r + 1) * NT]
                        await_group(dve, "g3_deg", r)
                        TS(inv, bank("g3_deg", r)[0:TN, 0:2 * NT].rearrange("p (n k) -> p n k", k=2)[:, :, 0], 1.0, None,
                           ALU.max).then_inc(S("g3_deg_read"), 1)
                        dve.wait_ge(*E("g3_deg_read", r + 1))
                        link(dve.reciprocal(inv, inv))
                    messages_low(key, f"{key}_agg{r}", k, 2 * k * r)
                    dve.wait_ge(*E(key + "_acc", 2 * NT * (r + 1)))
                    for i in range(2 * NT):
                        n, c = i % NT, i // NT
                        at = slice(c * width, (c + 1) * width)
                        await_group(dve, f"{key}_rel{r}", i)
                        STT(acc[:, n, at], bank(f"{key}_rel{r}", i)[0:TN, 0:width],
                            rel_inv[0:TN, r * NT + n:r * NT + n + 1], acc[:, n, at], ALU.mult, ALU.add
                            ).then_inc(S(key + "_acc"), 1)
                dve.wait_ge(*E(key + "_acc", 2 * NT * (RELS + 1)))
                if key != "g3c":
                    out_key, out_k = ("g3b", K1) if key == "g3a" else ("g3c", KD)
                    for n in range(NT):
                        TS(acc[:, n, 0:2 * width], acc[:, n, 0:2 * width], 0.0, None, ALU.max
                           ).then_inc(S(out_key + "_nodes"), 1)
                    nodes_low(2 * width, acc, out_key + "_nodes_high", out_key + "_nodes_low")
                else:
                    for n in range(NT):
                        STT(x[:, n], acc[:, n, 0:D], 0.0, x[:, n], ALU.max, ALU.add).then_inc(S("g3_x"), 1)
                    dve.wait_ge(*E("g3_x", NT))
            dve.memset(bias8[:], 0.0).then_inc(S("f3_rows_clear"), 1)
            expert_layer("f3", 12, False)

        @block.tensor
        def _(pe):
            def open_bank(label, i):
                g = WHERE[label, i]
                if g >= 8:
                    pe.wait_ge(*E(*GROUPS[g - 8]))
                return banks[g % 8]

            closed = [0]

            def close(ins, label, i):
                assert WHERE[label, i] == closed[0], (label, i)
                closed[0] += 1
                ins.then_inc(S("group_closed"), 1)

            def three(dst, l_hi, l_lo, r_hi, r_lo, start, stop):
                pe.matmul(dst, l_hi, r_hi, start=start, stop=False)
                pe.matmul(dst, l_hi, r_lo, start=False, stop=False)
                return pe.matmul(dst, l_lo, r_hi, start=False, stop=stop)

            def transposes(label, src, k, ready):
                for i in range(2 * NT):
                    n, (a, b) = i // 2, ((0, 4), (4, k))[i % 2]
                    if i % 2 == 0:
                        pe.wait_ge(*E(ready, n + 1))
                    dst = open_bank(label, i)
                    for j in range(a, b):
                        last = pe.transpose(dst[:, (j - a) * TN:(j - a + 1) * TN], src[:, n, j * P:(j + 1) * P],
                                            ident[0:TN, 0:TN])
                    close(last, label, i)

            def up(s, j):
                m, (c0, cn) = j // 2, CH[j % 2]
                u = FIRST_UNIT["u", s] + m
                if j % 2 == 0:
                    pe.wait_ge(*E("unit_split", u + 1))
                dst = open_bank(s + "_hidden", j)
                for k in range(KD):
                    w = slice(k * P, (k + 1) * P)
                    last = three(dst[:, 0:cn], w_hi[:, u % RING, w], w_lo[:, u % RING, w], xT_hi[:, k, c0:c0 + cn],
                                 xT_lo[:, k, c0:c0 + cn], k == 0, k == KD - 1)
                close(last, s + "_hidden", j)
                if j % 2:
                    pe.drain().then_inc(S("unit_used"), 1)

            def down(key, label, lhs_hi, lhs_lo, ready, feed=0, seed=None, after=None):
                kt, cw, chunks, per = DOWN[key]
                for c in range(chunks):
                    for k in range(kt):
                        u, pos = divmod(feed * kt * chunks + c * kt + k, per)
                        u += FIRST_UNIT["d", key]
                        w = slice(pos * cw, (pos + 1) * cw)
                        if pos == 0:
                            pe.wait_ge(*E("unit_split", u + 1))
                        if c == 0:
                            ready(k)
                        for n in range(NT):
                            i = c * NT + n
                            at = slice(n * TN, (n + 1) * TN)
                            if k == 0:
                                open_bank(label, i)
                                if seed:
                                    seed(bank(label, i), c, at)
                            last = three(bank(label, i)[0:TN, 0:cw], lhs_hi[:, k, at], lhs_lo[:, k, at],
                                         w_hi[:, u % RING, w], w_lo[:, u % RING, w], k == 0 and not seed, k == kt - 1)
                            if k == kt - 1:
                                close(last, label, i)
                        if pos == per - 1:
                            if k == kt - 1:
                                last = pe.drain()
                            last.then_inc(S("unit_used"), 1)
                    if after:
                        after(c)

            def gather(label, k, counts_of, first=0):
                for j in range(2 * k):
                    ft, (c0, cn) = j // 2, CH[j % 2]
                    dst = open_bank(label, j)
                    for s in range(NT):
                        for half in (nm_hi, nm_lo):
                            last = pe.matmul(dst[:, 0:cn], half[:, s, ft * P:(ft + 1) * P], counts_of(s, c0, cn),
                                             start=(s == 0 and half is nm_hi), stop=(s == NT - 1 and half is nm_lo))
                    close(last, label, j)

            def of_adj(s, c0, cn):
                return adj[:, s, c0:c0 + cn]

            def of_rel(r):
                return lambda s, c0, cn: rel[:, r, s, c0:c0 + cn]

            def count_edges(label):
                def step(span, t, k, first=False, last_tile=False):
                    pe.wait_ge(*E(label + "_hot", t * 2 + (2 + 2 * span * SPAN)))
                    for s in range(NT):
                        if first:
                            open_bank(label, span * NT + s)
                        ins = pe.matmul(bank(label, span * NT + s)[0:TN, 0:HALF + 1], src_hot[:, k, s * TN:(s + 1) * TN],
                                        dst_hot[:, k], start=first, stop=last_tile)
                        if last_tile:
                            close(ins, label, span * NT + s)
                    if not last_tile:
                        ins.then_inc(S(label + "_hot_used"), 1)

                for span in range(SPANS):
                    for t in range(OSLOTS):
                        step(span, t, t, first=t == 0)
                    with pe.Fori(1, SPAN // OSLOTS - 1) as q:
                        for k in range(OSLOTS):
                            step(span, q * OSLOTS + k, k)
                    for k in range(OSLOTS):
                        step(span, SPAN - OSLOTS + k, k, last_tile=k == OSLOTS - 1)

            def degrees(label, i, counts_of):
                dst = open_bank(label, i)
                for n in range(NT):
                    for s in range(NT):
                        last = pe.matmul(dst[0:TN, 2 * n:2 * n + 2], counts_of(s, n * TN, TN), ones_r[0:TN, 0:2],
                                         start=s == 0, stop=s == NT - 1)
                close(last, label, i)

            def expert_layer(s, tiles, gate):
                transposes(s + "_xT", xn, KD, s + "_xn")
                pe.wait_ge(*E(s + "_xT_pad", 2))
                for c, (c0, cn) in enumerate(CH):
                    pe.wait_ge(*E(s + "_xT_low", (6, 2 * NT)[c]))
                    dst = open_bank(s + "_routerT", c)
                    for k in range(KD):
                        g = slice(48 * gate + 8 * k, 48 * gate + 8 * k + 8)
                        last = three(dst[0:EXPERTS, 0:cn], gate_hi[:, g], gate_lo[:, g], xT_hi[:, k, c0:c0 + cn],
                                     xT_lo[:, k, c0:c0 + cn], k == 0, k == KD - 1)
                    close(last, s + "_routerT", c)
                jobs = 2 * tiles
                for j in range(jobs + EXPERT_LAG):
                    if j < jobs:
                        up(s, j)
                    if j == 0:
                        pe.wait_ge(*E(s + "_routerT_read", 2))
                        dst = open_bank(s + "_router", 0)
                        for n in range(NT):
                            last = pe.transpose(dst[0:TN, 8 * n:8 * n + 8], router_T[:, n * TN:(n + 1) * TN],
                                                ident[0:EXPERTS, 0:EXPERTS])
                        close(last, s + "_router", 0)
                    if j == EXPERT_LAG - 1:
                        if s == "f1":
                            pe.wait_ge(*E("f1_probs", 1))
                            dst = open_bank("f1_importance", 0)
                            for n in range(NT):
                                last = pe.matmul(dst[0:TN, 0:8], ones[0:TN, 0:TN], prob8[0:TN, 8 * n:8 * n + 8],
                                                 start=n == 0, stop=n == NT - 1)
                            close(last, "f1_importance", 0)
                        pe.wait_ge(*E(s + "_combine", 1))
                        for n in range(NT):
                            dst = open_bank(s + "_cT", n)
                            close(pe.transpose(dst[:, 0:TN], cpad[:, n], ident[0:TN, 0:TN]), s + "_cT", n)
                        pe.wait_ge(*E(s + "_cT_pad", 2))
                        pe.wait_ge(*E(s + "_combineT", NT))
                    if j >= EXPERT_LAG:
                        i = j - EXPERT_LAG
                        m, (c0, cn) = i // 2, CH[i % 2]
                        q, kind = (m // 3, m % 3) if tiles == 12 else (m // 2, 2 * (m % 2))
                        rows = slice(32 * q, 32 * q + 2)
                        dst = open_bank(s + "_cB", i)
                        pe.matmul(dst[:, 0:cn], pat[rows, kind], cT_hi[rows, c0:c0 + cn], start=True, stop=False)
                        close(pe.matmul(dst[:, 0:cn], pat[rows, kind], cT_lo[rows, c0:c0 + cn], start=False, stop=True),
                              s + "_cB", i)
                if s == "f1":
                    seed = None
                else:
                    pe.wait_ge(*E(s + "_rows_split", 2))

                    def seed(dst, c, at):
                        half = slice(c * 384, (c + 1) * 384)
                        three(dst[0:TN, 0:384], cT_hi[:, at], cT_lo[:, at], bias8_hi[:, half], bias8_lo[:, half],
                              True, False)

                down(s + "d", s + "_down", hT_hi, hT_lo, lambda k: pe.wait_ge(*E(s + "_low", 2 * k + 2)), seed=seed)

            pe.wait_ge(*E("consts", 21))
            pe.wait_ge(*E("g0_peak", 1))
            dst = open_bank("g0_maxT", 0)
            close(pe.matmul(dst[0:1, 0:TN], peak[0:TN, 5:6], ident[0:TN, 0:TN], start=True, stop=True), "g0_maxT", 0)
            pe.wait_ge(*E("g0_max_read", 1))
            dst = open_bank("g0_maxB", 0)
            close(pe.matmul(dst[0:TN, 0:1], ones[0:1, 0:TN], peak_all[0:1, 0:1], start=True, stop=True), "g0_maxB", 0)
            count_edges("A")
            transposes("g0_xT", xn, KD, "g0_xn")
            pe.wait_ge(*E("A_whole_added", (SPANS - 1) * NT))
            pe.wait_ge(*E("A_counts_ready", NT))
            pe.wait_ge(*E("g0_exp_low", NT))
            pe.wait_ge(*E("g0_num_low", NT))
            for j in range(2 * KD):
                ft, (c0, cn) = j // 2, CH[j % 2]
                for label, halves in (("g0_num", (nm_hi, nm_lo)), ("g0_den", (e_hi, e_lo))):
                    dst = open_bank(label, j)
                    for s in range(NT):
                        for half in halves:
                            last = pe.matmul(dst[:, 0:cn], half[:, s, ft * P:(ft + 1) * P], of_adj(s, c0, cn),
                                             start=(s == 0 and half is halves[0]), stop=(s == NT - 1 and half is halves[1]))
                    close(last, label, j)
            degrees("g1_deg", 0, of_adj)
            pe.wait_ge(*E("g0_xT_pad", 2))
            pe.wait_ge(*E("g0_out_low", 2 * KD))
            pe.wait_ge(*E("bn_ready", 1))
            for j in range(24):
                up("g0", j)
            down("g0d", "g0d", hT_hi, hT_lo, lambda k: pe.wait_ge(*E("g0_low", 2 * k + 2)))
            pe.wait_ge(*E("gates_split", 1))
            expert_layer("f0", 12, 0)
            pe.wait_ge(*E("self_loops", NT))
            pe.wait_ge(*E("g1_nodes_low", NT))
            gather("g1a_agg", KD, of_adj)
            down("g1a", "g1a", xT_hi, xT_lo, lambda k: pe.wait_ge(*E("g1a_low", 2 * k + 2)))
            pe.wait_ge(*E("g1b_nodes_low", 2 * NT))
            gather("g1b_agg", KD, of_adj)

            def edge_mask(c):
                if c == 0:
                    pe.wait_ge(*E("no_self_loops", NT))
                    for i in range(2 * NT):
                        d, (a, b) = i // 2, ((0, 4), (4, NT))[i % 2]
                        dst = open_bank("g2_maskT", i)
                        for s in range(a, b):
                            last = pe.transpose(dst[0:TN, (s - a) * TN:(s - a + 1) * TN],
                                                f(adj[:, s, d * TN:(d + 1) * TN]), ident[0:TN, 0:TN])
                        close(last, "g2_maskT", i)

            down("g1b", "g1b", xT_hi, xT_lo, lambda k: pe.wait_ge(*E("g1b_low", 2 * k + 2)), after=edge_mask)
            expert_layer("f1", 8, 1)
            transposes("g2_xT", xn, KD, "g2_xn")
            pe.wait_ge(*E("g2_xT_low", 2 * NT))

            def source_rows(label, c):
                for i, (a, b) in enumerate(((0, 4), (4, NT))):
                    dst = open_bank(label + "_asT", 2 * c + i)
                    for n in range(a, b):
                        last = pe.transpose(dst[0:2, (n - a) * TN:(n - a + 1) * TN],
                                            a_src[0:TN, 8 * n + 2 * c:8 * n + 2 * c + 2], ident[0:TN, 0:TN])
                    close(last, label + "_asT", 2 * c + i)

            def source_broadcast(label, c, heads=2):
                pe.wait_ge(*E(label + "_asT_read", 2 * (c + 1)))
                for h in range(2 * c, 2 * c + heads):
                    for half, (c0, cn) in enumerate(CH):
                        dst = open_bank(label + "_asB", 2 * h + half)
                        close(pe.matmul(dst[0:TN, 0:cn], head_sel[0:2, h % 2, 0:TN], asT[:, c0:c0 + cn],
                                        start=True, stop=True), label + "_asB", 2 * h + half)

            pe.wait_ge(*E("head_sel", 1))
            pe.wait_ge(*E("asT_pad", 1))

            def behind_quarter(c):
                if c:
                    pe.wait_ge(*E("g2p_scores", 4 * NT * c))
                    source_rows("g2p", c - 1)
                    source_broadcast("g2p", c - 1)

            down("g2a", "g2a", xT_hi, xT_lo, lambda k: None, after=behind_quarter)
            behind_quarter(4)

            def attention(layer, heads, product):
                pe.wait_ge(*E(layer + "_uv", 2))
                for i in range(4):
                    a, b = ((0, 4), (4, NT))[i % 2]
                    dst = open_bank(layer + "_uvT", i)
                    for n in range(a, b):
                        last = pe.transpose(dst[0:8, (n - a) * TN:(n - a + 1) * TN], uv[:, i // 2, n], ident[0:TN, 0:TN])
                    close(last, layer + "_uvT", i)
                pe.wait_ge(*E(layer + "_pads", 2))
                pe.wait_ge(*E(layer + "_uvT_read", 4))
                for h in range(heads + 2):
                    if h < heads:
                        for i in range(4):
                            c0, cn = CH[i % 2]
                            dst = open_bank(layer + "_uvB", 4 * h + i)
                            close(pe.matmul(dst[0:TN, 0:cn], head_sel[:, h, 0:TN], (uT, vT)[i // 2][:, c0:c0 + cn],
                                            start=True, stop=True), layer + "_uvB", 4 * h + i)
                    if heads > 1 and h >= 2:
                        turn_head(h - 2)
                    if 1 <= h <= heads:
                        product(h - 1)

            def head_product(h):
                pe.wait_ge(*E("g2p_prob", h + 1))
                for n in range(NT):
                    dst = open_bank("g2p_agg", NT * h + n)
                    for s in range(NT):
                        last = pe.matmul(dst[0:TN, 0:HEAD_DIM + 1], prob[h % 2][:, s, n * TN:(n + 1) * TN],
                                         h1[:, s, h, 0:HEAD_DIM + 1], start=s == 0, stop=s == NT - 1)
                    close(last, "g2p_agg", NT * h + n)

            def turn_head(h):
                for i, (a, b) in enumerate(((0, 4), (4, NT))):
                    pe.wait_ge(*E("g2p_mean", NT * h + b))
                    dst = open_bank("g2p_outT", 2 * h + i)
                    for n in range(a, b):
                        last = pe.transpose(dst[:, (n - a) * TN:(n - a + 1) * TN], mean[:, h % 2, n], ident[0:TN, 0:TN])
                    close(last, "g2p_outT", 2 * h + i)

            def last_product(_):
                pe.wait_ge(*E("g2q_prob", 1))
                for n in range(NT):
                    for i, at in ((2 * n, slice(384, D + 1)), (2 * n + 1, slice(0, 384))):
                        dst = open_bank("g2q_agg", i)
                        for s in range(NT):
                            last = pe.matmul(dst[0:TN, 0:at.stop - at.start], prob[0][:, s, n * TN:(n + 1) * TN],
                                             h2[:, s, at], start=s == 0, stop=s == NT - 1)
                        close(last, "g2q_agg", i)

            pe.wait_ge(*E("h1_ones", 1))
            attention("g2p", HEADS, head_product)
            down("g2b", "g2b", hT_hi, hT_lo, lambda k: pe.wait_ge(*E("g2p_low", k + 1)))
            pe.wait_ge(*E("g2q_scores", 2))
            source_rows("g2q", 0)
            source_broadcast("g2q", 0, 1)
            attention("g2q", 1, last_product)
            transposes("f2_xT", xn, KD, "f2_unit")
            pe.wait_ge(*E("slots_split", 1))
            pe.wait_ge(*E("f2_xT_pad", 2))
            for c, (c0, cn) in enumerate(CH):
                pe.wait_ge(*E("f2_xT_low", (6, 2 * NT)[c]))
                dst = open_bank("f2_logitsT", c)
                for k in range(KD):
                    last = three(dst[0:SLOTS, 0:cn], sp_hi[:, k], sp_lo[:, k], xT_hi[:, k, c0:c0 + cn],
                                 xT_lo[:, k, c0:c0 + cn], k == 0, k == KD - 1)
                close(last, "f2_logitsT", c)
            pe.wait_ge(*E("f2_logitsT_read", 2))
            dst = open_bank("f2_logits", 0)
            for n in range(NT):
                last = pe.transpose(dst[0:TN, n * SLOTS:(n + 1) * SLOTS], logitsT[:, n * TN:(n + 1) * TN],
                                    ident[0:SLOTS, 0:SLOTS])
            close(last, "f2_logits", 0)
            pe.wait_ge(*E("f2_dispatchT", 1))
            dst = open_bank("f2_dispatch", 0)
            for n in range(NT):
                last = pe.transpose(dst[0:TN, n * SLOTS:(n + 1) * SLOTS], logitsT[:, n * TN:(n + 1) * TN],
                                    ident[0:SLOTS, 0:SLOTS])
            close(last, "f2_dispatch", 0)
            pe.wait_ge(*E("f2_combine", 1))
            for i, (a, b) in enumerate(((0, 4), (4, NT))):
                dst = open_bank("f2_combineT", i)
                for n in range(a, b):
                    last = pe.transpose(dst[0:SLOTS, (n - a) * TN:(n - a + 1) * TN], combine[:, n], ident[0:TN, 0:TN])
                close(last, "f2_combineT", i)
            pe.wait_ge(*E("f2_dispatch_read", 1))
            dst = open_bank("f2_tilde", 0)
            for k in range(KD):
                for n in range(NT):
                    last = pe.matmul(dst[:, k * SLOTS:(k + 1) * SLOTS], xn[:, n, k * P:(k + 1) * P], dispatch[:, n],
                                     start=n == 0, stop=n == NT - 1)
            close(last, "f2_tilde", 0)
            pe.wait_ge(*E("slot_weights", 16 * (EXPERTS + 1)))
            pe.wait_ge(*E("f2_tilde_read", 1))
            dst = open_bank("f2_hidden", 0)
            for e in range(EXPERTS):
                for k in range(KD):
                    last = pe.matmul(dst[0:SLOT_H, 4 * e:4 * e + 4], w_down[:, e, k], tildeT[:, k, 4 * e:4 * e + 4],
                                     start=k == 0, stop=k == KD - 1)
            close(last, "f2_hidden", 0)
            pe.wait_ge(*E("f2_bias_full", 16))
            pe.wait_ge(*E("f2_diag", 1))
            for c in range(2):
                at = slice(c * 384, (c + 1) * 384)
                dst = open_bank("f2_up", c)
                pe.matmul(dst[0:SLOTS, 0:384], sel8[0:8, :], bias8[0:8, at], start=True, stop=False)
                for e in range(EXPERTS):
                    last = pe.matmul(dst[0:SLOTS, 0:384], hidden_diag[:, 32 * e:32 * e + 32], w_up[:, e, at],
                                     start=False, stop=e == EXPERTS - 1)
                close(last, "f2_up", c)
            pe.wait_ge(*E("f2_up_read", 2))
            pe.wait_ge(*E("f2_combineT_read", 2))
            for c in range(2):
                for n in range(NT):
                    dst = open_bank("f2_down", c * NT + n)
                    close(pe.matmul(dst[0:TN, 0:384], combineT[:, n * TN:(n + 1) * TN],
                                    slot_out[:, c * 384:(c + 1) * 384], start=True, stop=True), "f2_down", c * NT + n)
            pe.wait_ge(*E("type_hot", 1))
            pe.wait_ge(*E("emb_loaded", 16))
            for n in range(NT):
                dst = open_bank("g3_emb", n)
                close(pe.matmul(dst[0:TN, 0:TYPE_DIM], type_hot[:, n * TN:(n + 1) * TN], emb[:], start=True, stop=True),
                      "g3_emb", n)
            for r in range(RELS - 1):
                count_edges(f"R{r}")
            for key, k, ready in (("g3a", K1, "g3_emb_low"), ("g3b", K1, "g3b_nodes"), ("g3c", KD, "g3c_nodes")):
                transposes(key + "_hT", acc, k, ready)
                pe.wait_ge(*E(key + "_hT_pad", 2))
                pe.wait_ge(*E(key + "_hT_low", 2 * NT))
                down(key, key + "_root", xT_hi, xT_lo, lambda k: None)
                pe.wait_ge(*E(key + "_nodes_low", NT))
                for r in range(RELS):
                    if key == "g3a":
                        if r == 0:
                            pe.wait_ge(*E("last_relation", NT))
                        degrees("g3_deg", r, of_rel(r))
                    gather(f"{key}_agg{r}", k, of_rel(r))
                    first = 2 * k * r
                    down(key, f"{key}_rel{r}", xT_hi, xT_lo,
                         lambda t: pe.wait_ge(*E(key + "_low", first + 2 * t + 2)), feed=r + 1)
            expert_layer("f3", 12, 2)
            assert closed[0] == len(GROUPS)


NAMES = ["x_in", "edges_in", "wa", "wb", "wc", "cols_in", "bias_in", "rows_in", "att_in", "scalars_in",
         "w_down_in", "w_up_in", "emb_in", "types_in"]


def up_units(w):
    m = w.shape[1] // P
    return w.reshape(KD, P, m, P).transpose(2, 1, 0, 3).reshape(m, P, UNIT)


def down_slices(w, key):
    k, cw, chunks, per = DOWN[key]
    ws = w if isinstance(w, list) else [w]
    s = np.concatenate([v.reshape(k, P, chunks, cw).transpose(2, 0, 1, 3).reshape(chunks * k, P, cw) for v in ws])
    return s.reshape(-1, per, P, cw).transpose(0, 2, 1, 3).reshape(-1, P, per * cw)


def laid_out(i):
    i = {k: np.asarray(v) for k, v in i.items()}

    def per_expert_in(w):
        return w.transpose(1, 0, 2).reshape(w.shape[1], -1)

    def tiles(v):
        return v.reshape(-1, P).T

    feeds = {"g3a": "1", "g3b": "2", "g3c": "3"}
    down = {
        "g0d": i["L0_gnn_W2"], "f0d": i["L0_ffn_w2"].reshape(-1, D), "g1a": i["L1_gnn_W1"], "g1b": i["L1_gnn_W2"],
        "f1d": i["L1_ffn_w2"].transpose(0, 2, 1).reshape(-1, D), "g2a": i["L2_gnn_W1"].T, "g2b": i["L2_gnn_W2"].T,
        "f3d": i["L3_ffn_w2"].reshape(-1, D),
    }
    for key, n in feeds.items():
        down[key] = [i["L3_gnn_w_root" + n]] + list(i["L3_gnn_w_rel" + n])
    up = {
        "g0": i["L0_gnn_W1"], "f0": per_expert_in(i["L0_ffn_w1"]),
        "f1": i["L1_ffn_w1"].transpose(2, 0, 1).reshape(D, -1), "f3": per_expert_in(i["L3_ffn_w1"]),
    }

    def stream(seq):
        return np.concatenate([up_units(up[key]) if kind == "u" else down_slices(down[key], key) for kind, key in seq])

    def gate(w):
        return w.T.reshape(KD, P, EXPERTS).transpose(1, 0, 2).reshape(P, -1)

    b_down = np.concatenate([i["L2_ffn_b_down"].T, np.zeros((P - SLOT_H, EXPERTS), np.float32)])
    cols = np.concatenate(
        [tiles(i["L0_gnn_b1"]), tiles(i["L0_gnn_bn_gamma"]), tiles(i["L0_gnn_bn_beta"]), tiles(i["L0_gnn_bn_mean"]),
         tiles(i["L0_gnn_bn_var"]), tiles(i["L0_ffn_b1"].reshape(-1)), tiles(i["L3_ffn_b1"].reshape(-1)),
         tiles(i["L2_gnn_b1"]), gate(i["L0_ffn_gate_w"]), gate(i["L1_ffn_router_w"]), gate(i["L3_ffn_gate_w"]),
         i["L2_ffn_slot_params"].reshape(KD, P, SLOTS).transpose(1, 0, 2).reshape(P, -1), b_down], axis=1)

    def row(v):
        return np.concatenate([v, np.zeros(D1 - v.size, np.float32)])[None]

    def wide(v):
        return np.concatenate([v.reshape(-1), np.zeros(HEADS * HEAD_DIM - v.size, np.float32)])[None]

    return dict(
        x_in=i["x"],
        edges_in=np.stack([i["src"].reshape(TN, ET), i["dst"].reshape(TN, ET), i["edge_type_3"].reshape(TN, ET)], axis=1),
        wa=stream(SEQ_A), wb=stream(SEQ_B), wc=stream(SEQ_C), cols_in=cols,
        bias_in=np.concatenate([row(i[k]) for k in ("L0_gnn_b2", "L1_gnn_b1", "L1_gnn_b2", "L2_gnn_b2", "L3_gnn_b1",
                                                    "L3_gnn_b2", "L3_gnn_b3")]),
        rows_in=np.concatenate([i["L0_ffn_b2"], i["L2_ffn_b_up"], i["L3_ffn_b2"]]),
        att_in=np.concatenate([wide(i[k]) for k in ("L2_gnn_att_src1", "L2_gnn_att_dst1", "L2_gnn_att_src2",
                                                    "L2_gnn_att_dst2")]),
        scalars_in=np.stack([i["L0_gnn_t"].reshape(1), i["L2_ffn_scale"].reshape(1)]),
        w_down_in=i["L2_ffn_W_down"], w_up_in=i["L2_ffn_W_up"], emb_in=i["L3_gnn_node_emb"],
        types_in=i["node_type_3"][None],
    )


def kernel(**inputs):
    import concourse.bacc as bacc
    from concourse.bass_utils import run_bass_kernel_spmd

    arrays = {k: np.ascontiguousarray(v) for k, v in laid_out(inputs).items()}
    nc = bacc.Bacc("TRN2", target_bir_lowering=False, num_devices=1)
    args = [nc.dram_tensor(k, arrays[k].shape, mybir.dt.from_np(arrays[k].dtype), kind="ExternalInput").ap() for k in NAMES]
    out = nc.dram_tensor("out", (NODES, D), f32, kind="ExternalOutput").ap()
    network(nc, *args, out)
    r = run_bass_kernel_spmd(nc, [arrays], core_ids=[0])
    return r.results[0]["out"]
```

```python
import numpy as np
import concourse.bass as bass
import concourse.mybir as mybir
from concourse.alu_op_type import AluOpType as ALU
from contextlib import ExitStack

f32, f32r = mybir.dt.float32, mybir.dt.float32r
bf16, i16, i32, u32 = mybir.dt.bfloat16, mybir.dt.int16, mybir.dt.int32, mybir.dt.uint32
ACT = mybir.ActivationFunctionType
AX = mybir.AxisListType

P = 128
NODES, D = 625, 768
NT, TN = 5, 125
NP = NODES + 1
CH = [(0, 314), (314, 312)]
KD = D // P
EDGES = 10000
ET = EDGES // TN
HALF = NP // 2
FRACTION = 2.0 ** -12
SPAN = 16
SPANS = ET // SPAN
assert SPAN * SPANS == ET and SPAN * TN < 2048
ROUNDER = 1.5 * 2.0 ** 23
TYPE_DIM = 128
D1 = D + TYPE_DIM
K1 = D1 // P
RELS = 3
EXPERTS = 8
HEADS, HEAD_DIM = 8, 128
SLOTS = 32
SLOT_H = 96
UNIT, UNIT_WIDE = 768, 896
RING = 3
SMALL = 608
EXPERT_LAG = 5
LN_EPS = 1e-5
FAR = -2.0 ** 100

UP_UNITS = dict(g0=12, f0=12, f1=8, f3=12)
DOWN = {
    "g0d": (12, 384, 2, 2), "f0d": (12, 384, 2, 2), "g1a": (6, 384, 2, 2), "g1b": (6, 384, 2, 2),
    "f1d": (8, 384, 2, 2), "g2a": (6, 256, 4, 3), "g2b": (8, 384, 2, 2),
    "g3a": (K1, 448, 2, 2), "g3b": (K1, 384, 2, 2), "g3c": (KD, 384, 2, 2), "f3d": (12, 384, 2, 2),
}
FEEDS = RELS + 1


def down_units(key):
    k, _, chunks, per = DOWN[key]
    n = k * chunks * (FEEDS if key in ("g3a", "g3b", "g3c") else 1)
    assert n % per == 0
    return n // per


SEQ_A = [("u", "g0"), ("d", "g0d"), ("u", "f0"), ("d", "f0d"), ("d", "g1a"), ("d", "g1b"),
         ("u", "f1"), ("d", "f1d"), ("d", "g2a"), ("d", "g2b")]
SEQ_B = [("d", "g3a")]
SEQ_C = [("d", "g3b"), ("d", "g3c"), ("u", "f3"), ("d", "f3d")]
FIRST_UNIT, at = {}, 0
for kind, key in SEQ_A + SEQ_B + SEQ_C:
    FIRST_UNIT[kind, key] = at
    at += UP_UNITS[key] if kind == "u" else down_units(key)
UNITS_A, UNITS_B = FIRST_UNIT["d", "g3a"], down_units("g3a")
UNITS = at
UNITS_C = UNITS - UNITS_A - UNITS_B

COLS, at = {}, 0
for name, n in [("bn_b1", 12), ("bn_gamma", 12), ("bn_beta", 12), ("bn_mean", 12), ("bn_var", 12),
                ("f0_b1", 12), ("f3_b1", 12), ("g2_b1", 8), ("f0_gate", 48), ("f1_gate", 48),
                ("f3_gate", 48), ("slots", KD * SLOTS), ("b_down", 8)]:
    COLS[name] = (at, at + n)
    at += n
NCOLS = at


def job_of(s, j):
    if s == "g0" and j < 6:
        return j % 3, j // 3
    return j // 2, j % 2


def plan_groups():
    groups = []
    where = {}

    def add(label, idx, sem, value):
        where[label, idx] = len(groups)
        groups.append((sem, value))

    def several(label, n, sem, first=0, per=1):
        for i in range(n):
            add(label, i, sem, first + (i + 1) * per)

    def sweep(label):
        for i in range(SPANS * NT):
            add(label, i, label + "_counted", i + 1)

    def ffn(f, tiles):
        several(f + "_xT", 2 * NT, f + "_xT_low")
        several(f + "_routerT", 2, f + "_routerT_read")
        jobs, lag = 2 * tiles, EXPERT_LAG
        for j in range(jobs + lag):
            if j < jobs:
                add(f + "_hidden", j, f + "_activated", j + 1)
            if j == 0:
                add(f + "_router", 0, f + "_routed", 1)
            if j == lag - 1:
                if f == "f1":
                    add(f + "_importance", 0, f + "_importance_read", 1)
                several(f + "_cT", NT, f + "_combineT")
            if j >= lag:
                add(f + "_cB", j - lag, f + "_weighted", j - lag + 1)
        several(f + "_down", 2 * NT, f + "_x")

    def attention_groups(layer, heads):
        several(layer + "_uvT", 4, layer + "_uvT_read")
        def broadcast(h):
            for i in range(4):
                add(layer + "_uvB", 4 * h + i, layer + "_uvB_read", 4 * h + i + 1)

        broadcast(0)
        for h in range(heads + 2):
            if h + 1 < heads:
                broadcast(h + 1)
            if layer == "g2p" and 1 <= h <= heads:
                for i in range(2):
                    add("g2p_agg", 2 * (h - 1) + i, "g2p_mean", 2 * (h - 1) + i + 1)
            if layer == "g2p" and h >= 2:
                for i in range(2):
                    add("g2p_outT", 2 * (h - 2) + i, "g2p_relu", 2 * (h - 2) + i + 1)

    add("g0_maxT", 0, "g0_max_read", 1)
    add("g0_maxB", 0, "g0_maxB_read", 1)
    sweep("A")
    several("g0_xT", 2 * NT, "g0_xT_copied")
    for j in range(2 * KD):
        add("g0_num", j, "g0_num_read", j + 1)
        add("g0_den", j, "g0_den_read", j + 1)
    add("g1_deg", 0, "g1_deg_read", 1)
    several("g0_hidden", 24, "g0_activated")
    several("g0d", 2 * NT, "g0_x")
    ffn("f0", 12)
    several("g1a_agg", 2 * KD, "g1a_low")
    several("g1a", 2 * NT, "g1a_read")
    several("g1b_agg", 2 * KD, "g1b_low")
    for n in range(NT):
        add("g1b", n, "g1_x", n + 1)
    several("g2_maskT", 2 * NT, "g2_masked")
    for n in range(NT):
        add("g1b", NT + n, "g1_x", NT + n + 1)
    ffn("f1", 8)
    several("g2_xT", 2 * NT, "g2_xT_low")
    for c in range(5):
        for n in range(NT):
            if c < 4:
                add("g2a", c * NT + n, "g2_h1", c * NT + n + 1)
            if c and n == 1:
                for i in range(2):
                    add("g2p_asT", 2 * (c - 1) + i, "g2p_asT_read", 2 * (c - 1) + i + 1)
            if c and n == 2:
                for i in range(4):
                    add("g2p_asB", 4 * (c - 1) + i, "g2p_asB_read", 4 * (c - 1) + i + 1)
    attention_groups("g2p", HEADS)
    several("g2b", 2 * NT, "g2_h2")
    several("g2q_asT", 2, "g2q_asT_read")
    several("g2q_asB", 2, "g2q_asB_read")
    attention_groups("g2q", 1)
    several("g2q_agg", 2 * NT, "g2_x")
    several("f2_xT", 2 * NT, "f2_xT_low")
    several("f2_logitsT", 2, "f2_logitsT_read")
    several("f2_logits", 1, "f2_logits_read")
    several("f2_dispatch", 1, "f2_dispatch_read")
    several("f2_combineT", 2, "f2_combineT_read")
    several("f2_tilde", 1, "f2_tilde_read")
    several("f2_hidden", 1, "f2_hidden_read")
    several("g3_emb", NT, "g3_emb_low")
    several("f2_up", 2, "f2_up_read")
    several("f2_down", 2 * NT, "f2_x")
    for r in range(RELS - 1):
        sweep(f"R{r}")
    for key, k in (("g3a", K1), ("g3b", K1), ("g3c", KD)):
        several(key + "_hT", 2 * NT, key + "_hT_low")
        if key == "g3a":
            several("g3_deg", RELS - 1, "g3_deg_read")
        several(key + "_root", 2 * NT, key + "_acc", 0)
        for r in range(RELS):
            if key == "g3a" and r == RELS - 1:
                add("g3_deg", r, "g3_deg_read", r + 1)
            several(f"{key}_agg{r}", 2 * k, f"{key}_low", 2 * k * r)
            several(f"{key}_rel{r}", 2 * NT, key + "_acc", 2 * NT * (r + 1))
    ffn("f3", 12)
    return groups, where


GROUPS, WHERE = plan_groups()


def families():
    table = {}

    def family(kind, totals):
        base = 0
        for layer, total in totals:
            table[layer + "_" + kind] = (kind, base)
            base += total

    def each(layers, total):
        return [(s, total) for s in layers.split()]

    for kind, n in (("var", 1), ("std", 1), ("xn", NT)):
        family(kind, each("g0 f0 g1 f1 g2 f2 g3 f3", n))
    for half in ("high", "low"):
        family("T_" + half, each("f0_x f1_x g2_x f2_x g3a_h g3b_h g3c_h f3_x", 2 * NT))
        for layer in "f0_x f1_x g2_x f2_x g3a_h g3b_h g3c_h f3_x".split():
            table[layer + "T_" + half] = table.pop(layer + "_T_" + half)
        family(half, [("g0", 24), ("f0", 24), ("g1a", 12), ("g1b", 12), ("f1", 16), ("g2p", HEADS),
                      ("g3a", 6 * K1), ("g3b", 6 * K1), ("g3c", 6 * KD), ("f3", 24)])
        family("nodes_" + half, [("g1", NT), ("g1b", 2 * NT), ("g3a", NT), ("g3b", NT), ("g3c", NT)])
    family("T_pad", each("g0_x f0_x f1_x g2_x f2_x g3a_h g3b_h g3c_h f3_x", 2))
    for layer in "g0_x f0_x f1_x g2_x f2_x g3a_h g3b_h g3c_h f3_x".split():
        table[layer + "T_pad"] = table.pop(layer + "_T_pad")
    family("activated", [("g0", 24), ("f0", 24), ("f1", 16), ("f3", 24)])
    family("weighted", [("f0", 24), ("f1", 16), ("f3", 24)])
    family("x", each("g0 f0 g1 f1 g2 f2 g3 f3", 2 * NT))
    for kind, n in (("routed", 1), ("routerT_read", 2), ("shifted", 1), ("exp", 1), ("probs", 1), ("combine", 1), ("cT_pad", 2), ("cT_high", NT),
                    ("combineT", NT), ("cpad_clear", 1)):
        family(kind, each("f0 f1 f3", n))
    family("bias_full", [("g0", 16), ("f0", 64), ("g1", 16), ("g1b", 16), ("g2", 16), ("f2", 16), ("g3a", 16),
                         ("g3b", 16), ("g3c", 16), ("f3", 64)])
    family("rows_clear", each("f0 f3", 1))
    family("rows_split", each("f0 f3", 2))
    family("hot", each("A R0 R1", 2 * ET))
    family("hot_used", each("A R0 R1", ET - SPANS))
    for kind in ("rounded", "counted"):
        family(kind, each("A R0 R1", SPANS * NT))
    family("whole", each("A R0 R1", (SPANS - 1) * NT))
    family("whole_added", each("A R0 R1", (SPANS - 2) * NT))
    family("whole_summed", each("A R0 R1", NT))
    family("fraction_added", each("A R0 R1", (SPANS - 2) * NT))
    family("fraction_summed", each("A R0 R1", NT))
    family("counts_ready", each("A R0 R1", NT))
    family("nodes", each("g3b g3c", 2 * NT))
    family("acc", each("g3a g3b g3c", 2 * NT * FEEDS))
    for kind, n in (("asB_read", 2), ("max_done", NT), ("uvB_read", 4), ("shift", NT), ("leaky", NT), ):
        family(kind, [("g2p", n * HEADS), ("g2q", n)])
    for kind in ("powers", "prob"):
        family(kind, [("g2p", HEADS * NT), ("g2q", NT)])
    family("asT_read", [("g2p", 8), ("g2q", 2)])
    for kind, n in (("uvT_read", 4), ("uv", 2), ("pads", 2)):
        family(kind, each("g2p g2q", n))
    return table


FAMILY = families()


def network(nc, x_in, edges_in, wa, wb, wc, cols_in, bias_in, rows_in, att_in, scalars_in, w_down_in,
            w_up_in, emb_in, types_in, out):
    ctx = ExitStack()
    with ctx:
        sems = {}

        def S(event):
            name = FAMILY.get(event, (event, 0))[0]
            if name not in sems:
                sems[name] = ctx.enter_context(nc.semaphore(name))
            return sems[name]

        def E(event, count):
            return S(event), count + FAMILY.get(event, (event, 0))[1]

        arena_bytes = 212800
        start = -(-nc.sbuf_base // 64) * 64
        arena = ctx.enter_context(nc.sbuf_tensor("arena", [P, arena_bytes], mybir.dt.uint8))
        top = [start]

        def up32(n):
            return -(-n // 32) * 32

        def region(nbytes):
            off = top[0]
            top[0] += up32(nbytes)
            assert top[0] <= start + arena_bytes, (top[0] - start, arena_bytes)
            return off

        size = {f32: 4, f32r: 4, i32: 4, u32: 4, bf16: 2, i16: 2}

        def at_(name, shape, dt, off):
            return nc.alloc_sbuf_tensor_at(name, shape, dt, offset=off)

        def new(name, shape, dt=f32):
            return at_(name, shape, dt, region(int(np.prod(shape[1:])) * size[dt]))

        x = new("x", [TN, NT, D])
        XT = region(2 * up32(K1 * NP * 4) + 64)
        HT = region(2 * 12 * NP * 4)
        NM = region(2 * NT * D1 * 4)
        xt_lo_off = XT + up32(K1 * NP * 4)
        xT_hi, xT_lo = at_("xT_hi", [P, K1, NP], f32r, XT), at_("xT_lo", [P, K1, NP], f32r, xt_lo_off)
        ht_lo_off = HT + 12 * NP * 4
        hT_hi, hT_lo = at_("hT_hi", [P, 12, NP], f32r, HT), at_("hT_lo", [P, 12, NP], f32r, ht_lo_off)
        nm_hi = at_("nm_hi", [TN, NT, D1], f32r, NM)
        nm_lo = at_("nm_lo", [TN, NT, D1], f32r, NM + NT * D1 * 4)
        xn = at_("xn", [TN, NT, D], f32, HT)
        e_hi = at_("e_hi", [TN, NT, D], f32r, HT + 15360)
        e_lo = at_("e_lo", [TN, NT, D], f32r, HT + 30720)
        acc = at_("acc", [TN, NT, D1], f32, HT)
        rel = at_("rel", [TN, RELS, NT, NP], f32r, HT + 17920)
        OH = HT + 17920 + up32(RELS * NT * NP * 4)
        assert OH <= NM
        OSLOTS = 4
        src_hot = at_("src_hot", [TN, OSLOTS, NODES], bf16, XT)
        dst_hot = at_("dst_hot", [TN, OSLOTS, CH[0][1]], bf16, XT + up32(OSLOTS * NODES * 2))
        msg = at_("msg", [TN, NT, D], f32, xt_lo_off)
        xT_full = at_("xT_full", [P, KD, NP], f32, xt_lo_off)
        HD = HEAD_DIM + 2
        h1 = at_("h1", [TN, NT, HEADS, HD], f32, NM)
        mask_off = NM + NT * HEADS * HD * 4
        maskT = at_("maskT", [TN, NT, NP], bf16, mask_off)
        gat_small = mask_off + up32(NT * NP * 2)
        h2 = at_("h2", [TN, NT, D + 2], f32, NM)
        prob = [at_(f"prob{i}", [TN, NT, NP], f32, XT + i * up32(NT * NP * 4)) for i in range(2)]
        uB = [at_(f"uB{i}", [TN, 2, NP], f32, XT + 2 * up32(NT * NP * 4) + i * up32(2 * NP * 4)) for i in range(2)]
        att = at_("att", [TN, 2, HEADS * HEAD_DIM], f32, HT + 8 * NP * 4)
        w_down = at_("w_down", [P, EXPERTS, KD, SLOT_H], f32, HT + 15360)
        w_up = at_("w_up", [SLOT_H, EXPERTS, D], f32, HT + 15360 + 18432)
        sp_hi = at_("sp_hi", [P, KD, SLOTS], f32r, XT + up32(KD * NP * 4))
        sp_lo = at_("sp_lo", [P, KD, SLOTS], f32r, xt_lo_off + up32(KD * NP * 4))

        adj = new("adj", [TN, NT, NP], f32r)
        raw = new("raw", [P, RING, UNIT_WIDE])
        w_hi = new("w_hi", [P, RING, UNIT_WIDE], f32r)
        w_lo = new("w_lo", [P, RING, UNIT_WIDE], f32r)
        bias_off = region(D1 * 4)
        bias = at_("bias", [TN, D1], f32, bias_off)
        bias8 = at_("bias8", [P, D], f32, bias_off)
        TSLOTS = 6
        tmp_off = region(TSLOTS * CH[0][1] * 4)
        tmp = at_("tmp", [P, TSLOTS, CH[0][1]], f32, tmp_off)
        iota = new("iota", [TN, NP], i16)
        ident = new("ident", [P, P])
        ones_r = new("ones_r", [P, P], f32r)
        ones = ones_r[:].bitcast(f32)
        nm_at = [NM]

        def nm_new(name, shape, dt):
            off = nm_at[0]
            nm_at[0] += up32(int(np.prod(shape[1:])) * 4)
            return at_(name, shape, dt, off)

        cpad = nm_new("cpad", [TN, NT, P], f32)
        cT_hi, cT_lo = nm_new("cT_hi", [P, NP], f32r), nm_new("cT_lo", [P, NP], f32r)
        bias8_hi, bias8_lo = nm_new("bias8_hi", [P, D], f32r), nm_new("bias8_lo", [P, D], f32r)
        router_T = nm_new("router_T", [EXPERTS, NP], f32)
        assert nm_at[0] <= NM + 20480
        pat = new("pat", [P, 3, P], f32r)
        cols = new("cols", [P, NCOLS])
        gate_hi = new("gate_hi", [P, 3 * 48], f32r)
        gate_lo = new("gate_lo", [P, 3 * 48], f32r)
        e_int = at_("e_int", [TN, 3, ET], i32, NM)
        edge = new("edge", [TN, 3, ET])
        small = new("small", [P, SMALL])
        sp_tmp = at_("sp_tmp", [P, KD, SLOTS], f32, tmp_off)

        used_small = [0]

        def sm(n):
            a = used_small[0]
            used_small[0] += n
            assert used_small[0] <= SMALL
            return small[:, a:a + n]

        stats, moments, rstd = sm(NT * 12), sm(NT * 2), sm(NT)
        t_col, slot_scale, tiny, rounder, unrounder = (sm(1) for _ in range(5))
        dinv, rel_inv = sm(NT), sm(RELS * NT)
        peak, peak_all = sm(8), sm(2)
        bn_s, bn_b = sm(12), sm(12)
        iota8, rel_index = sm(8), sm(1)
        logit8, prob8, hot8, top8, idx8f = (sm(NT * 8) for _ in range(5))
        sum8, run8 = sm(NT), sm(8)
        sel8 = sm(SLOTS)
        a_src, a_dst, a_src5, a_max = (sm(NT * 8) for _ in range(4))
        no_edge, slot_sum = sm(NT), sm(KD * 4)
        a_part = sm(NT * 4)
        idx8 = new("idx8", [P, NT * 8], u32)
        emb = at_("emb", [RELS, TYPE_DIM], f32, tmp_off + 3200)
        asT = at_("asT", [2, NP], f32, gat_small)
        uT = at_("uT", [HEADS, NP], f32, gat_small + up32(NP * 4))
        vT = at_("vT", [HEADS, NP], f32, gat_small + 2 * up32(NP * 4))
        assert gat_small + 3 * up32(NP * 4) <= NM + 2 * NT * D1 * 4
        head_sel = at_("head_sel", [HEADS, HEADS, P], f32, ht_lo_off + 8 * NP * 4)
        uv = at_("uv", [TN, 2, NT, 8], f32, ht_lo_off + 8 * NP * 4 + 4096)
        asB = at_("asB", [TN, 2, NP], f32, tmp_off)
        mean = at_("mean", [TN, 2, NT, HEAD_DIM], f32, tmp_off)
        junk = at_("junk", [TN, D], f32, ht_lo_off + 8 * NP * 4 + 4096 + 512)
        edge_scores = [at_("edge_scores0", [TN, NP], f32, xt_lo_off + up32(KD * NP * 4)),
                       at_("edge_scores1", [TN, NP], f32, tmp_off + up32(2 * NP * 4))]
        head_T = at_("head_T", [P, NODES], f32, ht_lo_off + 8 * NP * 4 + 4096 + 512)
        e_full = [at_(f"e_full{i}", [TN, D], f32, HT + 46080 + i * 3072) for i in range(2)]
        logits = at_("logits", [TN, 2, D], f32, tmp_off)
        f2s = [NM]

        def f2_new(name, shape):
            off = f2s[0]
            f2s[0] += up32(int(np.prod(shape[1:])) * 4)
            assert f2s[0] <= NM + 2 * NT * D1 * 4
            return at_(name, shape, f32, off)

        slot_logits = f2_new("slot_logits", [TN, NT, SLOTS])
        combine = f2_new("combine", [TN, NT, SLOTS])
        dispatch = f2_new("dispatch", [TN, NT, SLOTS])
        logitsT, combineT = f2_new("logitsT", [SLOTS, NP]), f2_new("combineT", [SLOTS, NP])
        tildeT = f2_new("tildeT", [P, KD, SLOTS])
        slot_hidden = f2_new("slot_hidden", [SLOT_H, EXPERTS, 4])
        hidden_diag = f2_new("hidden_diag", [SLOT_H, EXPERTS * 36])
        slot_out = f2_new("slot_out", [SLOTS, D])
        col_peak, col_sum = f2_new("col_peak", [TN, NT]), f2_new("col_sum", [TN, NT])
        row_peak, row_sum = f2_new("row_peak", [SLOTS, 1]), f2_new("row_sum", [SLOTS, 1])
        f2_junk = f2_new("f2_junk", [TN, D])
        node_type_i = at_("node_type_i", [RELS, NODES], i32, tmp_off)
        types = at_("types", [TN, ET], f32, xt_lo_off + 6400)
        src_plus = at_("src_plus", [TN, ET], f32, xt_lo_off + 6400 + 320)
        rel_source = at_("rel_source", [TN, RELS - 1, ET], f32, xt_lo_off + 6400 + 640)
        rounded = at_("rounded", [TN, NT, HALF], f32, tmp_off)
        assert NT * HALF * 4 <= TSLOTS * CH[0][1] * 4
        parts_off = XT + up32(OSLOTS * (NODES + 2 * HALF) * 2) + 704
        fraction_parts = at_("fraction_parts", [TN, NT, HALF], f32, up32(parts_off))
        assert up32(parts_off) + NT * HALF * 4 <= xt_lo_off
        whole_parts = {"A": at_("whole_parts_A", [TN, NT, HALF], f32, HT + 52224),
                       "R": at_("whole_parts_R", [TN, NT, HALF], f32, xt_lo_off)}
        dst_place = at_("dst_place", [TN, ET], f32, XT + up32(OSLOTS * (NODES + 2 * HALF) * 2) + 64)
        dst_adds = at_("dst_adds", [TN, ET], f32, XT + up32(OSLOTS * (NODES + 2 * HALF) * 2) + 64 + 320)
        type_hot = at_("type_hot", [RELS, NODES], f32, tmp_off + 3712)

        banks = [ctx.enter_context(nc.psum_tensor(f"bank{b}", [P, 512], f32)) for b in range(8)]
        block = ctx.enter_context(nc.Block())

        def bank(label, i):
            return banks[WHERE[label, i] % 8]

        def col(name, i=None):
            a, b = COLS[name]
            return cols[:, a:b] if i is None else cols[:, a + i:a + i + 1]

        def await_group(engine, label, i):
            engine.wait_ge(*E("group_closed", WHERE[label, i] + 1))

        def f(ap):
            return ap.bitcast(f32)

        node_view = "(n p) d -> p n d"

        def ring_units(engine, first, count, body):
            last = first + count
            q0, q1 = -(-first // RING), last // RING
            for u in range(first, q0 * RING):
                body(u, u // RING, u % RING)
            with engine.Fori(q0, q1) as q:
                for k in range(RING):
                    body(q * RING + k, q, k)
            for u in range(q1 * RING, last):
                body(u, u // RING, u % RING)

        SEGMENTS = [(0, UNITS_A, wa, UNIT), (UNITS_A, UNITS_B, wb, UNIT_WIDE),
                    (UNITS_A + UNITS_B, UNITS_C, wc, UNIT)]

        @block.sync
        def _(sp):
            for n in range(NT):
                sp.dma_start(x[:, n], x_in[n * TN:(n + 1) * TN]).then_inc(S(f"x_loaded{n}"), 16)
            sp.dma_start(e_int[:], edges_in).then_inc(S("edges_loaded"), 16)
            sp.dma_start(cols[:], cols_in).then_inc(S("cols_loaded"), 16)

            def load(first, src, width):
                def body(u, q, k):
                    sp.wait_ge(*E("unit_split", u - RING + 1))
                    sp.dma_start(raw[:, k, 0:width], src[bass.ds(u - first, 1)].rearrange("a p n -> (a p) n")
                                 ).then_inc(S(f"raw_full{k}"), 16)
                return body

            for k in range(RING):
                sp.dma_start(raw[:, k, 0:UNIT], wa[k]).then_inc(S(f"raw_full{k}"), 16)
            ring_units(sp, RING, UNITS_A - RING, load(0, wa, UNIT))
            sp.wait_ge(*E("g2q_uvB_read", 4))
            for e in range(EXPERTS):
                sp.dma_start(w_down[:, e], w_down_in[e].rearrange("(k p) h -> p k h", p=P)
                             ).then_inc(S("slot_weights"), 16)
            sp.dma_start(w_up[:], w_up_in.rearrange("e h d -> h e d")).then_inc(S("slot_weights"), 16)
            ring_units(sp, UNITS_A, UNITS_B, load(UNITS_A, wb, UNIT_WIDE))
            ring_units(sp, UNITS_A + UNITS_B, UNITS_C, load(UNITS_A + UNITS_B, wc, UNIT))
            for c in range(2):
                sp.wait_ge(*E("f3_x", NT * (c + 1)))
                sp.dma_start(out.rearrange(node_view, p=TN)[:, :, c * 384:(c + 1) * 384],
                             x[:, :, c * 384:(c + 1) * 384]).then_inc(S("stored"), 16)
            sp.wait_ge(*E("stored", 32))

        @block.gpsimd
        def _(pool):
            pool.iota(iota[:], pattern=[[1, NP]], base=0, channel_multiplier=0).then_inc(S("consts"), 1)
            pool.iota(idx8[:, 0:8].bitcast(i32), pattern=[[1, 8]], base=0, channel_multiplier=0).then_inc(S("consts"), 1)
            pool.iota(idx8[:, 8:9].bitcast(i32), pattern=[[0, 1]], base=0, channel_multiplier=1).then_inc(S("consts"), 1)
            pool.memset(ones, 1.0).then_inc(S("blanks"), 1)
            pool.memset(f(pat[:]), 0.0).then_inc(S("blanks"), 1)
            pool.memset(sel8[0:8, :], 1.0).then_inc(S("blanks"), 1)
            pool.wait_ge(*E("blanks", 3))
            pool.affine_select(out=ident[:], in_=ones, compare_op=ALU.is_equal, fill=0.0, base=0,
                               pattern=[[-1, P]], channel_multiplier=1).then_inc(S("consts"), 1)
            pool.affine_select(out=sel8[0:8, :].rearrange("p (e s) -> p e s", e=8),
                               in_=sel8[0:8, :].rearrange("p (e s) -> p e s", e=8), compare_op=ALU.is_equal,
                               fill=0.0, base=0, pattern=[[-1, 8], [0, 4]], channel_multiplier=1
                               ).then_inc(S("consts"), 1)
            made = 5
            for q in range(4):
                rows = slice(32 * q, 32 * q + 2)
                for kind, a, b, first in ((0, 0, P, True), (1, 0, 64, True), (1, 64, P, False), (2, 0, P, False)):
                    pool.wait_ge(*E("consts", made))
                    made += 1
                    pool.affine_select(out=pat[rows, kind, a:b], in_=ones[rows, a:b],
                                       compare_op=ALU.is_equal, fill=0.0, base=0 if first else -1,
                                       pattern=[[0, b - a]], channel_multiplier=1).then_inc(S("consts"), 1)

            pool.wait_ge(*E("consts", made))

            def add_counts(label, target, span):
                for s in range(NT):
                    i = span * NT + s
                    pool.wait_ge(*E(label + "_whole", i + 1))
                    if span > 1:
                        pool.wait_ge(*E(label + "_whole_added", i - 2 * NT + 1))
                    pool.tensor_tensor(target[:, s, 0:HALF], f(target[:, s, 0:HALF]),
                                       whole_parts[label[0]][:, s], ALU.add).then_inc(S(label + "_whole_added"), 1)
                    pool.wait_ge(*E(label + "_counted", i + 1))
                    if span > 1:
                        pool.wait_ge(*E(label + "_fraction_added", i - 2 * NT + 1))
                    pool.tensor_tensor(target[:, s, HALF:NP], f(target[:, s, HALF:NP]),
                                       fraction_parts[:, s], ALU.add
                                       ).then_inc(S(label + "_fraction_added"), 1)

            for n in range(NT):
                pool.wait_ge(*E("g0_exp_high", n + 1))
                pool.tensor_tensor(msg[:, n], msg[:, n], e_full[n % 2][:], ALU.mult).then_inc(S("g0_num_full"), 1)
                pool.tensor_tensor(e_lo[:, n], e_full[n % 2][:], f(e_hi[:, n]), ALU.subtract).then_inc(S("g0_exp_low"), 1)
                pool.wait_ge(*E("g0_num_high", n + 1))
                pool.tensor_tensor(nm_lo[:, n, 0:D], msg[:, n], f(nm_hi[:, n, 0:D]), ALU.subtract
                                   ).then_inc(S("g0_num_low"), 1)
                if n >= 2:
                    add_counts("A", adj, n - 1)
            pool.wait_ge(*E("g0_bias_full", 16))
            for n in range(NT):
                pool.tensor_tensor(x[:, n], x[:, n], xn[:, n], ALU.add).then_inc(S("g0_residual"), 1)
            for n in range(NT):
                pool.wait_ge(*E("g0_residual", NT + n))
                pool.tensor_tensor(x[:, n], x[:, n], bias[:, 0:D], ALU.add).then_inc(S("g0_residual"), 1)

            def split(width):
                def body(u, q, k):
                    pool.wait_ge(*E(f"raw_full{k}", 16 * q + 16))
                    if not (isinstance(u, int) and u < RING):
                        pool.wait_ge(*E("unit_used", u - RING + 1))
                    pool.tensor_tensor(w_hi[:, k, 0:width], raw[:, k, 0:width],
                                       ones[:, 0:1].to_broadcast([P, width]), ALU.mult).then_inc(S("unit_high"), 1)
                    pool.wait_ge(*E("unit_high", u + 1))
                    pool.tensor_tensor(w_lo[:, k, 0:width], raw[:, k, 0:width], f(w_hi[:, k, 0:width]),
                                       ALU.subtract).then_inc(S("unit_split"), 1)
                return body

            for u in range(RING):
                split(UNIT)(u, 0, u)
            ring_units(pool, RING, UNITS_A - RING, split(UNIT))
            for r in range(RELS - 1):
                for span in range(1, SPANS - 1):
                    add_counts(f"R{r}", rel[:, r], span)
            ring_units(pool, UNITS_A, UNITS_B, split(UNIT_WIDE))
            ring_units(pool, UNITS_A + UNITS_B, UNITS_C, split(UNIT))

        @block.scalar
        def _(act):
            def fill_bias(name, row, width):
                act.dma_start(bias[:, 0:width], bias_in[row:row + 1, 0:width].to_broadcast([TN, width])
                              ).then_inc(S(name), 16)

            def fill_pairs(name, row):
                for q in range(4):
                    act.dma_start(bias8[32 * q:32 * q + 2, :], rows_in[row + 2 * q:row + 2 * q + 2, :]
                                  ).then_inc(S(name), 16)

            def root_of_variance(s):
                act.wait_ge(*E(s + "_var", 1))
                act.activation(rstd[0:TN], rstd[0:TN], ACT.Sqrt).then_inc(S(s + "_std"), 1)

            def xT_high(label, k):
                for i in range(2 * NT):
                    n, (a, b) = i // 2, ((0, 4), (4, k))[i % 2]
                    await_group(act, label, i)
                    act.activation(xT_hi[:, a:b, n * TN:(n + 1) * TN],
                                   bank(label, i)[:, 0:(b - a) * TN].rearrange("p (k n) -> p k n", n=TN),
                                   ACT.Copy).then_inc(S(label + "_high"), 1)

            def nodes_high(full, width, src, high, before=0):
                for n in range(NT):
                    act.wait_ge(*E(full, before + n + 1))
                    act.activation(nm_hi[:, n, 0:width], src[:, n, 0:width], ACT.Copy).then_inc(S(high), 1)

            def messages_high(key, label, k):
                for i in range(2 * k):
                    ft, (c0, cn) = i // 2, CH[i % 2]
                    await_group(act, label, i)
                    act.activation(xT_hi[:, ft, c0:c0 + cn], bank(label, i)[:, 0:cn], ACT.Copy
                                   ).then_inc(S(key + "_high"), 1)

            def counts(label, target, span):
                for s in range(NT):
                    i = span * NT + s
                    await_group(act, label, i)
                    if span or label == "R1":
                        act.wait_ge(*E(label + "_counted", max(i - NT + 1, 0)))
                        act.wait_ge(*E(label + "_whole", max(i - NT + 1, 0)))
                    if label == "R1" and span == 0:
                        act.wait_ge(*E("R0_whole_summed", NT))
                    act.activation(rounded[:, s], bank(label, i)[0:TN, 0:HALF], ACT.Identity,
                                   bias=rounder[0:TN]).then_inc(S(label + "_rounded"), 1)
                for s in range(NT if span < SPANS - 1 else 0):
                    i = span * NT + s
                    act.wait_ge(*E(label + "_rounded", i + 1))
                    if span and (span > 1 or label == "R1"):
                        act.wait_ge(*E(label + "_whole_added", max(i - 2 * NT + 1, 0)))
                    dst = whole_parts[label[0]][:, s] if span else target[:, s, 0:HALF]
                    act.activation(dst, rounded[:, s], ACT.Identity, bias=unrounder[0:TN]
                                   ).then_inc(S(label + "_whole"), 1)

            def second_half(label, target):
                for s in range(NT):
                    act.wait_ge(*E(label + "_fraction_summed", s + 1))
                    act.activation(target[:, s, HALF:NP], f(target[:, s, HALF:NP]), ACT.Copy, scale=-1 / FRACTION
                                   ).then_inc(S(label + "_counts_ready"), 1)

            def hidden(s, tiles, func, scale_bias, full):
                jobs = 2 * tiles
                for j in range(jobs + TSLOTS - 1):
                    if j < jobs:
                        m, c = job_of(s, j)
                        cn = CH[c][1]
                        await_group(act, s + "_hidden", j)
                        if j >= TSLOTS:
                            act.wait_ge(*E(s + "_low", j - TSLOTS + 1))
                        act.activation(tmp[:, j % TSLOTS, 0:cn], bank(s + "_hidden", j)[:, 0:cn], func,
                                       **scale_bias(m)).then_inc(S(s + "_activated"), 1)
                    if j >= TSLOTS - 1:
                        i = j - TSLOTS + 1
                        m, c = job_of(s, i)
                        c0, cn = CH[c]
                        act.wait_ge(*E(full, i + 1))
                        act.activation(hT_hi[:, m, c0:c0 + cn], tmp[:, i % TSLOTS, 0:cn], ACT.Copy
                                       ).then_inc(S(s + "_high"), 1)

            def expert_layer(s, tiles, func, biased, fill=None):
                root_of_variance(s)
                xT_high(s + "_xT", KD)
                for c, (c0, cn) in enumerate(CH):
                    await_group(act, s + "_routerT", c)
                    act.activation(router_T[:, c0:c0 + cn], bank(s + "_routerT", c)[0:EXPERTS, 0:cn], ACT.Copy
                                   ).then_inc(S(s + "_routerT_read"), 1)
                if fill:
                    fill()
                act.wait_ge(*E(s + "_shifted", 1))
                act.activation(prob8[0:TN], prob8[0:TN], ACT.Exp).then_inc(S(s + "_exp"), 1)
                hidden(s, tiles, func, (lambda m: dict(bias=col(s + "_b1", m))) if biased else (lambda m: {}),
                       s + "_weighted")

            def rows_broadcast(layer, first, heads=2):
                for h in range(first, first + heads):
                    for c, (c0, cn) in enumerate(CH):
                        await_group(act, layer + "_asB", 2 * h + c)
                        if h >= 2:
                            act.wait_ge(*E(layer + "_max_done", NT * (h - 1)))
                        act.activation(asB[:, h % 2, c0:c0 + cn], bank(layer + "_asB", 2 * h + c)[0:TN, 0:cn],
                                       ACT.Copy).then_inc(S(layer + "_asB_read"), 1)

            act.dma_start(t_col[0:TN, :], scalars_in[0:1, :].to_broadcast([TN, 1])).then_inc(S("scalars_loaded"), 16)
            act.dma_start(slot_scale, scalars_in[1:2, :].to_broadcast([P, 1])).then_inc(S("scalars_loaded"), 16)
            fill_bias("g0_bias_full", 0, D)
            act.wait_ge(*E("bn_var", 1))
            act.activation(bn_s, bn_s, ACT.Sqrt).then_inc(S("bn_std"), 1)

            root_of_variance("g0")
            act.wait_ge(*E("scalars_loaded", 32))
            for n in range(NT):
                act.wait_ge(*E("g0_msg", n + 1))
                if n >= 2:
                    act.wait_ge(*E("g0_peaks", n - 1))
                act.activation(logits[:, n % 2], msg[:, n], ACT.Copy, scale=t_col[0:TN, :]).then_inc(S("g0_logits"), 1)
            act.wait_ge(*E("g0_maxB_read", 1))
            for n in range(NT):
                if n >= 2:
                    act.wait_ge(*E("g0_exp_low", n - 1))
                act.activation(e_full[n % 2][:], msg[:, n], ACT.Exp, bias=peak_all[0:TN, 1:2], scale=t_col[0:TN, :]
                               ).then_inc(S("g0_exp"), 1)
                act.wait_ge(*E("g0_exp", n + 1))
                act.activation(e_hi[:, n], e_full[n % 2][:], ACT.Copy).then_inc(S("g0_exp_high"), 1)
                act.wait_ge(*E("g0_num_full", n + 1))
                act.activation(nm_hi[:, n, 0:D], msg[:, n], ACT.Copy).then_inc(S("g0_num_high"), 1)
                if n:
                    counts("A", adj, n - 1)
            counts("A", adj, NT - 1)
            second_half("A", adj)
            act.wait_ge(*E("cols_loaded", 16))
            act.activation(gate_hi[:], cols[:, COLS["f0_gate"][0]:COLS["f3_gate"][1]], ACT.Copy
                           ).then_inc(S("gates_high"), 1)
            act.wait_ge(*E("g0_num_low", NT))
            for i in range(2 * NT):
                n, (a, b) = i // 2, ((0, 4), (4, KD))[i % 2]
                await_group(act, "g0_xT", i)
                act.activation(xT_full[:, a:b, n * TN:(n + 1) * TN],
                               bank("g0_xT", i)[:, 0:(b - a) * TN].rearrange("p (k n) -> p k n", n=TN),
                               ACT.Copy).then_inc(S("g0_xT_copied"), 1)
            for j in range(2 * KD + 1):
                if j < 2 * KD:
                    cn = CH[j // KD][1]
                    await_group(act, "g0_den", j)
                    if j >= 2:
                        act.wait_ge(*E("g0_num_read", j - 1))
                    act.activation(tmp[:, 2 + j % 2, 0:cn], bank("g0_den", j)[:, 0:cn], ACT.Identity, bias=tiny
                                   ).then_inc(S("g0_den_read"), 1)
                if j:
                    c0, cn = CH[(j - 1) // KD]
                    act.wait_ge(*E("g0_sum", j))
                    act.activation(xT_hi[:, (j - 1) % KD, c0:c0 + cn], tmp[:, (j - 1) % 2, 0:cn], ACT.Copy
                                   ).then_inc(S("g0_out_high"), 1)
            act.wait_ge(*E("g1_deg_ready", 1))
            act.activation(dinv[0:TN], dinv[0:TN], ACT.Sqrt).then_inc(S("g1_dinv"), 1)
            act.wait_ge(*E("g0_residual", NT))
            hidden("g0", 12, ACT.Relu, lambda m: dict(scale=bn_s[:, m:m + 1], bias=bn_b[:, m:m + 1]), "g0_activated")
            act.wait_ge(*E("f0_rows_clear", 1))
            fill_pairs("f0_bias_full", 0)
            expert_layer("f0", 12, ACT.Gelu, True)
            act.wait_ge(*E("f0_x", 2 * NT))
            fill_bias("g1_bias_full", 2, D)
            root_of_variance("g1")
            nodes_high("g1_xn", D, xn, "g1_nodes_high")
            act.wait_ge(*E("g1_bias_used", 1))
            fill_bias("g1b_bias_full", 1, D)
            messages_high("g1a", "g1a_agg", KD)
            for i in range(2 * NT):
                n, c = i % NT, i // NT
                act.wait_ge(*E("g1a_full", i + 1))
                act.activation(nm_hi[:, n, c * 384:(c + 1) * 384], xn[:, n, c * 384:(c + 1) * 384], ACT.Copy
                               ).then_inc(S("g1b_nodes_high"), 1)
            fill_bias("g2_bias_full", 3, D)
            messages_high("g1b", "g1b_agg", KD)
            expert_layer("f1", 8, ACT.Silu, False)
            act.dma_start(att[:], att_in[0:2, :].unsqueeze(0).to_broadcast([TN, 2, HEADS * HEAD_DIM])
                          ).then_inc(S("g2p_att_full"), 16)
            root_of_variance("g2")
            xT_high("g2_xT", KD)
            for i in range(4 * NT):
                n, c = i % NT, i // NT
                await_group(act, "g2a", i)
                act.activation(h1[:, n, 2 * c:2 * c + 2, 0:HEAD_DIM],
                               bank("g2a", i)[0:TN, 0:256].rearrange("p (h d) -> p h d", h=2), ACT.Copy
                               ).then_inc(S("g2_h1"), 1)
                if n == 2 and c:
                    rows_broadcast("g2p", 2 * c - 2)
            rows_broadcast("g2p", 6)

            def attention(layer, heads):
                act.wait_ge(*E(layer + "_max_done", NT * heads))

                def head_out(h):
                    for i, (a, b) in enumerate(((0, 4), (4, NT))):
                        await_group(act, "g2p_outT", 2 * h + i)
                        if h:
                            act.wait_ge(*E("g2p_low", h))
                        act.activation(head_T[:, a * TN:b * TN], bank("g2p_outT", 2 * h + i)[:, 0:(b - a) * TN],
                                       ACT.Relu, bias=col("g2_b1", h)).then_inc(S("g2p_relu"), 1)
                    act.wait_ge(*E("g2p_relu", 2 * h + 2))
                    act.activation(hT_hi[:, h, 0:NODES], head_T[:], ACT.Copy).then_inc(S("g2p_high"), 1)

                def logit_parts(h):
                    for i in range(4):
                        c0, cn = CH[i % 2]
                        await_group(act, layer + "_uvB", 4 * h + i)
                        act.activation(uB[h % 2][:, i // 2, c0:c0 + cn], bank(layer + "_uvB", 4 * h + i)[0:TN, 0:cn],
                                       ACT.Copy).then_inc(S(layer + "_uvB_read"), 1)

                for h in range(heads + (3 if layer == "g2p" else 0)):
                    if h < heads:
                        logit_parts(h)
                        act.wait_ge(*E(layer + "_uvB_read", 4 * h + 4))
                        if h >= 2:
                            await_group(act, "g2p_agg", 2 * (h - 2) + 1)
                        for s in range(NT):
                            act.activation(prob[h % 2][:, s], uB[h % 2][:, 0], ACT.Identity,
                                           bias=a_src[0:TN, 8 * s + h:8 * s + h + 1]).then_inc(S(layer + "_shift"), 1)
                        for s in range(NT):
                            act.wait_ge(*E(layer + "_leaky", NT * h + s + 1))
                            act.activation(prob[h % 2][:, s], prob[h % 2][:, s], ACT.Exp).then_inc(S(layer + "_powers"), 1)
                    if h >= 3:
                        head_out(h - 3)

            attention("g2p", HEADS)
            act.wait_ge(*E("g2p_scores", 8 * 2 * NT))
            act.dma_start(att[:, :, 0:D], att_in[2:4, 0:D].unsqueeze(0).to_broadcast([TN, 2, D])
                          ).then_inc(S("g2q_att_full"), 16)
            for i in range(2 * NT):
                n, c = i % NT, i // NT
                await_group(act, "g2b", i)
                act.activation(h2[:, n, c * 384:(c + 1) * 384], bank("g2b", i)[0:TN, 0:384], ACT.Copy
                               ).then_inc(S("g2_h2"), 1)
            rows_broadcast("g2q", 0, 1)
            attention("g2q", 1)
            act.wait_ge(*E("slots_squared", 1))
            act.activation(slot_sum, slot_sum, ACT.Sqrt).then_inc(S("slots_norm"), 1)
            act.wait_ge(*E("g2_bias_used", 1))
            act.dma_start(bias8[0:8, :], rows_in[8:16, :]).then_inc(S("f2_bias_full"), 16)
            root_of_variance("f2")
            for n in range(NT):
                act.wait_ge(*E("f2_xn", n + 1))
                if n:
                    act.wait_ge(*E("f2_squared", n))
                act.activation(f2_junk[:], xn[:, n], ACT.Square, accum_out=sum8[0:TN, n:n + 1]
                               ).then_inc(S("f2_squared"), 1)
            act.wait_ge(*E("f2_squared", NT))
            act.activation(sum8[0:TN], sum8[0:TN], ACT.Sqrt).then_inc(S("f2_norm"), 1)
            xT_high("f2_xT", KD)
            act.wait_ge(*E("slots_split", 1))
            act.dma_start(node_type_i[:], types_in.to_broadcast([RELS, NODES])).then_inc(S("types_loaded"), 16)
            act.dma_start(emb[:], emb_in).then_inc(S("emb_loaded"), 16)
            act.wait_ge(*E("f2_rows_shifted", 1))
            act.activation(combine[:], combine[:], ACT.Exp).then_inc(S("f2_row_exp"), 1)
            act.wait_ge(*E("f2_column_peak", 1))
            await_group(act, "f2_logits", 0)
            act.activation(logitsT[:, 0:NODES], logitsT[:, 0:NODES], ACT.Exp, bias=row_peak[:],
                           accum_out=row_sum[:]).then_inc(S("f2_column_exp"), 1)
            act.wait_ge(*E("f2_hidden_read", 1))
            act.wait_ge(*E("f2_diag_clear", 1))
            act.activation(hidden_diag[:].rearrange("p (e s) -> p e s", s=36)[:, :, 0:4], slot_hidden[:], ACT.Gelu
                           ).then_inc(S("f2_diag"), 1)
            act.wait_ge(*E("f2_up_read", 2))
            fill_bias("g3a_bias_full", 4, D1)
            root_of_variance("g3")
            act.wait_ge(*E("g3_emb_low", NT))
            nodes_high("g3_xn", D1, acc, "g3a_nodes_high")
            for r in range(RELS - 1):
                for span in range(SPANS):
                    counts(f"R{r}", rel[:, r], span)
                second_half(f"R{r}", rel[:, r])
            for key, k, full in (("g3a", K1, "g3_xn"), ("g3b", K1, "g3b_nodes"), ("g3c", KD, "g3c_nodes")):
                xT_high(key + "_hT", k)
                if key != "g3a":
                    nodes_high(full, k * P, acc, key + "_nodes_high", NT)
                for r in range(RELS):
                    messages_high(key, f"{key}_agg{r}", k)
                if key == "g3a":
                    act.wait_ge(*E("g3a_acc", 2 * NT))
                    fill_bias("g3b_bias_full", 5, D)
                elif key == "g3b":
                    act.wait_ge(*E("g3b_acc", 2 * NT))
                    fill_bias("g3c_bias_full", 6, D)
            def fill_rows():
                act.wait_ge(*E("f3_rows_clear", 1))
                fill_pairs("f3_bias_full", 16)

            expert_layer("f3", 12, ACT.Gelu_apprx_tanh, True, fill_rows)

        @block.vector
        def _(dve):
            done = [0]

            def link(ins):
                done[0] += 1
                ins.then_inc(S("dve_step"), 1)
                dve.wait_ge(*E("dve_step", done[0]))

            TT, TS, STT = dve.tensor_tensor, dve.tensor_scalar, dve.scalar_tensor_tensor

            def node_stats(n, c):
                return dve.bn_stats(stats[0:TN, 12 * n + 6 * c:12 * n + 6 * c + 6], x[:, n, c * 384:(c + 1) * 384])

            def layer_norm(s, dst, measured=False, factor=None):
                if not measured:
                    for n in range(NT):
                        for c in range(2):
                            last = node_stats(n, c)
                    link(last)
                for n in range(NT):
                    last = dve.bn_aggr(moments[0:TN, 2 * n:2 * n + 2], stats[0:TN, 12 * n:12 * n + 12])
                link(last)
                TS(rstd[0:TN], moments[0:TN].rearrange("p (n k) -> p n k", k=2)[:, :, 1], LN_EPS, None, ALU.add
                   ).then_inc(S(s + "_var"), 1)
                dve.wait_ge(*E(s + "_std", 1))
                link(dve.reciprocal(rstd[0:TN], rstd[0:TN]))
                if factor is not None:
                    link(TT(rstd[0:TN], rstd[0:TN], factor[0:TN], ALU.mult))
                for n in range(NT):
                    TS(dst(n), x[:, n], moments[0:TN, 2 * n:2 * n + 1], rstd[0:TN, n:n + 1], ALU.subtract, ALU.mult
                       ).then_inc(S(s + "_xn"), 1)

            def add_bias(s):
                for n in range(NT):
                    last = TT(x[:, n], x[:, n], bias[:, 0:D], ALU.add)
                last.then_inc(S(s + "_bias_used"), 1)
                dve.wait_ge(*E(s + "_bias_used", 1))

            def clear_pad(name):
                dve.memset(f(xT_hi[:, :, NODES:NP]), 0.0).then_inc(S(name), 1)
                dve.memset(f(xT_lo[:, :, NODES:NP]), 0.0).then_inc(S(name), 1)

            def xT_low_half(label, k):
                clear_pad(label + "_pad")
                for i in range(2 * NT):
                    n, (a, b) = i // 2, ((0, 4), (4, k))[i % 2]
                    at = slice(n * TN, (n + 1) * TN)
                    dve.wait_ge(*E(label + "_high", i + 1))
                    TT(xT_lo[:, a:b, at], bank(label, i)[:, 0:(b - a) * TN].rearrange("p (k n) -> p k n", n=TN),
                       f(xT_hi[:, a:b, at]), ALU.subtract).then_inc(S(label + "_low"), 1)

            def nodes_low(width, src, high, low):
                for n in range(NT):
                    dve.wait_ge(*E(high, n + 1))
                    TT(nm_lo[:, n, 0:width], src[:, n, 0:width], f(nm_hi[:, n, 0:width]), ALU.subtract
                       ).then_inc(S(low), 1)

            def split_destinations(before):
                link(TS(dst_adds[:], edge[:, 1], float(HALF), None, ALU.is_ge))
                TS(dst_place[:], dst_adds[:], -float(HALF), None, ALU.mult).then_inc(S("dst_split"), 1)
                dve.wait_ge(*E("dst_split", before + 1))
                TT(dst_place[:], dst_place[:], edge[:, 1], ALU.add).then_inc(S("dst_split"), 1)
                TS(dst_adds[:], dst_adds[:], FRACTION - 1.0, 1.0, ALU.mult, ALU.add).then_inc(S("dst_split"), 1)
                dve.wait_ge(*E("dst_split", before + 3))

            def one_hots(sweeps, behind=None, behind_first=None):
                def hot(label, source, t, k):
                    TS(src_hot[:, k], iota[:, 0:NODES], source[:, bass.ds(t, 1)], None, ALU.is_equal
                       ).then_inc(S(label + "_hot"), 1)
                    TS(dst_hot[:, k], iota[:, 0:HALF + 1], dst_place[:, bass.ds(t, 1)], dst_adds[:, bass.ds(t, 1)],
                       ALU.is_equal, ALU.mult).then_inc(S(label + "_hot"), 1)

                def settle(label, target, span):
                    for s in range(NT):
                        i = span * NT + s
                        dve.wait_ge(*E(label + "_rounded", i + 1))
                        if span and (span > 1 or label == "R1"):
                            dve.wait_ge(*E(label + "_fraction_added", max(i - 2 * NT + 1, 0)))
                            if span == 1:
                                dve.wait_ge(*E("R0_fraction_summed", NT))
                        dst = fraction_parts[:, s] if span else target[:, s, HALF:NP]
                        STT(dst, rounded[:, s], -ROUNDER, bank(label, i)[0:TN, 0:HALF],
                            ALU.add, ALU.subtract).then_inc(S(label + "_counted"), 1)
                    if span == SPANS - 1:
                        for s in range(NT):
                            dve.wait_ge(*E(label + "_counted", span * NT + s + 1))
                            dve.wait_ge(*E(label + "_fraction_added", (SPANS - 3) * NT + s + 1))
                            TT(target[:, s, HALF:NP], f(target[:, s, HALF:NP]), fraction_parts[:, s], ALU.add
                               ).then_inc(S(label + "_fraction_summed"), 1)
                        for s in range(NT):
                            dve.wait_ge(*E(label + "_whole_added", (SPANS - 3) * NT + s + 1))
                            STT(target[:, s, 0:HALF], rounded[:, s], -ROUNDER, f(target[:, s, 0:HALF]), ALU.add, ALU.add
                                ).then_inc(S(label + "_whole_summed"), 1)

                spans = [(label, source, target, span) for label, source, target in sweeps for span in range(SPANS)]
                for n, (label, source, target, span) in enumerate(spans):
                    first, used = span * SPAN, span * (SPAN - 1)
                    for t in range(OSLOTS):
                        if n:
                            before, last = spans[n - 1][0], spans[n - 1][3]
                            if t < OSLOTS - 1:
                                dve.wait_ge(*E(before + "_hot_used", last * (SPAN - 1) + SPAN - OSLOTS + t + 1))
                            else:
                                await_group(dve, before, last * NT + NT - 1)
                        hot(label, source, first + t, t)
                    if n == 0 and behind_first:
                        behind_first()
                    if n:
                        before, _, its_target, last = spans[n - 1]
                        settle(before, its_target, last)
                        if behind:
                            behind(n)
                    with dve.Fori(1, SPAN // OSLOTS) as q:
                        for k in range(OSLOTS):
                            dve.wait_ge(*E(label + "_hot_used", q * OSLOTS + (k - OSLOTS + 1 + used)))
                            hot(label, source, q * OSLOTS + (first + k), k)
                label, _, target, span = spans[-1]
                settle(label, target, span)
                dve.wait_ge(*E(label + "_fraction_summed", NT))
                dve.wait_ge(*E(label + "_whole_summed", NT))

            def messages_low(key, label, k, first=0):
                for i in range(2 * k):
                    ft, (c0, cn) = i // 2, CH[i % 2]
                    dve.wait_ge(*E(key + "_high", first + i + 1))
                    TT(xT_lo[:, ft, c0:c0 + cn], bank(label, i)[:, 0:cn], f(xT_hi[:, ft, c0:c0 + cn]), ALU.subtract
                       ).then_inc(S(key + "_low"), 1)

            def add_to_nodes(s, label, factor=None, between=None):
                for i in range(2 * NT):
                    n, c = i % NT, i // NT
                    at = slice(c * 384, (c + 1) * 384)
                    await_group(dve, label, i)
                    if factor is None:
                        TT(x[:, n, at], bank(label, i)[0:TN, 0:384], x[:, n, at], ALU.add).then_inc(S(s + "_x"), 1)
                    else:
                        STT(x[:, n, at], bank(label, i)[0:TN, 0:384], factor[0:TN, n:n + 1], x[:, n, at],
                            ALU.mult, ALU.add).then_inc(S(s + "_x"), 1)
                    if i == NT - 1:
                        if between:
                            between()
                        if s != "f3":
                            dve.wait_ge(*E(s + "_x", NT))
                            for m in range(NT):
                                node_stats(m, 0)
                    if c and s != "f3":
                        if n:
                            dve.wait_ge(*E(s + "_x", i))
                            node_stats(n - 1, 1)
                        if n == NT - 1:
                            dve.wait_ge(*E(s + "_x", i + 1))
                            link(node_stats(n, 1))

            def hidden_low(s, tiles, weigh):
                jobs = 2 * tiles
                for j in range(jobs + 1):
                    if j < jobs and weigh:
                        cn = CH[j % 2][1]
                        dve.wait_ge(*E(s + "_activated", j + 1))
                        await_group(dve, s + "_cB", j)
                        TT(tmp[:, j % TSLOTS, 0:cn], tmp[:, j % TSLOTS, 0:cn], bank(s + "_cB", j)[:, 0:cn], ALU.mult
                           ).then_inc(S(s + "_weighted"), 1)
                    if j >= 1:
                        i = j - 1
                        m, c = job_of(s, i)
                        c0, cn = CH[c]
                        dve.wait_ge(*E(s + "_high", i + 1))
                        TT(hT_lo[:, m, c0:c0 + cn], tmp[:, i % TSLOTS, 0:cn], f(hT_hi[:, m, c0:c0 + cn]),
                           ALU.subtract).then_inc(S(s + "_low"), 1)

            def bc(cols8, n=NT):
                return cols8.unsqueeze(2).to_broadcast([TN, n, 8])

            def v8(t):
                return t[0:TN].rearrange("p (n e) -> p n e", e=8)

            def route(s):
                await_group(dve, s + "_router", 0)
                dve.tensor_copy(logit8[0:TN], bank(s + "_router", 0)[0:TN, 0:8 * NT]).then_inc(S(s + "_routed"), 1)
                dve.wait_ge(*E(s + "_routed", 1))
                for n in range(NT):
                    last = dve.max(top8[0:TN, 8 * n:8 * n + 8], logit8[0:TN, 8 * n:8 * n + 8])
                link(last)
                TT(v8(prob8), v8(logit8), v8(top8)[:, :, 0:1].to_broadcast([TN, NT, 8]), ALU.subtract
                   ).then_inc(S(s + "_shifted"), 1)
                for n in range(NT):
                    last = dve.max_index(idx8[0:TN, 8 * n:8 * n + 8], top8[0:TN, 8 * n:8 * n + 8],
                                         logit8[0:TN, 8 * n:8 * n + 8])
                link(last)
                link(dve.tensor_copy(idx8f[0:TN], idx8[0:TN, 0:NT * 8]))
                experts = iota8[0:TN].unsqueeze(1).to_broadcast([TN, NT, 8])
                TT(v8(hot8), experts, v8(idx8f)[:, :, 0:1].to_broadcast([TN, NT, 8]), ALU.is_equal)
                link(TT(v8(logit8), experts, v8(idx8f)[:, :, 1:2].to_broadcast([TN, NT, 8]), ALU.is_equal))
                link(TT(hot8[0:TN], hot8[0:TN], logit8[0:TN], ALU.add))
                dve.wait_ge(*E(s + "_exp", 1))
                link(dve.tensor_reduce(sum8[0:TN], v8(prob8), AX.X, ALU.add))
                link(dve.reciprocal(sum8[0:TN], sum8[0:TN]))
                TT(v8(prob8), v8(prob8), bc(sum8[0:TN]), ALU.mult).then_inc(S(s + "_probs"), 1)
                dve.wait_ge(*E(s + "_probs", 1))
                link(TT(hot8[0:TN], hot8[0:TN], prob8[0:TN], ALU.mult))
                if s == "f1":
                    await_group(dve, "f1_importance", 0)
                    TS(run8[0:TN], bank("f1_importance", 0)[0:TN, 0:8], 1.0, 1.0 - 0.9, ALU.subtract, ALU.mult
                       ).then_inc(S("f1_importance_read"), 1)
                    dve.wait_ge(*E("f1_importance_read", 1))
                    link(TS(run8[0:TN], run8[0:TN], 1.0, 0.01, ALU.add, ALU.add))
                    link(dve.reciprocal(run8[0:TN], run8[0:TN]))
                    link(TT(v8(hot8), v8(hot8), run8[0:TN].unsqueeze(1).to_broadcast([TN, NT, 8]), ALU.mult))
                link(dve.tensor_reduce(sum8[0:TN], v8(hot8), AX.X, ALU.add))
                if s != "f1":
                    link(TS(sum8[0:TN], sum8[0:TN], 1e-9, None, ALU.add))
                link(dve.reciprocal(sum8[0:TN], sum8[0:TN]))
                link(TT(hot8[0:TN].rearrange("p (n e) -> p n e", e=8), v8(hot8), bc(sum8[0:TN]), ALU.mult))
                dve.wait_ge(*E(s + "_cpad_clear", 1))
                dve.tensor_copy(cpad[:].rearrange("p n (q s) -> p n q s", s=32)[:, :, :, 0:2],
                                hot8[0:TN].rearrange("p (n q s) -> p n q s", q=4, s=2)).then_inc(S(s + "_combine"), 1)
                if s != "f1":
                    dve.wait_ge(*E(s + "_bias_full", 64))
                    dve.tensor_copy(bias8_hi[:], bias8[:]).then_inc(S(s + "_rows_split"), 1)
                for n in range(NT):
                    at = slice(n * TN, (n + 1) * TN)
                    await_group(dve, s + "_cT", n)
                    dve.tensor_copy(cT_hi[:, at], bank(s + "_cT", n)[:, 0:TN]).then_inc(S(s + "_cT_high"), 1)
                for n in range(NT):
                    at = slice(n * TN, (n + 1) * TN)
                    dve.wait_ge(*E(s + "_cT_high", n + 1))
                    TT(cT_lo[:, at], bank(s + "_cT", n)[:, 0:TN], f(cT_hi[:, at]), ALU.subtract
                       ).then_inc(S(s + "_combineT"), 1)
                if s != "f1":
                    dve.wait_ge(*E(s + "_rows_split", 1))
                    TT(bias8_lo[:], bias8[:], f(bias8_hi[:]), ALU.subtract).then_inc(S(s + "_rows_split"), 1)

            def expert_layer(s, tiles, measured=True):
                layer_norm(s, lambda n: xn[:, n], measured)
                dve.memset(cpad[:], 0.0).then_inc(S(s + "_cpad_clear"), 1)
                dve.memset(f(cT_hi[:, NODES:NP]), 0.0).then_inc(S(s + "_cT_pad"), 1)
                dve.memset(f(cT_lo[:, NODES:NP]), 0.0).then_inc(S(s + "_cT_pad"), 1)
                xT_low_half(s + "_xT", KD)
                if s == "f3":
                    dve.memset(bias8[:], 0.0).then_inc(S("f3_rows_clear"), 1)
                route(s)
                hidden_low(s, tiles, True)
                add_to_nodes(s, s + "_down")

            for n in range(NT):
                dve.wait_ge(*E(f"x_loaded{n}", 16))
                for c in range(2):
                    last = node_stats(n, c)
            link(last)
            dve.wait_ge(*E("cols_loaded", 16))
            TS(bn_s, col("bn_var"), 1e-5, None, ALU.add).then_inc(S("bn_var"), 1)
            layer_norm("g0", lambda n: xn[:, n], True)
            for n in range(NT):
                dve.wait_ge(*E("g0_xn", n + 1))
                TS(msg[:, n], xn[:, n], 0.0, 1e-7, ALU.max, ALU.add).then_inc(S("g0_msg"), 1)
            dve.wait_ge(*E("consts", 21))
            dve.tensor_copy(iota8, idx8[:, 0:8])
            dve.tensor_copy(rel_index, idx8[:, 8:9])
            dve.memset(tiny, 1e-30)
            dve.memset(rounder, ROUNDER)
            dve.memset(unrounder, -ROUNDER)
            dve.wait_ge(*E("edges_loaded", 16))
            link(dve.tensor_copy(edge[:], e_int[:]))
            for n in range(NT):
                dve.wait_ge(*E("g0_logits", n + 1))
                last = dve.tensor_reduce(peak[0:TN, n:n + 1], logits[:, n % 2], AX.X, ALU.max)
                last.then_inc(S("g0_peaks"), 1)
            dve.wait_ge(*E("g0_peaks", NT))
            dve.tensor_reduce(peak[0:TN, 5:6], peak[0:TN, 0:NT], AX.X, ALU.max).then_inc(S("g0_peak"), 1)
            await_group(dve, "g0_maxT", 0)
            dve.tensor_reduce(peak_all[0:1, 0:1], bank("g0_maxT", 0)[0:1, 0:TN], AX.X, ALU.max
                              ).then_inc(S("g0_max_read"), 1)
            await_group(dve, "g0_maxB", 0)
            TS(peak_all[0:TN, 1:2], bank("g0_maxB", 0)[0:TN, 0:1], -1.0, None, ALU.mult
               ).then_inc(S("g0_maxB_read"), 1)
            split_destinations(0)
            one_hots([("A", edge[:, 0], adj)])
            dve.wait_ge(*E("gates_high", 1))
            TT(gate_lo[:], cols[:, COLS["f0_gate"][0]:COLS["f3_gate"][1]], f(gate_hi[:]), ALU.subtract
               ).then_inc(S("gates_split"), 1)
            dve.wait_ge(*E("bn_std", 1))
            link(dve.reciprocal(bn_s, bn_s))
            TT(bn_b, col("bn_b1"), col("bn_mean"), ALU.subtract)
            link(TT(bn_s, bn_s, col("bn_gamma"), ALU.mult))
            link(TT(bn_b, bn_b, bn_s, ALU.mult))
            TT(bn_b, bn_b, col("bn_beta"), ALU.add).then_inc(S("bn_ready"), 1)
            await_group(dve, "A", SPANS * NT - 1)
            dve.memset(f(xT_hi[:, :, NODES:NP]), 0.0).then_inc(S("g0_xT_pad"), 1)
            dve.wait_ge(*E("g0_num_low", NT))
            dve.memset(xT_full[:, :, NODES:NP], 0.0).then_inc(S("g0_xT_pad"), 1)
            dve.wait_ge(*E("g0_xT_pad", 2))
            dve.wait_ge(*E("g0_xT_copied", 2 * NT))
            for j in range(2 * KD + 1):
                if j < 2 * KD:
                    (c0, cn), ft = CH[j // KD], j % KD
                    at, T, R = slice(c0, c0 + cn), tmp[:, j % 2, 0:cn], tmp[:, 2 + j % 2, 0:cn]
                    dve.wait_ge(*E("g0_den_read", j + 1))
                    link(dve.reciprocal(R, R))
                    TT(T, bank("g0_num", j)[:, 0:cn], R, ALU.mult).then_inc(S("g0_num_read"), 1)
                    dve.wait_ge(*E("g0_num_read", j + 1))
                    TT(T, T, xT_full[:, ft, at], ALU.add).then_inc(S("g0_sum"), 1)
                if j >= 1:
                    i = j - 1
                    (c0, cn), ft = CH[i // KD], i % KD
                    dve.wait_ge(*E("g0_out_high", i + 1))
                    TT(xT_lo[:, ft, c0:c0 + cn], tmp[:, i % 2, 0:cn], f(xT_hi[:, ft, c0:c0 + cn]), ALU.subtract
                       ).then_inc(S("g0_out_low"), 1)
            await_group(dve, "g1_deg", 0)
            TS(dinv[0:TN], bank("g1_deg", 0)[0:TN, 0:2 * NT].rearrange("p (n k) -> p n k", k=2)[:, :, 0], 1.0, None,
               ALU.add).then_inc(S("g1_deg_read"), 1)
            dve.wait_ge(*E("g1_deg_read", 1))
            dve.reciprocal(dinv[0:TN], dinv[0:TN]).then_inc(S("g1_deg_ready"), 1)
            for s in range(NT):
                at = slice(s * TN, (s + 1) * TN)
                TT(adj[:, s, at], f(adj[:, s, at]), ident[0:TN, 0:TN], ALU.add).then_inc(S("self_loops"), 1)
            dve.wait_ge(*E("g0_residual", 2 * NT))
            dve.memset(bias8[:], 0.0).then_inc(S("f0_rows_clear"), 1)
            hidden_low("g0", 12, False)
            add_to_nodes("g0", "g0d")
            expert_layer("f0", 12)

            dve.wait_ge(*E("g1_dinv", 1))
            layer_norm("g1", lambda n: xn[:, n], True, dinv)
            nodes_low(D, xn, "g1_nodes_high", "g1_nodes_low")
            dve.wait_ge(*E("g1_bias_full", 16))
            add_bias("g1")
            messages_low("g1a", "g1a_agg", KD)
            dve.wait_ge(*E("g1b_bias_full", 16))
            for i in range(2 * NT + 1):
                if i < 2 * NT:
                    n, c = i % NT, i // NT
                    at = slice(c * 384, (c + 1) * 384)
                    await_group(dve, "g1a", i)
                    STT(xn[:, n, at], bank("g1a", i)[0:TN, 0:384], dinv[0:TN, n:n + 1], bias[:, at],
                        ALU.mult, ALU.add).then_inc(S("g1a_read"), 1)
                    dve.wait_ge(*E("g1a_read", i + 1))
                    TS(xn[:, n, at], xn[:, n, at], 0.0, dinv[0:TN, n:n + 1], ALU.max, ALU.mult
                       ).then_inc(S("g1a_full"), 1)
                if i >= 1:
                    n, c = (i - 1) % NT, (i - 1) // NT
                    at = slice(c * 384, (c + 1) * 384)
                    dve.wait_ge(*E("g1b_nodes_high", i))
                    TT(nm_lo[:, n, at], xn[:, n, at], f(nm_hi[:, n, at]), ALU.subtract).then_inc(S("g1b_nodes_low"), 1)
            messages_low("g1b", "g1b_agg", KD)
            await_group(dve, "g1b_agg", 2 * KD - 1)
            for s in range(NT):
                at = slice(s * TN, (s + 1) * TN)
                TT(adj[:, s, at], f(adj[:, s, at]), ident[0:TN, 0:TN], ALU.subtract).then_inc(S("no_self_loops"), 1)
            dve.memset(maskT[:, :, NODES:NP], FAR)

            def edge_mask():
                for i in range(2 * NT):
                    d, (a, b) = i // 2, ((0, 4), (4, NT))[i % 2]
                    await_group(dve, "g2_maskT", i)
                    TS(maskT[:, d, a * TN:b * TN], bank("g2_maskT", i)[0:TN, 0:(b - a) * TN], 0.0, FAR,
                       ALU.is_equal, ALU.mult).then_inc(S("g2_masked"), 1)

            add_to_nodes("g1", "g1b", dinv, edge_mask)
            expert_layer("f1", 8)

            layer_norm("g2", lambda n: xn[:, n], True)
            dve.tensor_copy(head_sel[:], ident[0:8, 0:8].unsqueeze(2).to_broadcast([8, 8, P])).then_inc(S("head_sel"), 1)
            dve.memset(asT[:, NODES:NP], 0.0).then_inc(S("asT_pad"), 1)
            dve.memset(h1[:, :, :, HEAD_DIM:HD], 1.0).then_inc(S("h1_ones"), 1)
            xT_low_half("g2_xT", KD)
            dve.wait_ge(*E("g2_bias_full", 16))
            add_bias("g2")
            dve.wait_ge(*E("g2_masked", 2 * NT))
            link(dve.tensor_reduce(no_edge[0:TN], maskT[:], AX.X, ALU.max))
            dve.wait_ge(*E("g2p_att_full", 16))

            def greatest_scores(layer, h):
                dve.wait_ge(*E(layer + "_asB_read", 2 * h + 2))
                for d in range(NT):
                    made = NT * h + d
                    if made >= 2:
                        dve.wait_ge(*E(layer + "_max_done", made - 1))
                    dve.tensor_tensor_reduce(edge_scores[made % 2][:], asB[:, h % 2], maskT[:, d], 1.0, -3e38,
                                             ALU.add, ALU.max, a_max[0:TN, 8 * d + h:8 * d + h + 1]
                                             ).then_inc(S(layer + "_max_done"), 1)

            def read_source_rows(layer, c):
                for i, (a, b) in enumerate(((0, 4), (4, NT))):
                    await_group(dve, layer + "_asT", 2 * c + i)
                    dve.tensor_copy(asT[:, a * TN:b * TN], bank(layer + "_asT", 2 * c + i)[0:2, 0:(b - a) * TN]
                                    ).then_inc(S(layer + "_asT_read"), 1)

            for c in range(5):
                for n in range(NT):
                    i = c * NT + n
                    if c < 4:
                        dve.wait_ge(*E("g2_h1", i + 1))
                        for h in (2 * c, 2 * c + 1):
                            for kind, dst in ((0, a_src), (1, a_dst)):
                                made = 4 * i + 2 * (h % 2) + kind
                                if made >= 4:
                                    dve.wait_ge(*E("g2p_scores", made - 3))
                                dve.tensor_tensor_reduce(
                                    junk[:, kind * 256 + (h % 2) * 128:kind * 256 + (h % 2) * 128 + 128],
                                    h1[:, n, h, 0:HEAD_DIM], att[:, kind, h * HEAD_DIM:(h + 1) * HEAD_DIM], 1.0, 0.0,
                                    ALU.mult, ALU.add, dst[0:TN, 8 * n + h:8 * n + h + 1]).then_inc(S("g2p_scores"), 1)
                    if c and n == 1:
                        read_source_rows("g2p", c - 1)
                        if c > 1:
                            greatest_scores("g2p", 2 * c - 3)
                    if c and n == 3:
                        greatest_scores("g2p", 2 * c - 2)
            greatest_scores("g2p", HEADS - 1)
            dve.wait_ge(*E("g2p_scores", 8 * 2 * NT))

            def attention(layer, heads):
                dve.memset(uT[:, NODES:NP], 0.0).then_inc(S(layer + "_pads"), 1)
                dve.memset(vT[:, NODES:NP], 0.0).then_inc(S(layer + "_pads"), 1)
                TS(a_src5[0:TN], a_src[0:TN], 0.2, None, ALU.mult)
                dve.wait_ge(*E(layer + "_max_done", NT * heads))
                link(TT(v8(a_max), v8(a_max), bc(no_edge[0:TN]), ALU.subtract))
                link(TT(a_max[0:TN], a_max[0:TN], a_dst[0:TN], ALU.add))
                link(STT(hot8[0:TN], a_max[0:TN], 0.2, a_max[0:TN], ALU.mult, ALU.max))
                TT(uv[:, 0].rearrange("p n e -> p (n e)"), a_dst[0:TN], hot8[0:TN], ALU.subtract
                   ).then_inc(S(layer + "_uv"), 1)
                STT(uv[:, 1].rearrange("p n e -> p (n e)"), a_dst[0:TN], 0.2, hot8[0:TN], ALU.mult, ALU.subtract
                    ).then_inc(S(layer + "_uv"), 1)
                for i in range(4):
                    dst, (a, b) = (uT, vT)[i // 2], ((0, 4), (4, NT))[i % 2]
                    await_group(dve, layer + "_uvT", i)
                    dve.tensor_copy(dst[:, a * TN:b * TN], bank(layer + "_uvT", i)[0:8, 0:(b - a) * TN]
                                    ).then_inc(S(layer + "_uvT_read"), 1)

                def head_mean(h):
                    parts = ((0, 3), (3, NT))
                    total = prob8[0:TN, NT * h:NT * h + NT]

                    def sums(i):
                        a, b = parts[i]
                        return bank("g2p_agg", 2 * h + i)[0:TN, 0:(b - a) * (HEAD_DIM + 1)].rearrange(
                            "p (n d) -> p n d", d=HEAD_DIM + 1)

                    for i, (a, b) in enumerate(parts):
                        await_group(dve, "g2p_agg", 2 * h + i)
                        TS(total[:, a:b], sums(i)[:, :, HEAD_DIM], 1e-16, None, ALU.add).then_inc(S("g2p_sum"), 1)
                    dve.wait_ge(*E("g2p_sum", 2 * h + 2))
                    link(dve.reciprocal(total, total))
                    if h >= 2:
                        await_group(dve, "g2p_outT", 2 * (h - 2) + 1)
                    for i, (a, b) in enumerate(parts):
                        TT(mean[:, h % 2, a:b], sums(i)[:, :, 0:HEAD_DIM],
                           total[:, a:b].unsqueeze(2).to_broadcast([TN, b - a, HEAD_DIM]), ALU.mult
                           ).then_inc(S("g2p_mean"), 1)

                def head_low(h):
                    dve.wait_ge(*E("g2p_high", h + 1))
                    TT(hT_lo[:, h, 0:NODES], head_T[:], f(hT_hi[:, h, 0:NODES]), ALU.subtract).then_inc(S("g2p_low"), 1)

                for h in range(heads + (4 if layer == "g2p" else 0)):
                    if 2 <= h < heads + 2:
                        head_mean(h - 2)
                    if h < heads:
                        pr = prob[h % 2]
                        for s in range(NT):
                            dve.wait_ge(*E(layer + "_shift", NT * h + s + 1))
                            STT(pr[:, s], uB[h % 2][:, 1], a_src5[0:TN, 8 * s + h:8 * s + h + 1], pr[:, s],
                                ALU.add, ALU.max).then_inc(S(layer + "_leaky"), 1)
                        for s in range(NT):
                            dve.wait_ge(*E(layer + "_powers", NT * h + s + 1))
                            STT(pr[:, s], pr[:, s], 3.0, f(adj[:, s]), ALU.min, ALU.mult).then_inc(S(layer + "_prob"), 1)
                    if h >= 4:
                        head_low(h - 4)

            attention("g2p", HEADS)
            dve.wait_ge(*E("g2q_att_full", 16))
            dve.memset(a_src[0:TN], 0.0)
            link(dve.memset(a_dst[0:TN], 0.0))
            for i in range(2 * NT):
                n, c = i % NT, i // NT
                at = slice(c * 384, (c + 1) * 384)
                dve.wait_ge(*E("g2_h2", i + 1))
                for kind in range(2):
                    if i:
                        dve.wait_ge(*E("h2_scores", 2 * i + kind - 1))
                    dve.tensor_tensor_reduce(junk[:, kind * 384:kind * 384 + 384], h2[:, n, at],
                                                    att[:, kind, at], 1.0, 0.0, ALU.mult, ALU.add,
                                                    a_part[0:TN, (c * 2 + kind) * NT + n:(c * 2 + kind) * NT + n + 1]
                                             ).then_inc(S("h2_scores"), 1)
            dve.wait_ge(*E("h2_scores", 4 * NT))
            dve.memset(h2[:, :, D:D + 2], 1.0).then_inc(S("h2_ones"), 1)
            for kind, dst in ((0, a_src), (1, a_dst)):
                last = TT(v8(dst)[:, :, 0], a_part[0:TN, kind * NT:(kind + 1) * NT],
                          a_part[0:TN, (2 + kind) * NT:(3 + kind) * NT], ALU.add)
                last.then_inc(S("g2q_scores"), 1)
            dve.wait_ge(*E("g2q_scores", 2))
            read_source_rows("g2q", 0)
            greatest_scores("g2q", 0)
            attention("g2q", 1)
            def kp(t):
                return t.rearrange("d (k p) -> d k p", k=KD)

            slots = col("slots").rearrange("d (k n p) -> d k n p", k=KD, n=EXPERTS)
            link(TT(sp_tmp[:], col("slots").rearrange("d (k s) -> d k s", k=KD),
                    col("slots").rearrange("d (k s) -> d k s", k=KD), ALU.mult))
            dve.tensor_reduce(kp(slot_sum), sp_tmp[:].rearrange("d k (n p) -> d k p n", n=EXPERTS), AX.X, ALU.add
                              ).then_inc(S("slots_squared"), 1)
            dve.wait_ge(*E("slots_norm", 1))
            link(TS(slot_sum, slot_sum, 1e-6, None, ALU.add))
            link(dve.reciprocal(slot_sum, slot_sum))
            for n in range(EXPERTS):
                last = TT(sp_tmp[:].rearrange("d k (n p) -> d k n p", n=EXPERTS)[:, :, n], slots[:, :, n],
                          kp(slot_sum), ALU.mult)
            link(last)
            link(TS(sp_tmp[:], sp_tmp[:], slot_scale, None, ALU.mult))
            link(dve.tensor_copy(sp_hi[:], sp_tmp[:]))
            TT(sp_lo[:], sp_tmp[:], f(sp_hi[:]), ALU.subtract).then_inc(S("slots_split"), 1)
            for n in range(NT):
                for i, at, cn in ((2 * n, slice(384, D), 384), (2 * n + 1, slice(0, 384), 384)):
                    await_group(dve, "g2q_agg", i)
                    if i % 2 == 0:
                        link(TS(sum8[0:TN, n:n + 1], bank("g2q_agg", i)[0:TN, 384:385], 1e-16, None, ALU.add))
                        link(dve.reciprocal(sum8[0:TN, n:n + 1], sum8[0:TN, n:n + 1]))
                    STT(x[:, n, at], bank("g2q_agg", i)[0:TN, 0:cn], sum8[0:TN, n:n + 1], x[:, n, at],
                        ALU.mult, ALU.add).then_inc(S("g2_x"), 1)
                dve.wait_ge(*E("g2_x", 2 * n + 2))
                node_stats(n, 0)
                last = node_stats(n, 1)
            link(last)

            clear_pad("f2_xT_pad")
            layer_norm("f2", lambda n: xn[:, n], True)
            dve.wait_ge(*E("f2_xn", NT))
            dve.wait_ge(*E("f2_norm", 1))
            link(TS(sum8[0:TN], sum8[0:TN], 1e-6, None, ALU.add))
            link(dve.reciprocal(sum8[0:TN], sum8[0:TN]))
            for n in range(NT):
                TS(xn[:, n], xn[:, n], sum8[0:TN, n:n + 1], None, ALU.mult).then_inc(S("f2_unit"), 1)
            for i in range(2 * NT):
                n, (a, b) = i // 2, ((0, 4), (4, KD))[i % 2]
                at = slice(n * TN, (n + 1) * TN)
                dve.wait_ge(*E("f2_xT_high", i + 1))
                TT(xT_lo[:, a:b, at], bank("f2_xT", i)[:, 0:(b - a) * TN].rearrange("p (k n) -> p k n", n=TN),
                   f(xT_hi[:, a:b, at]), ALU.subtract).then_inc(S("f2_xT_low"), 1)
            for c, (c0, cn) in enumerate(CH):
                await_group(dve, "f2_logitsT", c)
                dve.tensor_copy(logitsT[:, c0:c0 + cn], bank("f2_logitsT", c)[0:SLOTS, 0:cn]
                                ).then_inc(S("f2_logitsT_read"), 1)
            dve.wait_ge(*E("f2_logitsT_read", 2))
            dve.tensor_reduce(row_peak[:], logitsT[:, 0:NODES], AX.X, ALU.max, negate=True
                              ).then_inc(S("f2_column_peak"), 1)
            await_group(dve, "f2_logits", 0)
            dve.tensor_copy(slot_logits[:].rearrange("p n s -> p (n s)"), bank("f2_logits", 0)[0:TN, 0:NT * SLOTS]
                            ).then_inc(S("f2_logits_read"), 1)
            dve.wait_ge(*E("f2_logits_read", 1))
            link(dve.tensor_reduce(col_peak[:], slot_logits[:], AX.X, ALU.max))
            TT(combine[:], slot_logits[:], col_peak[:].unsqueeze(2).to_broadcast([TN, NT, SLOTS]), ALU.subtract
               ).then_inc(S("f2_rows_shifted"), 1)
            dve.wait_ge(*E("f2_row_exp", 1))
            link(dve.tensor_reduce(col_sum[:], combine[:], AX.X, ALU.add))
            link(dve.reciprocal(col_sum[:], col_sum[:]))
            TT(combine[:], combine[:], col_sum[:].unsqueeze(2).to_broadcast([TN, NT, SLOTS]), ALU.mult
               ).then_inc(S("f2_combine"), 1)
            dve.wait_ge(*E("f2_column_exp", 1))
            link(dve.reciprocal(row_sum[:], row_sum[:]))
            TS(logitsT[:, 0:NODES], logitsT[:, 0:NODES], row_sum[:], None, ALU.mult).then_inc(S("f2_dispatchT"), 1)
            await_group(dve, "f2_dispatch", 0)
            dve.tensor_copy(dispatch[:].rearrange("p n s -> p (n s)"), bank("f2_dispatch", 0)[0:TN, 0:NT * SLOTS]
                            ).then_inc(S("f2_dispatch_read"), 1)
            for i, (a, b) in enumerate(((0, 4), (4, NT))):
                await_group(dve, "f2_combineT", i)
                dve.tensor_copy(combineT[:, a * TN:b * TN], bank("f2_combineT", i)[0:SLOTS, 0:(b - a) * TN]
                                ).then_inc(S("f2_combineT_read"), 1)
            await_group(dve, "f2_tilde", 0)
            dve.tensor_copy(tildeT[:].rearrange("p k s -> p (k s)"), bank("f2_tilde", 0)[:, 0:KD * SLOTS]
                            ).then_inc(S("f2_tilde_read"), 1)
            dve.memset(hidden_diag[:], 0.0).then_inc(S("f2_diag_clear"), 1)
            dve.wait_ge(*E("types_loaded", 16))
            TS(type_hot[:], node_type_i[:], rel_index[0:RELS], None, ALU.is_equal).then_inc(S("type_hot"), 1)
            link(dve.tensor_copy(types[:], edge[:, 2]))
            TS(src_plus[:], edge[:, 0], 1.0, None, ALU.add)
            for r in range(RELS - 1):
                last = TS(rel_source[:, r], types[:], float(r), None, ALU.is_equal)
            link(last)
            for r in range(RELS - 1):
                last = TT(rel_source[:, r], rel_source[:, r], src_plus[:], ALU.mult)
            link(last)
            for r in range(RELS - 1):
                last = TS(rel_source[:, r], rel_source[:, r], -1.0, None, ALU.add)
            link(last)
            split_destinations(3)
            await_group(dve, "f2_hidden", 0)
            TT(slot_hidden[:], bank("f2_hidden", 0)[0:SLOT_H, 0:SLOTS].rearrange("p (e s) -> p e s", s=4),
               col("b_down")[0:SLOT_H].unsqueeze(2).to_broadcast([SLOT_H, 8, 4]), ALU.add
               ).then_inc(S("f2_hidden_read"), 1)
            for n in range(NT):
                await_group(dve, "g3_emb", n)
                dve.tensor_copy(acc[:, n, D:D1], bank("g3_emb", n)[0:TN, 0:TYPE_DIM]).then_inc(S("g3_emb_low"), 1)
            for c in range(2):
                await_group(dve, "f2_up", c)
                dve.tensor_copy(slot_out[:, c * 384:(c + 1) * 384], bank("f2_up", c)[0:SLOTS, 0:384]
                                ).then_inc(S("f2_up_read"), 1)
            add_to_nodes("f2", "f2_down")


            def low_nodes(n):
                if n <= NT:
                    dve.wait_ge(*E("g3a_nodes_high", n))
                    TT(nm_lo[:, n - 1], acc[:, n - 1], f(nm_hi[:, n - 1]), ALU.subtract).then_inc(S("g3a_nodes_low"), 1)

            one_hots([(f"R{r}", rel_source[:, r], rel[:, r]) for r in range(RELS - 1)], low_nodes,
                     lambda: layer_norm("g3", lambda n: acc[:, n, 0:D], True))
            def degrees(r):
                inv = rel_inv[0:TN, r * NT:(r + 1) * NT]
                await_group(dve, "g3_deg", r)
                TS(inv, bank("g3_deg", r)[0:TN, 0:2 * NT].rearrange("p (n k) -> p n k", k=2)[:, :, 0], 1.0, None,
                   ALU.max).then_inc(S("g3_deg_read"), 1)
                dve.wait_ge(*E("g3_deg_read", r + 1))
                link(dve.reciprocal(inv, inv))

            for key, k, width in (("g3a", K1, 448), ("g3b", K1, 384), ("g3c", KD, 384)):
                clear_pad(key + "_hT_pad")
                for i in range(2 * NT):
                    n, (a, b) = i // 2, ((0, 4), (4, k))[i % 2]
                    at = slice(n * TN, (n + 1) * TN)
                    dve.wait_ge(*E(key + "_hT_high", i + 1))
                    TT(xT_lo[:, a:b, at], bank(key + "_hT", i)[:, 0:(b - a) * TN].rearrange("p (k n) -> p k n", n=TN),
                       f(xT_hi[:, a:b, at]), ALU.subtract).then_inc(S(key + "_hT_low"), 1)
                if key == "g3a":
                    for r in range(RELS - 1):
                        degrees(r)
                    for s in range(NT):
                        dve.wait_ge(*E("R0_whole_summed", NT))
                        dve.wait_ge(*E("R0_counts_ready", NT))
                        TT(rel[:, 2, s], f(adj[:, s]), f(rel[:, 0, s]), ALU.subtract).then_inc(S("others"), 1)
                    for s in range(NT):
                        dve.wait_ge(*E("R1_counts_ready", s + 1))
                        dve.wait_ge(*E("others", s + 1))
                        TT(rel[:, 2, s], f(rel[:, 2, s]), f(rel[:, 1, s]), ALU.subtract).then_inc(S("last_relation"), 1)
                else:
                    nodes_low(k * P, acc, key + "_nodes_high", key + "_nodes_low")
                dve.wait_ge(*E(key + "_nodes_low", NT))
                dve.wait_ge(*E(key + "_bias_full", 16))
                for i in range(2 * NT):
                    n, c = i % NT, i // NT
                    at = slice(c * width, (c + 1) * width)
                    await_group(dve, key + "_root", i)
                    TT(acc[:, n, at], bank(key + "_root", i)[0:TN, 0:width], bias[:, at], ALU.add
                       ).then_inc(S(key + "_acc"), 1)
                for r in range(RELS):
                    if key == "g3a" and r == RELS - 1:
                        degrees(r)
                    messages_low(key, f"{key}_agg{r}", k, 2 * k * r)
                    dve.wait_ge(*E(key + "_acc", 2 * NT * (r + 1)))
                    for i in range(2 * NT):
                        n, c = i % NT, i // NT
                        at = slice(c * width, (c + 1) * width)
                        await_group(dve, f"{key}_rel{r}", i)
                        STT(acc[:, n, at], bank(f"{key}_rel{r}", i)[0:TN, 0:width],
                            rel_inv[0:TN, r * NT + n:r * NT + n + 1], acc[:, n, at], ALU.mult, ALU.add
                            ).then_inc(S(key + "_acc"), 1)
                        if r == RELS - 1:
                            dve.wait_ge(*E(key + "_acc", 2 * NT * (r + 1) + i + 1))
                            if key != "g3c":
                                TS(acc[:, n, at], acc[:, n, at], 0.0, None, ALU.max
                                   ).then_inc(S({"g3a": "g3b", "g3b": "g3c"}[key] + "_nodes"), 1)
                            else:
                                STT(x[:, n, at], acc[:, n, at], 0.0, x[:, n, at], ALU.max, ALU.add
                                    ).then_inc(S("g3_x"), 1)
                                dve.wait_ge(*E("g3_x", i + 1))
                                last = node_stats(n, c)
                                if i == 2 * NT - 1:
                                    link(last)
            expert_layer("f3", 12)

        @block.tensor
        def _(pe):
            def open_bank(label, i):
                g = WHERE[label, i]
                if g >= 8:
                    pe.wait_ge(*E(*GROUPS[g - 8]))
                return banks[g % 8]

            closed = [0]

            def close(ins, label, i):
                assert WHERE[label, i] == closed[0], (label, i)
                closed[0] += 1
                ins.then_inc(S("group_closed"), 1)

            def three(dst, l_hi, l_lo, r_hi, r_lo, start, stop):
                pe.matmul(dst, l_hi, r_hi, start=start, stop=False)
                pe.matmul(dst, l_hi, r_lo, start=False, stop=False)
                return pe.matmul(dst, l_lo, r_hi, start=False, stop=stop)

            def transposes(label, src, k, ready, before=0):
                for i in range(2 * NT):
                    n, (a, b) = i // 2, ((0, 4), (4, k))[i % 2]
                    if i % 2 == 0:
                        pe.wait_ge(*E(ready, before + n + 1))
                    dst = open_bank(label, i)
                    for j in range(a, b):
                        last = pe.transpose(dst[:, (j - a) * TN:(j - a + 1) * TN], src[:, n, j * P:(j + 1) * P],
                                            ident[0:TN, 0:TN])
                    close(last, label, i)

            def up(s, j):
                m, c = job_of(s, j)
                c0, cn = CH[c]
                u = FIRST_UNIT["u", s] + m
                if c == 0:
                    pe.wait_ge(*E("unit_split", u + 1))
                dst = open_bank(s + "_hidden", j)
                for k in range(KD):
                    w = slice(k * P, (k + 1) * P)
                    last = three(dst[:, 0:cn], w_hi[:, u % RING, w], w_lo[:, u % RING, w], xT_hi[:, k, c0:c0 + cn],
                                 xT_lo[:, k, c0:c0 + cn], k == 0, k == KD - 1)
                close(last, s + "_hidden", j)
                if c:
                    pe.drain().then_inc(S("unit_used"), 1)

            def down(key, label, lhs_hi, lhs_lo, ready, feed=0, seed=None, after=None, tile_ready=None):
                kt, cw, chunks, per = DOWN[key]
                for c in range(chunks):
                    tail = 2 * per if c == chunks - 1 else 0
                    order = [(k, n) for k in range(kt - tail) for n in range(NT)]
                    order += [(k, n) for n in range(NT) for k in range(kt - tail, kt)] if tail else []
                    for k, n in order:
                        u, pos = divmod(feed * kt * chunks + c * kt + k, per)
                        u += FIRST_UNIT["d", key]
                        w = slice(pos * cw, (pos + 1) * cw)
                        if pos == 0 and n == 0:
                            pe.wait_ge(*E("unit_split", u + 1))
                        if c == 0 and n == 0:
                            ready(k)
                        if c == 0 and k == 0 and tile_ready:
                            tile_ready(n)
                        i = c * NT + n
                        at = slice(n * TN, (n + 1) * TN)
                        if k == 0:
                            open_bank(label, i)
                            if seed:
                                seed(bank(label, i), c, at)
                        last = three(bank(label, i)[0:TN, 0:cw], lhs_hi[:, k, at], lhs_lo[:, k, at],
                                     w_hi[:, u % RING, w], w_lo[:, u % RING, w], k == 0 and not seed, k == kt - 1)
                        if k == kt - 1:
                            close(last, label, i)
                        if pos == per - 1 and n == NT - 1:
                            if k == kt - 1:
                                last = pe.drain()
                            last.then_inc(S("unit_used"), 1)
                    if after:
                        after(c)

            def gather(label, k, counts_of, nodes, needed):
                for j in range(2 * k):
                    ft, (c0, cn) = j // 2, CH[j % 2]
                    dst = open_bank(label, j)
                    for half in (nm_hi, nm_lo):
                        for s in range(NT):
                            if needed(j, s):
                                pe.wait_ge(*E(nodes + ("_high" if half is nm_hi else "_low"), needed(j, s)))
                            last = pe.matmul(dst[:, 0:cn], half[:, s, ft * P:(ft + 1) * P], counts_of(s, c0, cn),
                                             start=(s == 0 and half is nm_hi), stop=(s == NT - 1 and half is nm_lo))
                    close(last, label, j)

            def of_adj(s, c0, cn):
                return adj[:, s, c0:c0 + cn]

            def of_rel(r):
                return lambda s, c0, cn: rel[:, r, s, c0:c0 + cn]

            def count_edges(label):
                def step(span, t, k, first=False, last_tile=False):
                    pe.wait_ge(*E(label + "_hot", t * 2 + (2 + 2 * span * SPAN)))
                    for s in range(NT):
                        if first:
                            open_bank(label, span * NT + s)
                        ins = pe.matmul(bank(label, span * NT + s)[0:TN, 0:HALF + 1], src_hot[:, k, s * TN:(s + 1) * TN],
                                        dst_hot[:, k], start=first, stop=last_tile)
                        if last_tile:
                            close(ins, label, span * NT + s)
                    if not last_tile:
                        ins.then_inc(S(label + "_hot_used"), 1)

                for span in range(SPANS):
                    for t in range(OSLOTS):
                        step(span, t, t, first=t == 0)
                    with pe.Fori(1, SPAN // OSLOTS - 1) as q:
                        for k in range(OSLOTS):
                            step(span, q * OSLOTS + k, k)
                    for k in range(OSLOTS):
                        step(span, SPAN - OSLOTS + k, k, last_tile=k == OSLOTS - 1)

            def degrees(label, i, counts_of):
                dst = open_bank(label, i)
                for n in range(NT):
                    for s in range(NT):
                        last = pe.matmul(dst[0:TN, 2 * n:2 * n + 2], counts_of(s, n * TN, TN), ones_r[0:TN, 0:2],
                                         start=s == 0, stop=s == NT - 1)
                close(last, label, i)

            def expert_layer(s, tiles, gate):
                transposes(s + "_xT", xn, KD, s + "_xn")
                pe.wait_ge(*E(s + "_xT_pad", 2))
                for c, (c0, cn) in enumerate(CH):
                    pe.wait_ge(*E(s + "_xT_low", (6, 2 * NT)[c]))
                    dst = open_bank(s + "_routerT", c)
                    for k in range(KD):
                        g = slice(48 * gate + 8 * k, 48 * gate + 8 * k + 8)
                        last = three(dst[0:EXPERTS, 0:cn], gate_hi[:, g], gate_lo[:, g], xT_hi[:, k, c0:c0 + cn],
                                     xT_lo[:, k, c0:c0 + cn], k == 0, k == KD - 1)
                    close(last, s + "_routerT", c)
                jobs = 2 * tiles
                for j in range(jobs + EXPERT_LAG):
                    if j < jobs:
                        up(s, j)
                    if j == 0:
                        pe.wait_ge(*E(s + "_routerT_read", 2))
                        dst = open_bank(s + "_router", 0)
                        for n in range(NT):
                            last = pe.transpose(dst[0:TN, 8 * n:8 * n + 8], router_T[:, n * TN:(n + 1) * TN],
                                                ident[0:EXPERTS, 0:EXPERTS])
                        close(last, s + "_router", 0)
                    if j == EXPERT_LAG - 1:
                        if s == "f1":
                            pe.wait_ge(*E("f1_probs", 1))
                            dst = open_bank("f1_importance", 0)
                            for n in range(NT):
                                last = pe.matmul(dst[0:TN, 0:8], ones[0:TN, 0:TN], prob8[0:TN, 8 * n:8 * n + 8],
                                                 start=n == 0, stop=n == NT - 1)
                            close(last, "f1_importance", 0)
                        pe.wait_ge(*E(s + "_combine", 1))
                        for n in range(NT):
                            dst = open_bank(s + "_cT", n)
                            close(pe.transpose(dst[:, 0:TN], cpad[:, n], ident[0:TN, 0:TN]), s + "_cT", n)
                        pe.wait_ge(*E(s + "_cT_pad", 2))
                        pe.wait_ge(*E(s + "_combineT", NT))
                    if j >= EXPERT_LAG:
                        i = j - EXPERT_LAG
                        m, (c0, cn) = i // 2, CH[i % 2]
                        q, kind = (m // 3, m % 3) if tiles == 12 else (m // 2, 2 * (m % 2))
                        rows = slice(32 * q, 32 * q + 2)
                        dst = open_bank(s + "_cB", i)
                        pe.matmul(dst[:, 0:cn], pat[rows, kind], cT_hi[rows, c0:c0 + cn], start=True, stop=False)
                        close(pe.matmul(dst[:, 0:cn], pat[rows, kind], cT_lo[rows, c0:c0 + cn], start=False, stop=True),
                              s + "_cB", i)
                if s == "f1":
                    seed = None
                else:
                    pe.wait_ge(*E(s + "_rows_split", 2))

                    def seed(dst, c, at):
                        half = slice(c * 384, (c + 1) * 384)
                        three(dst[0:TN, 0:384], cT_hi[:, at], cT_lo[:, at], bias8_hi[:, half], bias8_lo[:, half],
                              True, False)

                down(s + "d", s + "_down", hT_hi, hT_lo, lambda k: pe.wait_ge(*E(s + "_low", 2 * k + 2)), seed=seed)

            pe.wait_ge(*E("consts", 21))
            pe.wait_ge(*E("g0_peak", 1))
            dst = open_bank("g0_maxT", 0)
            close(pe.matmul(dst[0:1, 0:TN], peak[0:TN, 5:6], ident[0:TN, 0:TN], start=True, stop=True), "g0_maxT", 0)
            pe.wait_ge(*E("g0_max_read", 1))
            dst = open_bank("g0_maxB", 0)
            close(pe.matmul(dst[0:TN, 0:1], ones[0:1, 0:TN], peak_all[0:1, 0:1], start=True, stop=True), "g0_maxB", 0)
            count_edges("A")
            transposes("g0_xT", xn, KD, "g0_xn")
            pe.wait_ge(*E("A_whole_summed", NT))
            pe.wait_ge(*E("A_counts_ready", NT))
            pe.wait_ge(*E("g0_exp_low", NT))
            pe.wait_ge(*E("g0_num_low", NT))
            for j in range(2 * KD):
                ft, (c0, cn) = j % KD, CH[j // KD]
                for label, halves in (("g0_num", (nm_hi, nm_lo)), ("g0_den", (e_hi, e_lo))):
                    dst = open_bank(label, j)
                    for s in range(NT):
                        for half in halves:
                            last = pe.matmul(dst[:, 0:cn], half[:, s, ft * P:(ft + 1) * P], of_adj(s, c0, cn),
                                             start=(s == 0 and half is halves[0]), stop=(s == NT - 1 and half is halves[1]))
                    close(last, label, j)
            degrees("g1_deg", 0, of_adj)
            pe.wait_ge(*E("g0_xT_pad", 2))
            pe.wait_ge(*E("bn_ready", 1))
            for j in range(24):
                pe.wait_ge(*E("g0_out_low", 2 * KD if job_of("g0", j)[1] else KD))
                up("g0", j)
            down("g0d", "g0d", hT_hi, hT_lo, lambda k: pe.wait_ge(*E("g0_low", max(2 * k + 2, 6))))
            pe.wait_ge(*E("gates_split", 1))
            expert_layer("f0", 12, 0)
            pe.wait_ge(*E("self_loops", NT))
            gather("g1a_agg", KD, of_adj, "g1_nodes", lambda j, s: s + 1 if j == 0 else 0)
            down("g1a", "g1a", xT_hi, xT_lo, lambda k: pe.wait_ge(*E("g1a_low", 2 * k + 2)))
            gather("g1b_agg", KD, of_adj, "g1b_nodes",
                   lambda j, s: {0: s + 1, KD: NT + s + 1}.get(j, 0))

            def edge_mask(c):
                if c == 0:
                    pe.wait_ge(*E("no_self_loops", NT))
                    for i in range(2 * NT):
                        d, (a, b) = i // 2, ((0, 4), (4, NT))[i % 2]
                        dst = open_bank("g2_maskT", i)
                        for s in range(a, b):
                            last = pe.transpose(dst[0:TN, (s - a) * TN:(s - a + 1) * TN],
                                                f(adj[:, s, d * TN:(d + 1) * TN]), ident[0:TN, 0:TN])
                        close(last, "g2_maskT", i)

            down("g1b", "g1b", xT_hi, xT_lo, lambda k: pe.wait_ge(*E("g1b_low", 2 * k + 2)), after=edge_mask)
            expert_layer("f1", 8, 1)
            transposes("g2_xT", xn, KD, "g2_xn")

            def source_rows(label, c):
                for i, (a, b) in enumerate(((0, 4), (4, NT))):
                    dst = open_bank(label + "_asT", 2 * c + i)
                    for n in range(a, b):
                        last = pe.transpose(dst[0:2, (n - a) * TN:(n - a + 1) * TN],
                                            a_src[0:TN, 8 * n + 2 * c:8 * n + 2 * c + 2], ident[0:TN, 0:TN])
                    close(last, label + "_asT", 2 * c + i)

            def source_broadcast(label, c, heads=2):
                pe.wait_ge(*E(label + "_asT_read", 2 * (c + 1)))
                for h in range(2 * c, 2 * c + heads):
                    for half, (c0, cn) in enumerate(CH):
                        dst = open_bank(label + "_asB", 2 * h + half)
                        close(pe.matmul(dst[0:TN, 0:cn], head_sel[0:2, h % 2, 0:TN], asT[:, c0:c0 + cn],
                                        start=True, stop=True), label + "_asB", 2 * h + half)

            pe.wait_ge(*E("head_sel", 1))
            pe.wait_ge(*E("asT_pad", 1))

            kt, cw, chunks, per = DOWN["g2a"]
            for c in range(chunks + 1):
                for n in range(NT):
                    if c < chunks:
                        if c == 0:
                            pe.wait_ge(*E("g2_xT_low", 2 * n + 2))
                        dst = open_bank("g2a", c * NT + n)
                        at = slice(n * TN, (n + 1) * TN)
                        for k in range(kt):
                            u, pos = divmod(c * kt + k, per)
                            u += FIRST_UNIT["d", "g2a"]
                            w = slice(pos * cw, (pos + 1) * cw)
                            if n == 0 and pos == 0:
                                pe.wait_ge(*E("unit_split", u + 1))
                            last = three(dst[0:TN, 0:cw], xT_hi[:, k, at], xT_lo[:, k, at], w_hi[:, u % RING, w],
                                         w_lo[:, u % RING, w], k == 0, k == kt - 1)
                            if k == kt - 1:
                                close(last, "g2a", c * NT + n)
                            if n == NT - 1 and pos == per - 1:
                                if k == kt - 1:
                                    last = pe.drain()
                                last.then_inc(S("unit_used"), 1)
                    if c and n == 1:
                        pe.wait_ge(*E("g2p_scores", 4 * NT * c))
                        source_rows("g2p", c - 1)
                    if c and n == 2:
                        source_broadcast("g2p", c - 1)

            def attention(layer, heads, product):
                pe.wait_ge(*E(layer + "_uv", 2))
                for i in range(4):
                    a, b = ((0, 4), (4, NT))[i % 2]
                    dst = open_bank(layer + "_uvT", i)
                    for n in range(a, b):
                        last = pe.transpose(dst[0:8, (n - a) * TN:(n - a + 1) * TN], uv[:, i // 2, n], ident[0:TN, 0:TN])
                    close(last, layer + "_uvT", i)
                pe.wait_ge(*E(layer + "_pads", 2))
                pe.wait_ge(*E(layer + "_uvT_read", 4))
                def broadcast(h):
                    for i in range(4):
                        c0, cn = CH[i % 2]
                        dst = open_bank(layer + "_uvB", 4 * h + i)
                        close(pe.matmul(dst[0:TN, 0:cn], head_sel[:, h, 0:TN], (uT, vT)[i // 2][:, c0:c0 + cn],
                                        start=True, stop=True), layer + "_uvB", 4 * h + i)

                broadcast(0)
                for h in range(heads + 2):
                    if h + 1 < heads:
                        broadcast(h + 1)
                    if 1 <= h <= heads:
                        product(h - 1)
                    if heads > 1 and h >= 2:
                        turn_head(h - 2)

            def head_product(h):
                for i, (a, b) in enumerate(((0, 3), (3, NT))):
                    dst = open_bank("g2p_agg", 2 * h + i)
                    for n in range(a, b):
                        at = (n - a) * (HEAD_DIM + 1)
                        for s in range(NT):
                            if n == 0:
                                pe.wait_ge(*E("g2p_prob", NT * h + s + 1))
                            last = pe.matmul(dst[0:TN, at:at + HEAD_DIM + 1], prob[h % 2][:, s, n * TN:(n + 1) * TN],
                                             h1[:, s, h, 0:HEAD_DIM + 1], start=s == 0, stop=s == NT - 1)
                    close(last, "g2p_agg", 2 * h + i)

            def turn_head(h):
                for i, (a, b) in enumerate(((0, 4), (4, NT))):
                    pe.wait_ge(*E("g2p_mean", 2 * h + 2))
                    dst = open_bank("g2p_outT", 2 * h + i)
                    for n in range(a, b):
                        last = pe.transpose(dst[:, (n - a) * TN:(n - a + 1) * TN], mean[:, h % 2, n], ident[0:TN, 0:TN])
                    close(last, "g2p_outT", 2 * h + i)

            def last_product(_):
                for n in range(NT):
                    for i, at in ((2 * n, slice(384, D + 1)), (2 * n + 1, slice(0, 384))):
                        dst = open_bank("g2q_agg", i)
                        for s in range(NT):
                            if i == 0:
                                pe.wait_ge(*E("g2q_prob", s + 1))
                            last = pe.matmul(dst[0:TN, 0:at.stop - at.start], prob[0][:, s, n * TN:(n + 1) * TN],
                                             h2[:, s, at], start=s == 0, stop=s == NT - 1)
                        close(last, "g2q_agg", i)

            pe.wait_ge(*E("h1_ones", 1))
            attention("g2p", HEADS, head_product)
            down("g2b", "g2b", hT_hi, hT_lo, lambda k: pe.wait_ge(*E("g2p_low", k + 1)))
            pe.wait_ge(*E("g2q_scores", 2))
            source_rows("g2q", 0)
            source_broadcast("g2q", 0, 1)
            attention("g2q", 1, last_product)
            transposes("f2_xT", xn, KD, "f2_unit")
            pe.wait_ge(*E("slots_split", 1))
            pe.wait_ge(*E("f2_xT_pad", 2))
            for c, (c0, cn) in enumerate(CH):
                pe.wait_ge(*E("f2_xT_low", (6, 2 * NT)[c]))
                dst = open_bank("f2_logitsT", c)
                for k in range(KD):
                    last = three(dst[0:SLOTS, 0:cn], sp_hi[:, k], sp_lo[:, k], xT_hi[:, k, c0:c0 + cn],
                                 xT_lo[:, k, c0:c0 + cn], k == 0, k == KD - 1)
                close(last, "f2_logitsT", c)
            pe.wait_ge(*E("f2_logitsT_read", 2))
            dst = open_bank("f2_logits", 0)
            for n in range(NT):
                last = pe.transpose(dst[0:TN, n * SLOTS:(n + 1) * SLOTS], logitsT[:, n * TN:(n + 1) * TN],
                                    ident[0:SLOTS, 0:SLOTS])
            close(last, "f2_logits", 0)
            pe.wait_ge(*E("f2_dispatchT", 1))
            dst = open_bank("f2_dispatch", 0)
            for n in range(NT):
                last = pe.transpose(dst[0:TN, n * SLOTS:(n + 1) * SLOTS], logitsT[:, n * TN:(n + 1) * TN],
                                    ident[0:SLOTS, 0:SLOTS])
            close(last, "f2_dispatch", 0)
            pe.wait_ge(*E("f2_combine", 1))
            for i, (a, b) in enumerate(((0, 4), (4, NT))):
                dst = open_bank("f2_combineT", i)
                for n in range(a, b):
                    last = pe.transpose(dst[0:SLOTS, (n - a) * TN:(n - a + 1) * TN], combine[:, n], ident[0:TN, 0:TN])
                close(last, "f2_combineT", i)
            pe.wait_ge(*E("f2_dispatch_read", 1))
            dst = open_bank("f2_tilde", 0)
            for k in range(KD):
                for n in range(NT):
                    last = pe.matmul(dst[:, k * SLOTS:(k + 1) * SLOTS], xn[:, n, k * P:(k + 1) * P], dispatch[:, n],
                                     start=n == 0, stop=n == NT - 1)
            close(last, "f2_tilde", 0)
            pe.wait_ge(*E("slot_weights", 16 * (EXPERTS + 1)))
            pe.wait_ge(*E("f2_tilde_read", 1))
            dst = open_bank("f2_hidden", 0)
            for e in range(EXPERTS):
                for k in range(KD):
                    last = pe.matmul(dst[0:SLOT_H, 4 * e:4 * e + 4], w_down[:, e, k], tildeT[:, k, 4 * e:4 * e + 4],
                                     start=k == 0, stop=k == KD - 1)
            close(last, "f2_hidden", 0)
            pe.wait_ge(*E("type_hot", 1))
            pe.wait_ge(*E("emb_loaded", 16))
            for n in range(NT):
                dst = open_bank("g3_emb", n)
                close(pe.matmul(dst[0:TN, 0:TYPE_DIM], type_hot[:, n * TN:(n + 1) * TN], emb[:], start=True, stop=True),
                      "g3_emb", n)
            pe.wait_ge(*E("f2_bias_full", 16))
            pe.wait_ge(*E("f2_diag", 1))
            for c in range(2):
                at = slice(c * 384, (c + 1) * 384)
                dst = open_bank("f2_up", c)
                pe.matmul(dst[0:SLOTS, 0:384], sel8[0:8, :], bias8[0:8, at], start=True, stop=False)
                for e in range(EXPERTS):
                    last = pe.matmul(dst[0:SLOTS, 0:384], hidden_diag[:, 32 * e:32 * e + 32], w_up[:, e, at],
                                     start=False, stop=e == EXPERTS - 1)
                close(last, "f2_up", c)
            pe.wait_ge(*E("f2_up_read", 2))
            pe.wait_ge(*E("f2_combineT_read", 2))
            for c in range(2):
                for n in range(NT):
                    dst = open_bank("f2_down", c * NT + n)
                    close(pe.matmul(dst[0:TN, 0:384], combineT[:, n * TN:(n + 1) * TN],
                                    slot_out[:, c * 384:(c + 1) * 384], start=True, stop=True), "f2_down", c * NT + n)
            for r in range(RELS - 1):
                count_edges(f"R{r}")
            for key, k, ready in (("g3a", K1, "g3_xn"), ("g3b", K1, "g3b_nodes"), ("g3c", KD, "g3c_nodes")):
                if key == "g3a":
                    pe.wait_ge(*E("g3_emb_low", NT))
                transposes(key + "_hT", acc, k, ready, 0 if key == "g3a" else NT)
                if key == "g3a":
                    for r in range(RELS - 1):
                        pe.wait_ge(*E(f"R{r}_whole_summed", NT))
                        pe.wait_ge(*E(f"R{r}_counts_ready", NT))
                        degrees("g3_deg", r, of_rel(r))
                pe.wait_ge(*E(key + "_hT_pad", 2))
                down(key, key + "_root", xT_hi, xT_lo, lambda k: None,
                     tile_ready=lambda n: pe.wait_ge(*E(key + "_hT_low", 2 * n + 2)))
                for r in range(RELS):
                    if key == "g3a" and r == RELS - 1:
                        pe.wait_ge(*E("last_relation", NT))
                        degrees("g3_deg", r, of_rel(r))
                    gather(f"{key}_agg{r}", k, of_rel(r), key + "_nodes", lambda j, s: s + 1 if j == 0 else 0)
                    first = 2 * k * r
                    down(key, f"{key}_rel{r}", xT_hi, xT_lo,
                         lambda t: pe.wait_ge(*E(key + "_low", first + 2 * t + 2)), feed=r + 1)
            expert_layer("f3", 12, 2)
            assert closed[0] == len(GROUPS)


NAMES = ["x_in", "edges_in", "wa", "wb", "wc", "cols_in", "bias_in", "rows_in", "att_in", "scalars_in",
         "w_down_in", "w_up_in", "emb_in", "types_in"]


def up_units(w):
    m = w.shape[1] // P
    return w.reshape(KD, P, m, P).transpose(2, 1, 0, 3).reshape(m, P, UNIT)


def down_slices(w, key):
    k, cw, chunks, per = DOWN[key]
    ws = w if isinstance(w, list) else [w]
    s = np.concatenate([v.reshape(k, P, chunks, cw).transpose(2, 0, 1, 3).reshape(chunks * k, P, cw) for v in ws])
    return s.reshape(-1, per, P, cw).transpose(0, 2, 1, 3).reshape(-1, P, per * cw)


def laid_out(i):
    i = {k: np.asarray(v) for k, v in i.items()}

    def per_expert_in(w):
        return w.transpose(1, 0, 2).reshape(w.shape[1], -1)

    def tiles(v):
        return v.reshape(-1, P).T

    feeds = {"g3a": "1", "g3b": "2", "g3c": "3"}
    down = {
        "g0d": i["L0_gnn_W2"], "f0d": i["L0_ffn_w2"].reshape(-1, D), "g1a": i["L1_gnn_W1"], "g1b": i["L1_gnn_W2"],
        "f1d": i["L1_ffn_w2"].transpose(0, 2, 1).reshape(-1, D), "g2a": i["L2_gnn_W1"].T, "g2b": i["L2_gnn_W2"].T,
        "f3d": i["L3_ffn_w2"].reshape(-1, D),
    }
    for key, n in feeds.items():
        down[key] = [i["L3_gnn_w_root" + n]] + list(i["L3_gnn_w_rel" + n])
    up = {
        "g0": i["L0_gnn_W1"], "f0": per_expert_in(i["L0_ffn_w1"]),
        "f1": i["L1_ffn_w1"].transpose(2, 0, 1).reshape(D, -1), "f3": per_expert_in(i["L3_ffn_w1"]),
    }

    def stream(seq):
        return np.concatenate([up_units(up[key]) if kind == "u" else down_slices(down[key], key) for kind, key in seq])

    def gate(w):
        return w.T.reshape(KD, P, EXPERTS).transpose(1, 0, 2).reshape(P, -1)

    b_down = np.concatenate([i["L2_ffn_b_down"].T, np.zeros((P - SLOT_H, EXPERTS), np.float32)])
    cols = np.concatenate(
        [tiles(i["L0_gnn_b1"]), tiles(i["L0_gnn_bn_gamma"]), tiles(i["L0_gnn_bn_beta"]), tiles(i["L0_gnn_bn_mean"]),
         tiles(i["L0_gnn_bn_var"]), tiles(i["L0_ffn_b1"].reshape(-1)), tiles(i["L3_ffn_b1"].reshape(-1)),
         tiles(i["L2_gnn_b1"]), gate(i["L0_ffn_gate_w"]), gate(i["L1_ffn_router_w"]), gate(i["L3_ffn_gate_w"]),
         i["L2_ffn_slot_params"].reshape(KD, P, SLOTS).transpose(1, 0, 2).reshape(P, -1), b_down], axis=1)

    def row(v):
        return np.concatenate([v, np.zeros(D1 - v.size, np.float32)])[None]

    def wide(v):
        return np.concatenate([v.reshape(-1), np.zeros(HEADS * HEAD_DIM - v.size, np.float32)])[None]

    return dict(
        x_in=i["x"],
        edges_in=np.stack([i["src"].reshape(TN, ET), i["dst"].reshape(TN, ET), i["edge_type_3"].reshape(TN, ET)], axis=1),
        wa=stream(SEQ_A), wb=stream(SEQ_B), wc=stream(SEQ_C), cols_in=cols,
        bias_in=np.concatenate([row(i[k]) for k in ("L0_gnn_b2", "L1_gnn_b1", "L1_gnn_b2", "L2_gnn_b2", "L3_gnn_b1",
                                                    "L3_gnn_b2", "L3_gnn_b3")]),
        rows_in=np.concatenate([i["L0_ffn_b2"], i["L2_ffn_b_up"], i["L3_ffn_b2"]]),
        att_in=np.concatenate([wide(i[k]) for k in ("L2_gnn_att_src1", "L2_gnn_att_dst1", "L2_gnn_att_src2",
                                                    "L2_gnn_att_dst2")]),
        scalars_in=np.stack([i["L0_gnn_t"].reshape(1), i["L2_ffn_scale"].reshape(1)]),
        w_down_in=i["L2_ffn_W_down"], w_up_in=i["L2_ffn_W_up"], emb_in=i["L3_gnn_node_emb"],
        types_in=i["node_type_3"][None],
    )


def kernel(**inputs):
    import concourse.bacc as bacc
    from concourse.bass_utils import run_bass_kernel_spmd

    arrays = {k: np.ascontiguousarray(v) for k, v in laid_out(inputs).items()}
    nc = bacc.Bacc("TRN2", target_bir_lowering=False, num_devices=1)
    args = [nc.dram_tensor(k, arrays[k].shape, mybir.dt.from_np(arrays[k].dtype), kind="ExternalInput").ap() for k in NAMES]
    out = nc.dram_tensor("out", (NODES, D), f32, kind="ExternalOutput").ap()
    network(nc, *args, out)
    r = run_bass_kernel_spmd(nc, [arrays], core_ids=[0])
    return r.results[0]["out"]
```
